# Optimizing a Trainium2 kernel written in Bass

```python
import numpy as np
import jax
import jax.numpy as jnp

def _softmax(x, axis=-1):
    return jax.nn.softmax(x, axis=axis)

def _gelu(x):
    return jax.nn.gelu(x, approximate=True)

def _silu(x):
    return jax.nn.silu(x)

def _sigmoid(x):
    return jax.nn.sigmoid(x)

def _layernorm(x, axis=-1, eps=1e-05):
    m = jnp.mean(x, axis=axis, keepdims=True)
    v = jnp.var(x, axis=axis, keepdims=True)
    return (x - m) / jnp.sqrt(v + eps)

def _scatter_add(tgt, idx, src, axis=0):
    return tgt.at[idx].add(src)

def _segment_sum(src, seg, n):
    return jax.ops.segment_sum(src, seg, n)
kernel_name = 'mk_flamingo_gated_d2_seqx_r8_3dd1ea'

def setup_inputs(seed: int=0):
    np.random.seed(seed)
    _w = jnp.asarray

    def _rec_inputs():
        import jax
        import jax.numpy as jnp
        _rk = jax.random.key(seed)
        x = -0.0002928 + 1 * jax.random.normal(jax.random.fold_in(_rk, 1), (16, 256, 128), jnp.float32)
        _lenS = 256 - jax.random.randint(jax.random.fold_in(_rk, 7), (16,), 0, max(1, 256 // 4) + 1, jnp.int32)
        _lenS2 = 1601 - jax.random.randint(jax.random.fold_in(_rk, 8), (16,), 0, max(1, 1601 // 4) + 1, jnp.int32)
        _ctx_1024P = jax.random.normal(jax.random.fold_in(_rk, 11), (16, 16, 128), jnp.float32)
        _ctx_1024c = jax.random.dirichlet(jax.random.fold_in(_rk, 511), 0.3 * jnp.ones((16,), jnp.float32), (16, 1601))
        _ctx_1024t = jnp.einsum('bsk,bkd->bsd', _ctx_1024c, _ctx_1024P)
        _ctx_1024t = _ctx_1024t * jax.lax.rsqrt(jnp.mean(jnp.square(_ctx_1024t)) + 1e-12) * 0.953939
        ctx_1024 = -1.39393e-06 + 0.999914 * (_ctx_1024t + 0.3 * jax.random.normal(jax.random.fold_in(_rk, 611), (16, 1601, 128), jnp.float32))
        fside_BxSxS2_0 = jax.random.uniform(jax.random.fold_in(_rk, 12), (16, 256, 1601), jnp.float32, 0.0, 1)
        _validS = jnp.arange(256)[None, :] < _lenS[:, None]
        _validS2 = jnp.arange(1601)[None, :] < _lenS2[:, None]
        _causal = jnp.tril(jnp.ones((256, 256), dtype=bool))
        mask_BxSxS2_ik1 = jnp.where(jnp.broadcast_to(_validS2[:, None, :], (16, 256, 1601)), 1, 0).astype(jnp.int32)
        mask_1x1xSxS2_ik0 = jnp.where(jnp.broadcast_to(_validS2[0:1, None, None, :], (1, 1, 256, 1601)), 0, 1).astype(jnp.int32)
        _g = jax.random.normal(jax.random.fold_in(_rk, 9001), (2, 2), jnp.float32)
        _g = jnp.sign(_g) * jnp.maximum(jnp.abs(_g), 1.0) + (_g == 0) * 1.0
        g_xattn = _g[0]
        g_ffn = _g[1]
        return (x, ctx_1024, fside_BxSxS2_0, mask_BxSxS2_ik1, mask_1x1xSxS2_ik0, g_xattn, g_ffn)
    x, ctx_1024, fside_BxSxS2_0, mask_BxSxS2_ik1, mask_1x1xSxS2_ik0, g_xattn, g_ffn = _rec_inputs()

    def _L0_xattn_setup():
        import jax, jax.numpy as jnp
        import numpy as np
        NUM_HEADS = 16
        HIDDEN = 128
        B, S = (2, 256)

        def _split_heads(x, H):
            b, s, d = x.shape
            return x.reshape(b, s, H, d // H).transpose(0, 2, 1, 3)
        key = jax.random.key(seed)
        ks = jax.random.split(key, 14)
        D = HIDDEN
        scale = 1.0 / np.sqrt(D)
        inp = {'query': jax.random.normal(ks[0], (B, S, D), jnp.float32), 'key_in': jax.random.normal(ks[1], (B, S, D), jnp.float32), 'value': jax.random.normal(ks[2], (B, S, D), jnp.float32), 'group_prob': jax.random.uniform(ks[3], (B, S, S), jnp.float32), 'mask': jax.random.randint(ks[4], (B, S, S), 0, 2, jnp.int32), 'wq_k': jax.random.normal(ks[5], (D, D), jnp.float32) * scale, 'wq_b': jnp.zeros((D,), jnp.float32), 'wk_k': jax.random.normal(ks[6], (D, D), jnp.float32) * scale, 'wk_b': jnp.zeros((D,), jnp.float32), 'wv_k': jax.random.normal(ks[7], (D, D), jnp.float32) * scale, 'wv_b': jnp.zeros((D,), jnp.float32), 'wo_k': jax.random.normal(ks[8], (D, D), jnp.float32) * scale, 'wo_b': jnp.zeros((D,), jnp.float32)}
        return inp
    _L0_xattn_all = _L0_xattn_setup()
    _L0_xattn_in = {k: v for k, v in _L0_xattn_all.items() if k in ('wq_k', 'wq_b', 'wk_k', 'wk_b', 'wv_k', 'wv_b', 'wo_k', 'wo_b')}
    del _L0_xattn_all

    def _L0_ffn_setup():
        import jax, jax.numpy as jnp
        import numpy as np
        D_MODEL, D_FF, N_EXPERTS, TOP_K = (128, 512, 8, 2)
        B, S = (2, 256)
        key = jax.random.key(seed)
        ks = jax.random.split(key, 7)
        scale = 0.02
        return {'x': jax.random.normal(ks[0], (B, S, D_MODEL), dtype=jnp.float32), 'W1': jax.random.normal(ks[1], (N_EXPERTS, D_MODEL, D_FF), dtype=jnp.float32) * scale, 'b1': jnp.zeros((N_EXPERTS, D_FF), dtype=jnp.float32), 'W2': jax.random.normal(ks[2], (N_EXPERTS, D_FF, D_MODEL), dtype=jnp.float32) * scale, 'b2': jnp.zeros((N_EXPERTS, D_MODEL), dtype=jnp.float32), 'Wg': jax.random.normal(ks[3], (D_MODEL, N_EXPERTS), dtype=jnp.float32) * scale, 'bg': jnp.zeros((N_EXPERTS,), dtype=jnp.float32)}
    _L0_ffn_all = _L0_ffn_setup()
    _L0_ffn_in = {k: v for k, v in _L0_ffn_all.items() if k in ('W1', 'b1', 'W2', 'b2', 'Wg', 'bg')}
    del _L0_ffn_all

    def _L1_xattn_setup():
        import jax, jax.numpy as jnp
        import numpy as np
        import math
        B, S, D, H = (2, 256, 128, 16)
        DK = D // H

        def _split_heads(x):
            b, s, _ = x.shape
            return x.reshape(b, s, H, DK).transpose(0, 2, 1, 3)
        key = jax.random.key(seed)
        ks = jax.random.split(key, 12)
        std = 1.0 / math.sqrt(D)
        inp = {'q': jax.random.normal(ks[0], (B, S, D), jnp.float32), 'k': jax.random.normal(ks[1], (B, S, D), jnp.float32), 'v': jax.random.normal(ks[2], (B, S, D), jnp.float32), 'mask': jnp.tril(jnp.ones((S, S), jnp.int32))[None, None, :, :], 'wq': jax.random.normal(ks[3], (D, D), jnp.float32) * std, 'bq': jax.random.normal(ks[4], (D,), jnp.float32) * std, 'wk': jax.random.normal(ks[5], (D, D), jnp.float32) * std, 'bk': jax.random.normal(ks[6], (D,), jnp.float32) * std, 'wv': jax.random.normal(ks[7], (D, D), jnp.float32) * std, 'bv': jax.random.normal(ks[8], (D,), jnp.float32) * std, 'wo': jax.random.normal(ks[9], (D, D), jnp.float32) * std, 'bo': jax.random.normal(ks[10], (D,), jnp.float32) * std}
        return inp
    _L1_xattn_all = _L1_xattn_setup()
    _L1_xattn_in = {k: v for k, v in _L1_xattn_all.items() if k in ('wq', 'bq', 'wk', 'bk', 'wv', 'bv', 'wo', 'bo')}
    del _L1_xattn_all

    def _L1_ffn_setup():
        import jax, jax.numpy as jnp
        import numpy as np
        E, D, F, GATE_DIM = (8, 128, 512, 16)
        B, T = (2, 256)
        key = jax.random.key(seed)
        ks = jax.random.split(key, 7)
        s = 0.02
        return {'hidden_states': jax.random.normal(ks[0], (B, T, D), dtype=jnp.float32), 'w_red': jax.random.normal(ks[1], (D, GATE_DIM), dtype=jnp.float32) * s, 'wg': jax.random.normal(ks[2], (E, GATE_DIM), dtype=jnp.float32), 'w1': jax.random.normal(ks[3], (E, D, F), dtype=jnp.float32) * s, 'b1': jax.random.normal(ks[4], (E, F), dtype=jnp.float32) * s, 'w2': jax.random.normal(ks[5], (E, F, D), dtype=jnp.float32) * s, 'b2': jax.random.normal(ks[6], (E, D), dtype=jnp.float32) * s}
    _L1_ffn_all = _L1_ffn_setup()
    _L1_ffn_in = {k: v for k, v in _L1_ffn_all.items() if k in ('w_red', 'wg', 'w1', 'b1', 'w2', 'b2')}
    del _L1_ffn_all
    return {'x': x, 'ctx_1024': ctx_1024, 'fside_BxSxS2_0': fside_BxSxS2_0, 'mask_BxSxS2_ik1': mask_BxSxS2_ik1, 'mask_1x1xSxS2_ik0': mask_1x1xSxS2_ik0, 'g_xattn': g_xattn, 'g_ffn': g_ffn, 'L0_xattn_wq_k': _L0_xattn_in['wq_k'], 'L0_xattn_wq_b': _L0_xattn_in['wq_b'], 'L0_xattn_wk_k': _L0_xattn_in['wk_k'], 'L0_xattn_wk_b': _L0_xattn_in['wk_b'], 'L0_xattn_wv_k': _L0_xattn_in['wv_k'], 'L0_xattn_wv_b': _L0_xattn_in['wv_b'], 'L0_xattn_wo_k': _L0_xattn_in['wo_k'], 'L0_xattn_wo_b': _L0_xattn_in['wo_b'], 'L0_ffn_W1': _L0_ffn_in['W1'], 'L0_ffn_b1': _L0_ffn_in['b1'], 'L0_ffn_W2': _L0_ffn_in['W2'], 'L0_ffn_b2': _L0_ffn_in['b2'], 'L0_ffn_Wg': _L0_ffn_in['Wg'], 'L0_ffn_bg': _L0_ffn_in['bg'], 'L1_xattn_wq': _L1_xattn_in['wq'], 'L1_xattn_bq': _L1_xattn_in['bq'], 'L1_xattn_wk': _L1_xattn_in['wk'], 'L1_xattn_bk': _L1_xattn_in['bk'], 'L1_xattn_wv': _L1_xattn_in['wv'], 'L1_xattn_bv': _L1_xattn_in['bv'], 'L1_xattn_wo': _L1_xattn_in['wo'], 'L1_xattn_bo': _L1_xattn_in['bo'], 'L1_ffn_w_red': _L1_ffn_in['w_red'], 'L1_ffn_wg': _L1_ffn_in['wg'], 'L1_ffn_w1': _L1_ffn_in['w1'], 'L1_ffn_b1': _L1_ffn_in['b1'], 'L1_ffn_w2': _L1_ffn_in['w2'], 'L1_ffn_b2': _L1_ffn_in['b2']}

def reference(x, ctx_1024, fside_BxSxS2_0, mask_BxSxS2_ik1, mask_1x1xSxS2_ik0, g_xattn, g_ffn, L0_xattn_wq_k, L0_xattn_wq_b, L0_xattn_wk_k, L0_xattn_wk_b, L0_xattn_wv_k, L0_xattn_wv_b, L0_xattn_wo_k, L0_xattn_wo_b, L0_ffn_W1, L0_ffn_b1, L0_ffn_W2, L0_ffn_b2, L0_ffn_Wg, L0_ffn_bg, L1_xattn_wq, L1_xattn_bq, L1_xattn_wk, L1_xattn_bk, L1_xattn_wv, L1_xattn_bv, L1_xattn_wo, L1_xattn_bo, L1_ffn_w_red, L1_ffn_wg, L1_ffn_w1, L1_ffn_b1, L1_ffn_w2, L1_ffn_b2):
    import jax
    import jax.numpy as jnp

    def _L0_xattn_ref(query, key_in, value, group_prob, mask, wq_k, wq_b, wk_k, wk_b, wv_k, wv_b, wo_k, wo_b):
        import jax, jax.numpy as jnp
        import numpy as np
        NUM_HEADS = 16
        HIDDEN = 128
        B, S = (2, 256)

        def _split_heads(x, H):
            b, s, d = x.shape
            return x.reshape(b, s, H, d // H).transpose(0, 2, 1, 3)
        H = NUM_HEADS
        dh = query.shape[-1] // H
        q = _split_heads(query @ wq_k + wq_b, H)
        k = _split_heads(key_in @ wk_k + wk_b, H)
        v = _split_heads(value @ wv_k + wv_b, H)
        logits = jnp.einsum('bhqd,bhkd->bhqk', q, k) / jnp.sqrt(jnp.asarray(dh, q.dtype))
        neg = (1.0 - mask.astype(q.dtype)) * -1000000000.0
        logits = logits + neg[:, None, :, :]
        attn = jax.nn.softmax(logits, axis=-1)
        attn = attn * group_prob[:, None, :, :]
        out = jnp.einsum('bhqk,bhkd->bhqd', attn, v)
        out = out.transpose(0, 2, 1, 3).reshape(query.shape[0], -1, H * dh)
        return out @ wo_k + wo_b

    def _L0_ffn_ref(x, W1, b1, W2, b2, Wg, bg):
        import jax, jax.numpy as jnp
        import numpy as np
        D_MODEL, D_FF, N_EXPERTS, TOP_K = (128, 512, 8, 2)
        B, S = (2, 256)
        Bx, Sx, d = x.shape
        E = W1.shape[0]
        logits = jnp.einsum('bsd,de->bse', x, Wg) + bg
        topk_scores, topk_idx = jax.lax.top_k(logits, TOP_K)
        topk_scores = jax.nn.softmax(topk_scores, axis=-1)
        tokens = x.reshape(-1, d)
        idx_flat = topk_idx.reshape(-1, TOP_K)
        sc_flat = topk_scores.reshape(-1, TOP_K)
        comb = (jax.nn.one_hot(idx_flat, E, dtype=x.dtype) * sc_flat[..., None]).sum(axis=1)
        h = jnp.einsum('td,edf->etf', tokens, W1) + b1[:, None, :]
        even = (jnp.arange(E) % 2 == 0)[:, None, None]
        a = jnp.where(even, jax.nn.gelu(h, approximate=False), jax.nn.silu(h))
        y = jnp.einsum('etf,efd->etd', a, W2) + b2[:, None, :]
        out = jnp.einsum('te,etd->td', comb, y)
        return out.reshape(Bx, Sx, d)

    def _L1_xattn_ref(q, k, v, mask, wq, bq, wk, bk, wv, bv, wo, bo):
        import jax, jax.numpy as jnp
        import numpy as np
        import math
        B, S, D, H = (2, 256, 128, 16)
        DK = D // H

        def _split_heads(x):
            b, s, _ = x.shape
            return x.reshape(b, s, H, DK).transpose(0, 2, 1, 3)
        query = _split_heads(q @ wq.T + bq)
        key_h = _split_heads(k @ wk.T + bk)
        value = _split_heads(v @ wv.T + bv)
        scale = 1.0 / math.sqrt(DK)
        scores = jnp.einsum('bhqd,bhkd->bhqk', query, key_h) * scale
        scores = jnp.where(mask == 0, jnp.float32(-1000000000.0), scores)
        attn = jax.nn.softmax(scores, axis=-1)
        x = jnp.einsum('bhqk,bhkd->bhqd', attn, value)
        x = x.transpose(0, 2, 1, 3).reshape(q.shape[0], -1, H * DK)
        return x @ wo.T + bo

    def _L1_ffn_ref(hidden_states, w_red, wg, w1, b1, w2, b2):
        import jax, jax.numpy as jnp
        import numpy as np
        E, D, F, GATE_DIM = (8, 128, 512, 16)
        B, T = (2, 256)
        b, t, c = hidden_states.shape
        x = hidden_states.reshape(-1, c)
        red = x @ w_red
        wg_n = wg / jnp.maximum(jnp.linalg.norm(wg, axis=1, keepdims=True), 0.0001)
        logits = red @ wg_n.T
        gates = jax.nn.softmax(logits, axis=1)
        idx = jnp.argmax(gates, axis=1)
        scores = jnp.take_along_axis(gates, idx[:, None], axis=1)
        h = jax.nn.gelu(jnp.einsum('td,edf->etf', x, w1) + b1[:, None, :], approximate=False)
        y = jnp.einsum('etf,efd->etd', h, w2) + b2[:, None, :]
        out = jnp.take_along_axis(y, idx[None, :, None], axis=0)[0]
        out = out * scores
        return out.reshape(b, t, c)
    x = x + jnp.tanh(g_xattn[0]) * _L0_xattn_ref(_layernorm(x, axis=-1), ctx_1024, ctx_1024, fside_BxSxS2_0, mask_BxSxS2_ik1, L0_xattn_wq_k, L0_xattn_wq_b, L0_xattn_wk_k, L0_xattn_wk_b, L0_xattn_wv_k, L0_xattn_wv_b, L0_xattn_wo_k, L0_xattn_wo_b)
    x = x + jnp.tanh(g_ffn[0]) * _L0_ffn_ref(_layernorm(x, axis=-1), L0_ffn_W1, L0_ffn_b1, L0_ffn_W2, L0_ffn_b2, L0_ffn_Wg, L0_ffn_bg)
    x = x + jnp.tanh(g_xattn[1]) * _L1_xattn_ref(_layernorm(x, axis=-1), ctx_1024, ctx_1024, mask_1x1xSxS2_ik0, L1_xattn_wq, L1_xattn_bq, L1_xattn_wk, L1_xattn_bk, L1_xattn_wv, L1_xattn_bv, L1_xattn_wo, L1_xattn_bo)
    x = x + jnp.tanh(g_ffn[1]) * _L1_ffn_ref(_layernorm(x, axis=-1), L1_ffn_w_red, L1_ffn_wg, L1_ffn_w1, L1_ffn_b1, L1_ffn_w2, L1_ffn_b2)
    return x

_drawn_inputs = setup_inputs


def setup_inputs(seed=0):
    import zlib

    import numpy as np

    out = dict(_drawn_inputs(seed))
    spreads = {'g_ffn': (-1.0, 0.6),
     'L0_xattn_wq_b': (0.0, 0.8),
     'L0_xattn_wk_b': (0.0, 0.8),
     'L0_xattn_wv_b': (0.0, 0.1),
     'L0_xattn_wo_b': (0.0, 0.1),
     'L0_ffn_b1': (0.0, 0.686),
     'L0_ffn_b2': (0.0, 0.1),
     'L0_ffn_bg': (0.0, 0.1)}
    factors = {'fside_BxSxS2_0': 5.072,
     'L1_xattn_bq': 3.236,
     'L1_xattn_bk': 8.0,
     'L1_ffn_w_red': 8.0,
     'L1_ffn_wg': 8.0,
     'L1_ffn_w1': 8.0,
     'L1_ffn_b1': 8.0,
     'L1_ffn_w2': 8.0,
     'L1_ffn_b2': 8.0}
    for name, (base, spread) in spreads.items():
        noise = np.random.default_rng([zlib.crc32(name.encode()), seed]).standard_normal(out[name].shape)
        drawn = base * np.exp(spread * noise) if base else spread * noise
        out[name] = jnp.asarray(drawn.astype(out[name].dtype))
    for name, factor in factors.items():
        out[name] = (out[name] * factor).astype(out[name].dtype)
    return out
```

```python
from contextlib import ExitStack, nullcontext

import numpy as np

import concourse.bass as bass
from concourse import mybir

F32 = mybir.dt.float32
BF16 = mybir.dt.bfloat16
I32 = mybir.dt.int32
U32 = mybir.dt.uint32
ALU = mybir.AluOpType
ACT = mybir.ActivationFunctionType
AX = mybir.AxisListType

P = 128
B, S, D = 16, 256, 128
S2 = 1601
H, DH = 16, 8
T = B * S
NT = T // P
E, F = 8, 512
FT = F // P
KT = -(-S2 // P)
TAIL = S2 - (KT - 1) * P
HG = 4
NG = H // HG
QT = S // P
STEPS = QT * NG
UNITS = STEPS * HG
TERMS = ((0, 0), (1, 0), (2, 0), (0, 1), (1, 1), (0, 2))
NTERM = len(TERMS)
ROWS = NTERM * DH
SCALE = float(DH) ** -0.5
EPS = 1e-5
BANK = 512
KCUTS = [(n, min(n + BANK, S2)) for n in range(0, S2, BANK)]
CH = 512
NC = T // CH
TPC = CH // P
LATE = 9


def width(kt):
    return P if kt < KT - 1 else TAIL


def held(count):
    return max(count, 0) if isinstance(count, int) else count


def looped(engine, first, last, body):
    body(first, first == last - 1)
    if last - first > 2:
        with engine.Fori(first + 1, last - 1) as i:
            body(i, False)
    if last - first > 1:
        body(last - 1, True)


def on_path(engine, kept, late):
    if late is None:
        return nullcontext()
    return engine.If(engine.value_load(kept["late_only"][0:1, 0:1], min_val=0, max_val=1) == late)


class Chip:

    def __init__(self, nc, ctx, phase):
        self.nc, self.ctx, self.phase, self.semaphores = nc, ctx, phase, []
        ctx.callback(self.clear)

    def clear(self):
        with self.nc.Block() as block:
            @block.sync
            def _(sp):
                for s in self.semaphores:
                    sp.sem_clear(s)

        for s in self.semaphores:
            self.nc.release_semaphore(s)

    def sb(self, name, shape, dt=F32):
        return self.ctx.enter_context(self.nc.sbuf_tensor(f"{self.phase}_{name}", shape, dt))

    def ps(self, name, shape, dt=F32):
        return self.ctx.enter_context(self.nc.psum_tensor(f"{self.phase}_{name}", shape, dt))

    def sem(self, name):
        s = self.nc.alloc_semaphore(name=f"{self.phase}_{name}")
        self.semaphores.append(s)
        return s


def constants(nc, kept, w):
    ident, gates, late_only = kept["ident"], kept["gates"], kept["late_only"]
    with ExitStack() as ctx:
        c = Chip(nc, ctx, "const")
        loaded, cleared, made, done = c.sem("loaded"), c.sem("cleared"), c.sem("made"), c.sem("done")
        mask_in, hidden_made, none_made, path_made, summed = (
            c.sem(n) for n in ("mask_in", "hidden_made", "none_made", "path_made", "summed"))
        raw = c.sb("raw_gates", [P, 4])
        mask, hidden = c.sb("mask", [P, QT, S2], I32), c.sb("hidden", [P, QT, S2])
        none_early, none_late, fits = c.sb("none_early", [P, QT]), c.sb("none_late", [P, QT]), c.sb("fits", [P, QT])
        ones, sum_ps = c.sb("ones", [P, 1]), c.ps("sum_ps", [P, BANK])
        with nc.Block() as block:
            @block.sync
            def _(sp):
                for n, g in enumerate((w["g_xattn"], w["g_ffn"])):
                    sp.dma_start(raw[:, 2 * n:2 * n + 2], g.partition_broadcast(P)).then_inc(loaded, 16)
                sp.dma_start(mask[:], w["mask1"].rearrange("(t p) k -> p t k", p=P)).then_inc(mask_in, 16)

            @block.gpsimd
            def _(pool):
                nc.gpsimd.memset(ones[:], 1.0).then_inc(cleared, 1)
                nc.gpsimd.memset(ident[:], 0.0).then_inc(cleared, 1)
                pool.wait_ge(cleared, 2)
                nc.gpsimd.affine_select(out=ident[:], in_=ident[:], compare_op=ALU.not_equal, fill=1.0,
                                        base=0, pattern=[[-1, P]], channel_multiplier=1).then_inc(made, 1)
                pool.wait_ge(made, 1)

            @block.scalar
            def _(act):
                act.wait_ge(loaded, 32)
                nc.scalar.activation(gates[:], raw[:], ACT.Tanh).then_inc(done, 1)
                act.wait_ge(done, 1)

            @block.vector
            def _(dve):
                dve.wait_ge(mask_in, 16)
                nc.vector.tensor_scalar(hidden[:], mask[:], 0.0, 1.0, ALU.is_equal, ALU.mult).then_inc(hidden_made, 1)
                dve.wait_ge(hidden_made, 1)
                nc.vector.tensor_reduce(none_early[:], hidden[:, :, 0:LATE * P], AX.X, ALU.min)
                nc.vector.tensor_reduce(none_late[:], hidden[:, :, LATE * P:], AX.X, ALU.min).then_inc(none_made, 1)
                dve.wait_ge(none_made, 1)
                nc.vector.tensor_tensor(fits[:], none_early[:], none_late[:], ALU.subtract).then_inc(path_made, 1)
                dve.wait_ge(summed, 1)
                nc.vector.tensor_scalar(late_only[:], sum_ps[0:1, 0:1], float(S), None, ALU.is_equal).then_inc(path_made, 1)
                dve.wait_ge(path_made, 2)

            @block.tensor
            def _(pe):
                pe.wait_ge(cleared, 2)
                pe.wait_ge(path_made, 1)
                for qt in range(QT):
                    last = nc.tensor.matmul(sum_ps[0:1, 0:1], ones[:], fits[:, qt:qt + 1], start=(qt == 0), stop=(qt == QT - 1))
                last.then_inc(summed, 1)


def context_phase(nc, kept, w, k_stack, v_rows):
    with ExitStack() as ctx:
        c = Chip(nc, ctx, "context")
        wk, wv = c.sb("wk", [P, 2, P]), c.sb("wv", [P, 2 * P])
        bk, bv = c.sb("bk", [P, 2]), c.sb("bv", [P, 2 * P])
        ctx_t = c.sb("ctx_t", [P, 2, S2])
        part = [[[c.sb(f"part{s}{l}{n}", [P, S2], BF16) for n in range(3)] for l in range(2)] for s in range(2)]
        rest = [c.sb(f"rest{l}", [P, S2]) for l in range(2)]
        v_stage = c.sb("v_stage", [P, 2, 2, NG, KT, 32])
        k_ps = c.ps("k_ps", [P, 4, BANK])
        v_ps = c.ps("v_ps", [P, 2, 4, 2 * P])
        weights_in, zeroed = c.sem("weights_in"), c.sem("zeroed")
        ctx_in = [c.sem(f"ctx_in{s}") for s in range(2)]
        k_made, v_made = c.sem("k_made"), c.sem("v_made")
        high_made, rest_made, mid_made, low_made = (c.sem(n) for n in ("high_made", "rest_made", "mid_made", "low_made"))
        v_out = c.sem("v_out")
        k_stored = [c.sem(f"k_stored{s}") for s in range(2)]
        v_stored = [c.sem(f"v_stored{s}") for s in range(2)]
        VC = -(-KT // 4)
        kview = k_ps[:].rearrange("p a b -> p (a b)")[:, 0:S2]

        with nc.Block() as block:
            @block.sync
            def _(sp):
                for l in range(2):
                    sp.dma_start(wk[:, l, :], w[f"wk{l}"]).then_inc(weights_in, 16)
                    sp.dma_start(wv[:, l * P:(l + 1) * P], w[f"wv{l}"]).then_inc(weights_in, 16)
                    sp.dma_start(bk[:, l:l + 1], w[f"bk{l}"]).then_inc(weights_in, 16)
                    sp.dma_start(bv[:, l * P:(l + 1) * P], w[f"bv{l}"].partition_broadcast(P)).then_inc(weights_in, 16)
                for s in range(2):
                    sp.dma_start(ctx_t[:, s, :], w["ctx_t"][s]).then_inc(ctx_in[s], 16)

                def store_keys(b, s, l, first):
                    for t, (_, kp) in enumerate(TERMS):
                        sp.dma_start(k_stack[l, b, :, t * DH:(t + 1) * DH, first * P:],
                                     part[s][l][kp][:, first * P:]).then_inc(k_stored[s], 16)

                def store_values(b, s, l, first):
                    sp.dma_start(v_rows[l, b, :, :, first:].rearrange("g p k c -> p g k c"),
                                 v_stage[:, s, l, :, first:]).then_inc(v_stored[s], 16)

                late_only = sp.value_load(kept["late_only"][0:1, 0:1], min_val=0, max_val=1)

                def two_batches(i, _):
                    for s in range(2):
                        b = i * 2 + s
                        sp.wait_ge(low_made, b * 2 + 1)
                        store_keys(b, s, 0, 0)
                        sp.wait_ge(low_made, b * 2 + 2)
                        sp.wait_ge(v_out, b * VC + VC)
                        store_values(b, s, 0, 0)
                        with sp.If(late_only == 1):
                            store_keys(b, s, 1, LATE)
                            store_values(b, s, 1, LATE)
                        with sp.Else():
                            store_keys(b, s, 1, 0)
                            store_values(b, s, 1, 0)

                looped(sp, 0, B // 2, two_batches)
                for s in range(2):
                    sp.wait_ge(k_stored[s], B // 2 * 2 * NTERM * 16)
                    sp.wait_ge(v_stored[s], B // 2 * 2 * 16)

            @block.gpsimd
            def _(pool):
                nc.gpsimd.memset(v_stage[:], 0.0).then_inc(zeroed, 1)

                def two_batches(i, _):
                    for s in range(2):
                        b = i * 2 + s
                        for l in range(2):
                            pool.wait_ge(mid_made, b * 2 + l + 1)
                            nc.gpsimd.tensor_tensor(part[s][l][2][:], rest[l][:], part[s][l][1][:],
                                                    ALU.subtract).then_inc(low_made, 1)

                looped(pool, 0, B // 2, two_batches)

            @block.tensor
            def _(pe):
                pe.wait_ge(weights_in, 8 * 16)

                def two_batches(i, _):
                    for s in range(2):
                        b = i * 2 + s
                        pe.wait_ge(ctx_in[s], i * 16 + 16)
                        for l in range(2):
                            pe.wait_ge(rest_made, b * 2 + l)
                            for n0, n1 in KCUTS:
                                last = nc.tensor.matmul(kview[:, n0:n1], wk[:, l, :], ctx_t[:, s, n0:n1], start=True, stop=True)
                            last.then_inc(k_made, 1)
                            for v in range(2 * l, 2 * l + 2):
                                pe.wait_ge(v_out, held(b * VC + v - 1))
                                for kt in range(4 * v, min(4 * v + 4, KT)):
                                    last = nc.tensor.matmul(v_ps[0:width(kt), v % 2, kt % 4, :],
                                                            ctx_t[:, s, kt * P:kt * P + width(kt)], wv[:], start=True, stop=True)
                                last.then_inc(v_made, 1)

                looped(pe, 0, B // 2, two_batches)

            @block.scalar
            def _(act):
                act.wait_ge(weights_in, 8 * 16)

                def two_batches(i, ends):
                    for s in range(2):
                        b = i * 2 + s
                        for l in range(2):
                            act.wait_ge(k_made, b * 2 + l + 1)
                            if l == 0:
                                act.wait_ge(k_stored[s], i * (2 * NTERM * 16))
                            nc.scalar.activation(part[s][l][0][:], kview, ACT.Identity, bias=bk[:, l:l + 1]).then_inc(high_made, 1)
                            act.wait_ge(rest_made, b * 2 + l + 1)
                            nc.scalar.copy(part[s][l][1][:], rest[l][:]).then_inc(mid_made, 1)
                        if not ends:
                            act.wait_ge(v_made, b * VC + VC)
                            act.dma_start(ctx_t[:, s, :], w["ctx_t"][b + 2]).then_inc(ctx_in[s], 16)

                looped(act, 0, B // 2, two_batches)

            @block.vector
            def _(dve):
                dve.wait_ge(weights_in, 8 * 16)
                dve.wait_ge(zeroed, 1)

                def two_batches(i, _):
                    for s in range(2):
                        b = i * 2 + s
                        for l in range(2):
                            dve.wait_ge(high_made, b * 2 + l + 1)
                            dve.wait_ge(low_made, held(b * 2 + l - 1))
                            nc.vector.scalar_tensor_tensor(out=rest[l][:], in0=kview, scalar=bk[:, l:l + 1],
                                                           in1=part[s][l][0][:], op0=ALU.add, op1=ALU.subtract).then_inc(rest_made, 1)
                            for v in range(2 * l, 2 * l + 2):
                                dve.wait_ge(v_made, b * VC + v + 1)
                                if v == 0:
                                    dve.wait_ge(v_stored[s], i * 32)
                                n = min(4, KT - 4 * v)
                                m = width(4 * v)
                                for k in range(2):
                                    last = nc.vector.tensor_tensor(
                                        v_stage[0:m, s, k, :, 4 * v:4 * v + n, :].rearrange("p g k c -> p k g c"),
                                        v_ps[0:m, v % 2, 0:n, k * P:(k + 1) * P].rearrange("p k (g c) -> p k g c", g=NG),
                                        bv[0:m, None, k * P:(k + 1) * P].rearrange("p k (g c) -> p k g c", g=NG).broadcast_to([m, n, NG, 32]),
                                        ALU.add)
                                last.then_inc(v_out, 1)

                looped(dve, 0, B // 2, two_batches)


def queries_phase(nc, kept, w, layer, x_rows, q_stack):
    ident = kept["ident"]
    with ExitStack() as ctx:
        c = Chip(nc, ctx, f"queries{layer}")
        wq, bq = c.sb("wq", [P, P]), c.sb("bq", [P, 1])
        x_in = c.sb("x_in", [P, 2, TPC, P])
        stats, moments = c.sb("stats", [P, TPC, 6]), c.sb("moments", [P, TPC, 2])
        deviation, inverse = c.sb("deviation", [P, TPC]), c.sb("inverse", [P, TPC])
        normed = c.sb("normed", [P, 2, TPC, P])
        x_t = c.sb("x_t", [P, 2, CH])
        scaled, rest = c.sb("scaled", [P, CH]), c.sb("rest", [P, CH])
        part = [[c.sb(f"part{s}{n}", [P, CH], BF16) for n in range(3)] for s in range(2)]
        t_ps, q_ps = c.ps("t_ps", [P, 2, BANK]), c.ps("q_ps", [P, 2, BANK])
        weights_in = c.sem("weights_in")
        x_loaded = [c.sem(f"x_loaded{s}") for s in range(2)]
        stats_made, moments_made, var_made, root_made, inverse_made, normed_made = (
            c.sem(n) for n in ("stats_made", "moments_made", "var_made", "root_made", "inverse_made", "normed_made"))
        turned, x_t_made, q_made, scaled_made, high_made, rest_made, mid_made, low_made = (
            c.sem(n) for n in ("turned", "x_t_made", "q_made", "scaled_made", "high_made", "rest_made", "mid_made", "low_made"))
        stored = [c.sem(f"stored{s}") for s in range(2)]
        per = CH // S

        with nc.Block() as block:
            @block.sync
            def _(sp):
                sp.dma_start(wq[:], w[f"wq{layer}"]).then_inc(weights_in, 16)
                sp.dma_start(bq[:], w[f"bq{layer}"]).then_inc(weights_in, 16)
                for s in range(2):
                    sp.dma_start(x_in[:, s], x_rows[s * TPC:(s + 1) * TPC].rearrange("j p d -> p j d")).then_inc(x_loaded[s], 16)

                def two_chunks(i, ends):
                    for s in range(2):
                        n = i * 2 + s
                        if not ends:
                            sp.wait_ge(normed_made, n + 1)
                            sp.dma_start(x_in[:, s], x_rows[bass.ds((n + 2) * TPC, TPC)].rearrange("j p d -> p j d")).then_inc(x_loaded[s], 16)
                        sp.wait_ge(low_made, n + 1)
                        for t, (qp, _) in enumerate(TERMS):
                            for k in range(per):
                                sp.dma_start(q_stack[layer, n * per + k, :, t * DH:(t + 1) * DH, :],
                                             part[s][qp][:, k * S:(k + 1) * S]).then_inc(stored[s], 16)

                looped(sp, 0, NC // 2, two_chunks)
                for s in range(2):
                    sp.wait_ge(stored[s], NC // 2 * NTERM * per * 16)

            @block.vector
            def _(dve):
                dve.wait_ge(weights_in, 32)

                def two_chunks(i, _):
                    for s in range(2):
                        n = i * 2 + s
                        dve.wait_ge(x_loaded[s], i * 16 + 16)
                        for j in range(TPC):
                            last = nc.vector.bn_stats(stats[:, j], x_in[:, s, j])
                        last.then_inc(stats_made, 1)
                        dve.wait_ge(stats_made, n + 1)
                        dve.nop(nofuse=True)
                        for j in range(TPC):
                            last = nc.vector.bn_aggr(moments[:, j], stats[:, j])
                        last.then_inc(moments_made, 1)
                        dve.wait_ge(moments_made, n + 1)
                        nc.vector.tensor_scalar(deviation[:], moments[:, :, 1], EPS, None, ALU.add).then_inc(var_made, 1)
                        dve.wait_ge(root_made, n + 1)
                        nc.vector.reciprocal(inverse[:], deviation[:]).then_inc(inverse_made, 1)
                        dve.wait_ge(inverse_made, n + 1)
                        dve.wait_ge(turned, n)
                        for j in range(TPC):
                            last = nc.vector.tensor_scalar(normed[:, s, j], x_in[:, s, j], moments[:, j, 0:1], inverse[:, j:j + 1],
                                                           ALU.subtract, ALU.mult)
                        last.then_inc(normed_made, 1)
                        dve.wait_ge(q_made, n + 1)
                        nc.vector.tensor_scalar(scaled[:], q_ps[:, s], bq[:], -SCALE, ALU.add, ALU.mult).then_inc(scaled_made, 1)
                        dve.wait_ge(high_made, n + 1)
                        nc.vector.tensor_tensor(rest[:], scaled[:], part[s][0][:], ALU.subtract).then_inc(rest_made, 1)
                        dve.wait_ge(mid_made, n + 1)
                        nc.vector.tensor_tensor(part[s][2][:], rest[:], part[s][1][:], ALU.subtract).then_inc(low_made, 1)

                looped(dve, 0, NC // 2, two_chunks)

            @block.scalar
            def _(act):

                def two_chunks(i, _):
                    for s in range(2):
                        n = i * 2 + s
                        act.wait_ge(var_made, n + 1)
                        nc.scalar.activation(deviation[:], deviation[:], ACT.Sqrt).then_inc(root_made, 1)
                        act.wait_ge(turned, n + 1)
                        nc.scalar.copy(x_t[:, s], t_ps[:, s]).then_inc(x_t_made, 1)
                        act.wait_ge(scaled_made, n + 1)
                        act.wait_ge(stored[s], i * (NTERM * per * 16))
                        nc.scalar.copy(part[s][0][:], scaled[:]).then_inc(high_made, 1)
                        act.wait_ge(rest_made, n + 1)
                        nc.scalar.copy(part[s][1][:], rest[:]).then_inc(mid_made, 1)

                looped(act, 0, NC // 2, two_chunks)

            @block.tensor
            def _(pe):
                pe.wait_ge(weights_in, 32)

                def two_chunks(i, _):
                    for s in range(2):
                        n = i * 2 + s
                        pe.wait_ge(normed_made, n + 1)
                        pe.wait_ge(x_t_made, n)
                        for j in range(TPC):
                            last = nc.tensor.transpose(t_ps[:, s, j * P:(j + 1) * P], normed[:, s, j], ident[:])
                        last.then_inc(turned, 1)
                        pe.wait_ge(x_t_made, n + 1)
                        pe.wait_ge(scaled_made, n)
                        nc.tensor.matmul(q_ps[:, s], wq[:], x_t[:, s], start=True, stop=True).then_inc(q_made, 1)

                looped(pe, 0, NC // 2, two_chunks)


def attention_phase(nc, kept, w, layer, k_stack, v_rows, q_stack, x_rows, x_new_rows,
                    first=0, late=None):
    weigh = layer == 0
    KEY0, KEYS, KT = first * P, S2 - first * P, -(-S2 // P) - first
    key_cuts = [(n, min(n + BANK, KEYS)) for n in range(0, KEYS, BANK)]
    GT = 8 if weigh else 0
    by_act = {0, 2} if first else set(range(8))
    by_dve = [k for k in range(KT) if k not in by_act]
    QUARTER = [0, 1, 2, 3, 4] if first else [0, 3, 6, 9, KT]
    order = [0, 1, 2, 3] if first else [0, 1, 8, 2, 3, 9, 4, 5, 10, 6, 7, 11, 12]
    NA, NV = len(by_act), len(by_dve)
    rank = {k: sum((m in by_act) == (k in by_act) for m in order[:n]) for n, k in enumerate(order)}
    CHUNKS = STEPS * KT
    NPT = 4
    LAG = 2
    END = min(LAG + 3, KT - 1)
    NSCORE = 4 // len(key_cuts)
    AHEAD = 6
    NSLOT = 16
    ident, gates = kept["ident"], kept["gates"]

    with ExitStack() as ctx:
        c = Chip(nc, ctx, f"attention{layer}{'late' if first else ''}")
        keys, queries = c.sb("keys", [P, NG, 2, KEYS], BF16), c.sb("queries", [P, QT, NG, 2, P], BF16)
        values = c.sb("values", [P, NG, KT, 32])
        mask, away = c.sb("mask", [P, QT, KEYS], I32), c.sb("away", [P, QT, KEYS])
        if weigh:
            side = c.sb("side", [P, QT, GT * P])
            side_t = c.sb("side_t", [P, QT, KT - GT, P])
        prob = c.sb("prob", [P, NSLOT, KEYS])
        lowest, total, inverse = c.sb("lowest", [P, UNITS]), c.sb("total", [P, UNITS]), c.sb("inverse", [P, UNITS])
        turned_sb = c.sb("turned_sb", [P, NPT, BANK])
        o_sb, o_rows, o_t = c.sb("o_sb", [P, P]), c.sb("o_rows", [P, P]), c.sb("o_t", [P, P])
        wo, bo = c.sb("wo", [P, P]), c.sb("bo", [P, P])
        x_old, x_new = c.sb("x_old", [P, QT, P]), c.sb("x_new", [P, QT, P])
        s_ps, t_ps = c.ps("s_ps", [P, 4, BANK]), c.ps("t_ps", [P, 2, BANK])
        o_ps = c.ps("o_ps", [P, 2, 4, P])

        def scores(u):
            at = u % NSCORE * len(key_cuts) * BANK
            return s_ps[:].rearrange("p a b -> p (a b)")[:, at:at + KEYS]

        def key_width(kt):
            return P if kt < KT - 1 else TAIL

        weights_in, bias_made, o_cleared = c.sem("weights_in"), c.sem("bias_made"), c.sem("o_cleared")
        keys_in = [c.sem(f"keys_in{g}") for g in range(NG)]
        values_in = [c.sem(f"values_in{g}") for g in range(NG)]
        queries_in, mask_in, side_in, side_t_in, x_in, x_stored = (
            [c.sem(f"{n}{q}") for q in range(QT)] for n in ("queries_in", "mask_in", "side_in", "side_t_in", "x_in", "x_stored"))
        away_made, x_ready = c.sem("away_made"), c.sem("x_ready")
        scored, masked, exped, weighted = (c.sem(n) for n in ("scored", "masked", "exped", "weighted"))
        turned, out_by_act, out_by_dve, valued = (c.sem(n) for n in ("turned", "out_by_act", "out_by_dve", "valued"))
        o_out, o_turned, inverse_made, o_normed = (c.sem(n) for n in ("o_out", "o_turned", "inverse_made", "o_normed"))
        rows_turned, rows_out, projected, finished = (c.sem(n) for n in ("rows_turned", "rows_out", "projected", "finished"))

        def walk(b, last, unit=None, turn=None, value=None, fetch=None, step_end=None, unit_late=False):
            ahead = AHEAD - 1 if unit_late else AHEAD
            for s in range(STEPS):
                for j in range(HG):
                    if unit and not unit_late:
                        one_unit(b, last, s * HG + j + ahead, unit)
                    for pos in range(QUARTER[j], QUARTER[j + 1]):
                        if turn:
                            turn(b, s, pos)
                        at = s * KT + pos - LAG
                        if value and at >= 0:
                            value(b, at // KT, at % KT)
                        if s and pos == LAG and fetch:
                            fetch(b, s - 1)
                        if s and pos == END and step_end:
                            step_end(b, s - 1)
                    if unit and unit_late:
                        one_unit(b, last, s * HG + j + ahead, unit)
            for at in range(CHUNKS - LAG, CHUNKS):
                if value:
                    value(b, at // KT, at % KT)
            if fetch:
                fetch(b, STEPS - 1)
            if step_end:
                step_end(b, STEPS - 1)

        def one_unit(b, last, u, unit):
            if u < UNITS:
                unit(b, u // HG, u % HG)
            elif not last:
                unit(b + 1, (u - UNITS) // HG, u % HG)

        with nc.Block() as block:
            @block.sync
            def _(sp):
                with on_path(sp, kept, late):
                    sp.dma_start(wo[:], w[f"wo{layer}"]).then_inc(weights_in, 16)
                    sp.dma_start(bo[:], w[f"bo{layer}"].partition_broadcast(P)).then_inc(weights_in, 16)

                    def load_queries(b, qt):
                        for par in range(2):
                            for k in range(2):
                                sp.dma_start(queries[par * 64:par * 64 + ROWS, qt, :, k, :],
                                             q_stack[layer, b, 2 * par + k:H:HG, :, qt * P:(qt + 1) * P].rearrange("g r q -> r g q")
                                             ).then_inc(queries_in[qt], 16)

                    def load_rows(b, qt):
                        rows = slice(qt * P, (qt + 1) * P)
                        if weigh:
                            sp.dma_start(mask[:, qt], w["mask0"][b, rows, KEY0:]).then_inc(mask_in[qt], 16)
                            sp.dma_start(side[:, qt], w["side"][b, rows, 0:GT * P]).then_inc(side_in[qt], 16)
                            sp.dma_start(side_t[:, qt, 0:KT - GT - 1],
                                         w["side_t"][b, 0:(KT - GT - 1) * P, rows].rearrange("(k p) q -> p k q", p=P)).then_inc(side_t_in[qt], 16)
                            sp.dma_start(side_t[0:TAIL, qt, KT - GT - 1],
                                         w["side_t"][b, (KT - GT - 1) * P:, rows]).then_inc(side_t_in[qt], 16)
                        sp.dma_start(x_old[:, qt], x_rows[b * QT + qt]).then_inc(x_in[qt], 16)

                    def load_keys(b, g):
                        for par in range(2):
                            h = g * HG + 2 * par
                            sp.dma_start(keys[par * 64:par * 64 + ROWS, g], k_stack[layer, b, h:h + 2, :, KEY0:].rearrange("h r s -> r h s")
                                         ).then_inc(keys_in[g], 16)

                    def load_values(b, g):
                        sp.dma_start(values[:, g], v_rows[layer, b, g, :, first:]).then_inc(values_in[g], 16)

                    def store(b, qt):
                        sp.wait_ge(finished, b * QT + qt + 1)
                        sp.dma_start(x_new_rows[b * QT + qt], x_new[:, qt]).then_inc(x_stored[qt], 16)

                    load_queries(0, 0)
                    load_keys(0, 0)
                    if not weigh:
                        for qt in range(QT):
                            sp.dma_start(mask[:, qt], w["mask1"][qt * P:(qt + 1) * P, KEY0:]).then_inc(mask_in[qt], 16)
                    load_rows(0, 0)
                    load_values(0, 0)
                    for g in range(1, NG):
                        load_keys(0, g)
                        load_values(0, g)
                    load_queries(0, 1)
                    load_rows(0, 1)

                    def free_rows(b, qt):
                        sp.wait_ge(masked, b * UNITS + (qt + 1) * NG * HG)
                        if weigh:
                            sp.wait_ge(weighted, b * UNITS + (qt + 1) * NG * HG)
                            sp.wait_ge(out_by_dve, (b * STEPS + (qt + 1) * NG) * NV)

                    def fetch_next(b, ends):
                        if ends:
                            store(b, 0)
                            store(b, 1)
                            return
                        sp.wait_ge(scored, b * UNITS + NG * HG)
                        load_queries(b + 1, 0)
                        for g in range(NG):
                            sp.wait_ge(scored, b * UNITS + (NG + g + 1) * HG)
                            load_keys(b + 1, g)
                            if g:
                                sp.wait_ge(valued, (b * STEPS + NG + g) * KT)
                                load_values(b + 1, g - 1)
                            if g == 1:
                                store(b, 0)
                                free_rows(b, 0)
                                load_rows(b + 1, 0)
                        load_queries(b + 1, 1)
                        sp.wait_ge(valued, (b + 1) * CHUNKS)
                        load_values(b + 1, NG - 1)
                        store(b, 1)
                        free_rows(b, 1)
                        load_rows(b + 1, 1)

                    looped(sp, 0, B, fetch_next)
                    for qt in range(QT):
                        sp.wait_ge(x_stored[qt], B * 16)

            @block.gpsimd
            def _(pool):
                with on_path(pool, kept, late):
                    def unit(b, s, j):
                        qt, g = s // NG, s % NG
                        if g == 0 and j == 0:
                            pool.wait_ge(bias_made, 1)
                            pool.wait_ge(x_in[qt], b * 16 + 16)
                            nc.gpsimd.tensor_tensor(x_old[:, qt], x_old[:, qt], bo[:], ALU.add).then_inc(x_ready, 1)
                            if weigh:
                                pool.wait_ge(side_in[qt], b * 16 + 16)
                        if weigh:
                            slot = (s * HG + j) % NSLOT
                            pool.wait_ge(exped, (b * STEPS + s) * HG + j + 1)
                            nc.gpsimd.tensor_tensor(prob[:, slot, 0:GT * P], prob[:, slot, 0:GT * P], side[:, qt], ALU.mult).then_inc(weighted, 1)

                    for u in range(AHEAD):
                        unit(0, u // HG, u % HG)
                    looped(pool, 0, B, lambda b, last: walk(b, last, unit))

            @block.tensor
            def _(pe):
                with on_path(pe, kept, late):
                    pe.wait_ge(weights_in, 32)
                    pe.wait_ge(o_cleared, 1)

                    def unit(b, s, j):
                        qt, g, par, k = s // NG, s % NG, j // 2, j % 2
                        if j == 0 and g == 0:
                            pe.wait_ge(queries_in[qt], b * 64 + 64)
                        if j == 0 and qt == 0:
                            pe.wait_ge(keys_in[g], b * 32 + 32)
                        pe.wait_ge(masked, held((b * STEPS + s) * HG + j + 1 - NSCORE))
                        rows = slice(par * 64, par * 64 + ROWS)
                        for n0, n1 in key_cuts:
                            last = nc.tensor.matmul(scores(s * HG + j)[:, n0:n1], queries[rows, qt, g, k, :], keys[rows, g, k, n0:n1], start=True, stop=True)
                        last.then_inc(scored, 1)

                    def turn(b, s, pos):
                        kt, n = order[pos], b * CHUNKS + s * KT + pos
                        if pos == 0:
                            pe.wait_ge(exped, (b * STEPS + s + 1) * HG)
                        if weigh and kt in by_act and rank[kt] == 0:
                            pe.wait_ge(weighted, (b * STEPS + s + 1) * HG)
                        was = order[(pos - 2) % KT]
                        back = s if pos >= 2 else s - 1
                        if was in by_act:
                            pe.wait_ge(out_by_act, held((b * STEPS + back) * NA + rank[was] + 1))
                        else:
                            pe.wait_ge(out_by_dve, held((b * STEPS + back) * NV + rank[was] + 1))
                        m = key_width(kt)
                        for j in range(HG):
                            last = nc.tensor.transpose(t_ps[0:m, (s * KT + pos) % 2, j * P:(j + 1) * P],
                                                       prob[:, (s * HG + j) % NSLOT, kt * P:kt * P + m], ident[:])
                        last.then_inc(turned, 1)

                    def value(b, s, pos):
                        kt, g, m = order[pos], s % NG, key_width(order[pos])
                        if pos == 0:
                            pe.wait_ge(o_normed, held(b * STEPS + s - 1))
                            if (s - 2) % NG == NG - 1:
                                pe.wait_ge(finished, held(b * QT + (s - 2) // NG + 1))
                            if s < NG:
                                pe.wait_ge(values_in[g], b * 16 + 16)
                        if kt in by_act:
                            pe.wait_ge(out_by_act, (b * STEPS + s) * NA + rank[kt] + 1)
                        else:
                            pe.wait_ge(out_by_dve, (b * STEPS + s) * NV + rank[kt] + 1)
                        for j in range(HG):
                            last = nc.tensor.matmul(o_ps[32 * j:32 * j + DH, s % 2, 0], values[0:m, g, kt, j * DH:(j + 1) * DH],
                                                    turned_sb[0:m, (s * KT + pos) % NPT, j * P:(j + 1) * P],
                                                    start=(pos == 0), stop=(pos == KT - 1))
                        last.then_inc(valued, 1)

                    def step_end(b, s):
                        qt, g = s // NG, s % NG
                        pe.wait_ge(o_out, b * STEPS + s + 1)
                        nc.tensor.transpose(o_ps[:, s % 2, 1], o_sb[:], ident[:]).then_inc(o_turned, 1)
                        if g == NG - 1:
                            pe.wait_ge(o_normed, b * STEPS + s + 1)
                            nc.tensor.transpose(o_ps[:, s % 2, 2], o_rows[:], ident[:]).then_inc(rows_turned, 1)
                            pe.wait_ge(rows_out, b * QT + qt + 1)
                            nc.tensor.matmul(o_ps[:, s % 2, 3], o_t[:], wo[:], start=True, stop=True).then_inc(projected, 1)

                    for u in range(AHEAD):
                        unit(0, u // HG, u % HG)
                    looped(pe, 0, B, lambda b, last: walk(b, last, unit, turn, value, None, step_end))

            @block.scalar
            def _(act):
                with on_path(act, kept, late):
                    def unit(b, s, j):
                        u = s * HG + j
                        slot = (s * HG + j) % NSLOT
                        act.wait_ge(masked, b * UNITS + u + 1)
                        nc.scalar.activation(prob[:, slot], prob[:, slot], ACT.Exp, bias=lowest[:, u:u + 1], scale=-1.0,
                                             accum_out=total[:, u:u + 1]).then_inc(exped, 1)

                    def turn(b, s, pos):
                        kt, n = order[pos], b * CHUNKS + s * KT + pos
                        if kt not in by_act:
                            return
                        act.wait_ge(turned, n + 1)
                        act.wait_ge(valued, held(n - NPT + 1))
                        m = key_width(kt)
                        nc.scalar.copy(turned_sb[0:m, (s * KT + pos) % NPT], t_ps[0:m, (s * KT + pos) % 2]).then_inc(out_by_act, 1)

                    def fetch(b, s):
                        act.wait_ge(valued, (b * STEPS + s + 1) * KT)
                        act.wait_ge(o_turned, b * STEPS + s)
                        nc.scalar.copy(o_sb[:], o_ps[:, s % 2, 0]).then_inc(o_out, 1)

                    def step_end(b, s):
                        qt, g = s // NG, s % NG
                        if g == NG - 1:
                            act.wait_ge(rows_turned, b * QT + qt + 1)
                            act.wait_ge(projected, b * QT + qt)
                            nc.scalar.copy(o_t[:], o_ps[:, s % 2, 2]).then_inc(rows_out, 1)

                    for u in range(AHEAD - 1):
                        unit(0, u // HG, u % HG)
                    looped(act, 0, B, lambda b, last: walk(b, last, unit, turn, None, fetch, step_end, unit_late=True))

            @block.vector
            def _(dve):
                with on_path(dve, kept, late):
                    nc.vector.memset(o_ps[:], 0.0).then_inc(o_cleared, 1)
                    dve.wait_ge(weights_in, 32)
                    nc.vector.tensor_scalar(bo[:], bo[:], gates[:, layer:layer + 1], None, ALU.mult).then_inc(bias_made, 1)

                    def push_away(b, qt):
                        if weigh:
                            dve.wait_ge(mask_in[qt], b * 16 + 16)
                            nc.vector.tensor_scalar(away[:, qt], mask[:, qt], -1e9, 1e9, ALU.mult, ALU.add).then_inc(away_made, 1)
                            dve.wait_ge(away_made, b * QT + qt + 1)
                        else:
                            dve.wait_ge(mask_in[qt], 16)
                            nc.vector.tensor_scalar(away[:, qt], mask[:, qt], 0.0, 1e30, ALU.is_equal, ALU.mult).then_inc(away_made, 1)
                            dve.wait_ge(away_made, qt + 1)

                    if not weigh:
                        for qt in range(QT):
                            push_away(0, qt)

                    def unit(b, s, j):
                        qt, g, u = s // NG, s % NG, s * HG + j
                        if weigh and g == 0 and j == 0:
                            push_away(b, qt)
                        dve.wait_ge(turned, held((b * STEPS + s + 1 - NSLOT // HG) * KT))
                        dve.wait_ge(scored, b * UNITS + u + 1)
                        dve.nop(nofuse=True)
                        nc.vector.tensor_tensor_reduce(prob[:, (s * HG + j) % NSLOT], scores(u), away[:, qt], 1.0, 3e38,
                                                       ALU.add, ALU.min, lowest[:, u:u + 1]).then_inc(masked, 1)

                    def turn(b, s, pos):
                        kt, n, qt = order[pos], b * CHUNKS + s * KT + pos, s // NG
                        if kt in by_act:
                            return
                        if weigh and s % NG == 0 and rank[kt] == 0:
                            dve.wait_ge(side_t_in[qt], b * 32 + 32)
                        dve.wait_ge(turned, n + 1)
                        dve.wait_ge(valued, held(n - NPT + 1))
                        m = key_width(kt)
                        out, bank = turned_sb[0:m, (s * KT + pos) % NPT], t_ps[0:m, (s * KT + pos) % 2]
                        if weigh:
                            last = nc.vector.tensor_tensor(out.rearrange("p (j q) -> p j q", j=HG), bank.rearrange("p (j q) -> p j q", j=HG),
                                                           side_t[0:m, qt, None, kt - GT, :].broadcast_to([m, HG, P]), ALU.mult)
                        else:
                            last = nc.vector.tensor_copy(out, bank)
                        last.then_inc(out_by_dve, 1)

                    def step_end(b, s):
                        qt, g, u = s // NG, s % NG, s * HG
                        dve.wait_ge(exped, (b * STEPS + s + 1) * HG)
                        nc.vector.reciprocal(inverse[:, u:u + HG], total[:, u:u + HG]).then_inc(inverse_made, 1)
                        dve.wait_ge(inverse_made, b * STEPS + s + 1)
                        if g == 0:
                            dve.wait_ge(rows_turned, b * QT + qt)
                        dve.wait_ge(o_turned, b * STEPS + s + 1)
                        nc.vector.tensor_tensor(o_rows[:, g * 32:(g + 1) * 32].rearrange("p (j d) -> p j d", d=DH),
                                                o_ps[:, s % 2, 1].rearrange("p (j x) -> p j x", j=HG)[:, :, 0:DH],
                                                inverse[:, u:u + HG, None].broadcast_to([P, HG, DH]), ALU.mult).then_inc(o_normed, 1)
                        if g == NG - 1:
                            dve.wait_ge(projected, b * QT + qt + 1)
                            dve.wait_ge(x_ready, b * QT + qt + 1)
                            dve.wait_ge(x_stored[qt], b * 16)
                            nc.vector.scalar_tensor_tensor(out=x_new[:, qt], in0=o_ps[:, s % 2, 3], scalar=gates[:, layer:layer + 1],
                                                           in1=x_old[:, qt], op0=ALU.mult, op1=ALU.add).then_inc(finished, 1)

                    for u in range(AHEAD):
                        unit(0, u // HG, u % HG)
                    looped(dve, 0, B, lambda b, last: walk(b, last, unit, turn, None, None, step_end))


def experts_phase(nc, kept, w, layer, x_rows, x_new_rows):
    EF = E * FT
    LAG = 3
    RING = 4
    experts = [e for e in range(E) if e % 2 == 0] + [e for e in range(E) if e % 2] if layer == 0 else list(range(E))
    ident, gates = kept["ident"], kept["gates"]
    GATE = 10 if layer == 0 else 8
    RED = 16

    with ExitStack() as ctx:
        c = Chip(nc, ctx, f"experts{layer}")
        w1, w2 = c.sb("w1", [P, E, F]), c.sb("w2", [P, E, FT, P])
        b1, b2 = c.sb("b1", [P, E, FT]), c.sb("b2", [E, P])
        x_in = c.sb("x_in", [P, 2, TPC, P])
        stats, moments = c.sb("stats", [P, TPC, 6]), c.sb("moments", [P, TPC, 2])
        deviation, inverse = c.sb("deviation", [P, TPC]), c.sb("inverse", [P, TPC])
        normed = c.sb("normed", [P, TPC, P])
        x_t = [c.sb(f"x_t{s}", [P, CH]) for s in range(2)]
        logits, top, index = c.sb("logits", [P, TPC, E]), c.sb("top", [P, TPC, E]), c.sb("index", [P, TPC, E], U32)
        chosen = c.sb("chosen", [P, TPC, 2])
        below, grown = c.sb("below", [P, TPC, E]), c.sb("grown", [P, TPC, E])
        first, second = c.sb("first", [P, TPC]), c.sb("second", [P, TPC])
        share, other = c.sb("share", [P, TPC, E]), c.sb("other", [P, TPC, E])
        share_t = [c.sb(f"share_t{s}", [E, CH]) for s in range(2)]
        number = c.sb("number", [P, E])
        pick = c.sb("pick", [E, E, P])
        acts, weighted = c.sb("acts", [P, RING, CH]), c.sb("weighted", [P, RING, CH])
        y_sb, x_new = c.sb("y_sb", [P, CH]), c.sb("x_new", [P, 2, TPC, P])
        if layer == 0:
            wg, bg = c.sb("wg", [P, E]), c.sb("bg", [P, E])
        else:
            w_red, wg, wg_t = c.sb("w_red", [P, RED]), c.sb("wg", [E, RED]), c.sb("wg_t", [RED, E])
            squares, norm = c.sb("squares", [E, RED]), c.sb("norm", [E, 4])
            reduced = c.sb("reduced", [RED, CH])
        h_ps, share_ps, y_ps = c.ps("h_ps", [P, 2, BANK]), c.ps("share_ps", [P, 2, BANK]), c.ps("y_ps", [P, 2, BANK])
        small_ps, o_ps = c.ps("small_ps", [P, BANK]), c.ps("o_ps", [P, BANK])

        small_in, weights_in, setup, wg_rooted, wg_turned = (c.sem(n) for n in ("small_in", "weights_in", "setup", "wg_rooted", "wg_turned"))
        numbered = c.sem("numbered")
        x_loaded = [c.sem(f"x_loaded{s}") for s in range(2)]
        stats_made, moments_made, var_made, root_made, inverse_made, normed_made = (
            c.sem(n) for n in ("stats_made", "moments_made", "var_made", "root_made", "inverse_made", "normed_made"))
        turned, x_t_made, reduced_made, reduced_out, gated, below_made, grown_made, gate_step, share_turned, share_t_made = (
            c.sem(n) for n in ("turned", "x_t_made", "reduced_made", "reduced_out", "gated", "below_made", "grown_made", "gate_step",
                               "share_turned", "share_t_made"))
        shared, upped, acted, shares_on, downed = (c.sem(n) for n in ("shared", "upped", "acted", "shares_on", "downed"))
        y_out, y_turned, added = c.sem("y_out"), c.sem("y_turned"), c.sem("added")
        stored = [c.sem(f"stored{s}") for s in range(2)]

        def walk(n, s, is_first, is_last, norm=None, gate=None, turn_share=None, spread=None, up=None, down=None, tail=None):
            if spread:
                spread(n, s, 0)
            for k in range(EF):
                if up:
                    up(n, s, k)
                if spread and k % FT == 1 and k // FT + 1 < E:
                    spread(n, s, k // FT + 1)
                if down and k >= LAG:
                    down(n, s, k - LAG)
                if tail and k == 5 and not is_first:
                    tail(n - 1, 1 - s)
                if norm and k == 6 and not is_last:
                    norm(n + 1, 1 - s)
                if gate and k == 12 and not is_last:
                    gate(n + 1, 1 - s)
                if turn_share and k == 24 and not is_last:
                    turn_share(n + 1, 1 - s)
            if down:
                for k in range(EF - LAG, EF):
                    down(n, s, k)
            if tail and is_last:
                tail(n, s)

        def two_chunks(i, **do):
            for s in range(2):
                n = i * 2 + s
                fixed = isinstance(n, int)
                walk(n, s, fixed and n == 0, fixed and n == NC - 1, **do)

        with nc.Block() as block:
            @block.sync
            def _(sp):
                def norm(n, s):
                    sp.wait_ge(added, held(n - 1))
                    sp.dma_start(x_in[:, s], x_rows[n * TPC:(n + 1) * TPC].rearrange("j p d -> p j d") if isinstance(n, int) else
                                 x_rows[bass.ds(n * TPC, TPC)].rearrange("j p d -> p j d")).then_inc(x_loaded[s], 16)

                def tail(n, s):
                    sp.wait_ge(added, n + 1)
                    sp.dma_start(x_new_rows[n * TPC:(n + 1) * TPC].rearrange("j p d -> p j d") if isinstance(n, int) else
                                 x_new_rows[bass.ds(n * TPC, TPC)].rearrange("j p d -> p j d"), x_new[:, s]).then_inc(stored[s], 16)

                sp.dma_start(b1[:], w[f"b1_{layer}"]).then_inc(small_in, 16)
                sp.dma_start(b2[:], w[f"b2_{layer}"]).then_inc(small_in, 16)
                if layer == 0:
                    sp.dma_start(wg[:], w["wg0"]).then_inc(small_in, 16)
                    sp.dma_start(bg[:], w["bg0"].partition_broadcast(P)).then_inc(small_in, 16)
                else:
                    sp.dma_start(wg[:], w["wg1"]).then_inc(small_in, 16)
                    sp.dma_start(w_red[:], w["w_red"]).then_inc(small_in, 16)
                norm(0, 0)
                sp.dma_start(w1[:], w[f"w1_{layer}"].rearrange("e d f -> d e f")).then_inc(weights_in, 16)
                for e in range(E):
                    sp.dma_start(w2[:, e], w[f"w2_{layer}"][e].rearrange("(t f) d -> f t d", f=P)).then_inc(weights_in, 16)

                looped(sp, 0, NC // 2, lambda i, _: two_chunks(i, norm=norm, tail=tail))
                for s in range(2):
                    sp.wait_ge(stored[s], NC // 2 * 16)

            @block.gpsimd
            def _(pool):
                nc.gpsimd.iota(number[:], pattern=[[1, E]], base=0, channel_multiplier=0, allow_small_or_imprecise_dtypes=True).then_inc(numbered, 1)

            @block.tensor
            def _(pe):
                pe.wait_ge(small_in, 4 * 16)
                if layer == 1:
                    pe.wait_ge(setup, 5)
                    nc.tensor.transpose(small_ps[0:RED, 0:E], wg[:], ident[0:E, 0:E]).then_inc(wg_turned, 1)
                    pe.wait_ge(setup, 6)

                def norm(n, s):
                    pe.wait_ge(normed_made, n + 1)
                    pe.wait_ge(share_t_made, n)
                    for j in range(TPC):
                        last = nc.tensor.transpose(small_ps[:, j * P:(j + 1) * P], normed[:, j], ident[:])
                    last.then_inc(turned, 1)

                def gate(n, s):
                    pe.wait_ge(x_t_made, n + 1)
                    if layer == 0:
                        for j in range(TPC):
                            last = nc.tensor.matmul(small_ps[:, j * E:(j + 1) * E], x_t[s][:, j * P:(j + 1) * P], wg[:], start=True, stop=True)
                    else:
                        nc.tensor.matmul(small_ps[0:RED, :], w_red[:], x_t[s][:], start=True, stop=True).then_inc(reduced_made, 1)
                        pe.wait_ge(reduced_out, n + 1)
                        for j in range(TPC):
                            last = nc.tensor.matmul(small_ps[:, j * E:(j + 1) * E], reduced[:, j * P:(j + 1) * P], wg_t[:], start=True, stop=True)
                    last.then_inc(gated, 1)

                def turn_share(n, s):
                    pe.wait_ge(gate_step, (n + 1) * GATE)
                    for j in range(TPC):
                        last = nc.tensor.transpose(small_ps[0:E, j * P:(j + 1) * P], share[:, j], ident[:])
                    last.then_inc(share_turned, 1)

                def spread(n, s, k):
                    if k == 0:
                        pe.wait_ge(share_t_made, n + 1)
                    pe.wait_ge(shares_on, held(n * EF + (k - 1) * FT))
                    nc.tensor.matmul(share_ps[:, k % 2], pick[:, experts[k]], share_t[s][:], start=True, stop=True).then_inc(shared, 1)
                    if k == 0:
                        pe.wait_ge(y_out, held(n - 1))
                        nc.tensor.matmul(y_ps[:, s], b2[:], share_t[s][:], start=True, stop=False)

                def up(n, s, k):
                    if k == 0 and isinstance(n, int) and n == 0:
                        pe.wait_ge(weights_in, (1 + E) * 16)
                    pe.wait_ge(acted, held(n * EF + k - 1))
                    nc.tensor.matmul(h_ps[:, k % 2], w1[:, experts[k // FT], (k % FT) * P:(k % FT + 1) * P], x_t[s][:],
                                     start=True, stop=True).then_inc(upped, 1)

                def down(n, s, k):
                    pe.wait_ge(shares_on, n * EF + k + 1)
                    nc.tensor.matmul(y_ps[:, s], w2[:, experts[k // FT], k % FT], weighted[:, k % RING],
                                     start=False, stop=(k == EF - 1)).then_inc(downed, 1)

                def tail(n, s):
                    pe.wait_ge(y_out, n + 1)
                    pe.wait_ge(added, n)
                    for j in range(TPC):
                        last = nc.tensor.transpose(o_ps[:, j * P:(j + 1) * P], y_sb[:, j * P:(j + 1) * P], ident[:])
                    last.then_inc(y_turned, 1)

                pe.wait_ge(setup, 1)
                norm(0, 0)
                gate(0, 0)
                turn_share(0, 0)
                looped(pe, 0, NC // 2, lambda i, _: two_chunks(i, norm=norm, gate=gate, turn_share=turn_share, spread=spread,
                                                               up=up, down=down, tail=tail))

            @block.scalar
            def _(act):
                act.wait_ge(small_in, 4 * 16)
                if layer == 1:
                    act.wait_ge(setup, 2)
                    nc.scalar.activation(norm[:, 1:2], norm[:, 0:1], ACT.Sqrt).then_inc(wg_rooted, 1)

                def norm_(n, s):
                    act.wait_ge(var_made, n + 1)
                    nc.scalar.activation(deviation[:], deviation[:], ACT.Sqrt).then_inc(root_made, 1)
                    act.wait_ge(turned, n + 1)
                    nc.scalar.copy(x_t[s][:], small_ps[:]).then_inc(x_t_made, 1)

                def gate(n, s):
                    if layer == 1:
                        act.wait_ge(reduced_made, n + 1)
                        nc.scalar.copy(reduced[:], small_ps[0:RED, :]).then_inc(reduced_out, 1)
                    act.wait_ge(below_made, n + 1)
                    nc.scalar.activation(grown[:], below[:], ACT.Exp).then_inc(grown_made, 1)

                def turn_share(n, s):
                    act.wait_ge(share_turned, n + 1)
                    nc.scalar.copy(share_t[s][:], small_ps[0:E, :]).then_inc(share_t_made, 1)

                def up(n, s, k):
                    e = experts[k // FT]
                    act.wait_ge(upped, n * EF + k + 1)
                    act.wait_ge(shares_on, held(n * EF + k + 1 - RING))
                    func = ACT.Silu if layer == 0 and e % 2 else ACT.Gelu
                    nc.scalar.activation(acts[:, k % RING], h_ps[:, k % 2], func, bias=b1[:, e, k % FT:k % FT + 1]).then_inc(acted, 1)

                def tail(n, s):
                    act.wait_ge(downed, (n + 1) * EF)
                    act.wait_ge(y_turned, n)
                    nc.scalar.activation(y_sb[:], y_ps[:, s], ACT.Copy, scale=gates[:, 2 + layer:3 + layer]).then_inc(y_out, 1)

                norm_(0, 0)
                gate(0, 0)
                turn_share(0, 0)
                looped(act, 0, NC // 2, lambda i, _: two_chunks(i, norm=norm_, gate=gate, turn_share=turn_share, up=up, tail=tail))

            @block.vector
            def _(dve):
                nc.vector.tensor_copy(pick[:], ident[0:E, 0:E, None].broadcast_to([E, E, P])).then_inc(setup, 1)
                if layer == 1:
                    dve.wait_ge(small_in, 4 * 16)
                    nc.vector.tensor_tensor_reduce(squares[:], wg[:], wg[:], 1.0, 0.0, ALU.mult, ALU.add, norm[:, 0:1]).then_inc(setup, 1)
                    dve.wait_ge(wg_rooted, 1)
                    nc.vector.tensor_scalar(norm[:, 2:3], norm[:, 1:2], 1e-4, None, ALU.max).then_inc(setup, 1)
                    dve.wait_ge(setup, 3)
                    nc.vector.reciprocal(norm[:, 3:4], norm[:, 2:3]).then_inc(setup, 1)
                    dve.wait_ge(setup, 4)
                    nc.vector.tensor_scalar(wg[:], wg[:], norm[:, 3:4], None, ALU.mult).then_inc(setup, 1)
                    dve.wait_ge(wg_turned, 1)
                    nc.vector.tensor_copy(wg_t[:], small_ps[0:RED, 0:E]).then_inc(setup, 1)
                dve.wait_ge(small_in, 4 * 16)
                dve.wait_ge(numbered, 1)

                def norm_(n, s):
                    dve.wait_ge(x_loaded[s], (n // 2 + 1) * 16 if isinstance(n, int) else n * 8 + (16 if s == 0 else 8))
                    for j in range(TPC):
                        last = nc.vector.bn_stats(stats[:, j], x_in[:, s, j])
                    last.then_inc(stats_made, 1)
                    dve.wait_ge(stats_made, n + 1)
                    dve.nop(nofuse=True)
                    for j in range(TPC):
                        last = nc.vector.bn_aggr(moments[:, j], stats[:, j])
                    last.then_inc(moments_made, 1)
                    dve.wait_ge(moments_made, n + 1)
                    nc.vector.tensor_scalar(deviation[:], moments[:, :, 1], EPS, None, ALU.add).then_inc(var_made, 1)
                    dve.wait_ge(root_made, n + 1)
                    nc.vector.reciprocal(inverse[:], deviation[:]).then_inc(inverse_made, 1)
                    dve.wait_ge(inverse_made, n + 1)
                    dve.wait_ge(turned, n)
                    for j in range(TPC):
                        last = nc.vector.tensor_scalar(normed[:, j], x_in[:, s, j], moments[:, j, 0:1], inverse[:, j:j + 1],
                                                       ALU.subtract, ALU.mult)
                    last.then_inc(normed_made, 1)

                def gate(n, s):
                    at = n * GATE

                    def step(k, ins):
                        ins.then_inc(gate_step, 1)
                        dve.wait_ge(gate_step, at + k)

                    dve.wait_ge(gated, n + 1)
                    dve.wait_ge(share_turned, n)
                    raw = small_ps[:, 0:TPC * E].rearrange("p (j e) -> p j e", e=E)
                    if layer == 0:
                        step(1, nc.vector.tensor_tensor(logits[:], raw, bg[:, None, :].broadcast_to([P, TPC, E]), ALU.add))
                    else:
                        step(1, nc.vector.tensor_copy(logits[:], raw))
                    dve.nop(nofuse=True)
                    for j in range(TPC):
                        last = nc.vector.max(top[:, j], logits[:, j])
                    step(2, last)
                    dve.nop(nofuse=True)
                    for j in range(TPC):
                        last = nc.vector.max_index(index[:, j], top[:, j], logits[:, j])
                    step(3, last)
                    nc.vector.tensor_tensor(below[:], logits[:] if layer else top[:], top[:, :, 0:1].broadcast_to([P, TPC, E]),
                                            ALU.subtract).then_inc(below_made, 1)
                    step(4, nc.vector.tensor_copy(chosen[:], index[:, :, 0:2]))
                    step(5, nc.vector.tensor_tensor(share[:], number[:, None, :].broadcast_to([P, TPC, E]),
                                                    chosen[:, :, 0:1].broadcast_to([P, TPC, E]), ALU.is_equal))
                    dve.wait_ge(grown_made, n + 1)
                    if layer == 0:
                        nc.vector.tensor_tensor(other[:], number[:, None, :].broadcast_to([P, TPC, E]),
                                                chosen[:, :, 1:2].broadcast_to([P, TPC, E]), ALU.is_equal)
                        step(6, nc.vector.tensor_scalar(second[:], grown[:, :, 1], 1.0, None, ALU.add))
                        step(7, nc.vector.reciprocal(first[:], second[:]))
                        step(8, nc.vector.tensor_tensor(second[:], grown[:, :, 1], first[:], ALU.mult))
                        nc.vector.tensor_tensor(share[:], share[:], first[:, :, None].broadcast_to([P, TPC, E]), ALU.mult)
                        step(9, nc.vector.tensor_tensor(other[:], other[:], second[:, :, None].broadcast_to([P, TPC, E]), ALU.mult))
                        nc.vector.tensor_tensor(share[:], share[:], other[:], ALU.add).then_inc(gate_step, 1)
                    else:
                        step(6, nc.vector.tensor_reduce(second[:], grown[:], AX.X, ALU.add))
                        step(7, nc.vector.reciprocal(first[:], second[:]))
                        nc.vector.tensor_tensor(share[:], share[:], first[:, :, None].broadcast_to([P, TPC, E]), ALU.mult).then_inc(gate_step, 1)

                def up(n, s, k):
                    if k % FT == 0:
                        dve.wait_ge(shared, n * E + k // FT + 1)
                    dve.wait_ge(acted, n * EF + k + 1)
                    dve.wait_ge(downed, held(n * EF + k + 1 - RING))
                    nc.vector.tensor_tensor(weighted[:, k % RING], acts[:, k % RING], share_ps[:, (k // FT) % 2], ALU.mult).then_inc(shares_on, 1)

                def tail(n, s):
                    dve.wait_ge(y_turned, n + 1)
                    if not isinstance(n, int) or n >= 2:
                        dve.wait_ge(stored[s], held(n // 2 * 16 if isinstance(n, int) else n * 8 - 8 * s))
                    nc.vector.tensor_tensor(x_new[:, s], o_ps[:].rearrange("p (j d) -> p j d", d=P), x_in[:, s], ALU.add).then_inc(added, 1)

                norm_(0, 0)
                gate(0, 0)
                looped(dve, 0, NC // 2, lambda i, _: two_chunks(i, norm=norm_, gate=gate, up=up, tail=tail))


def build(nc, w, out):
    k_stack = nc.dram_tensor("k_stack", (2, B, H, ROWS, S2), BF16).ap()
    v_rows = nc.dram_tensor("v_rows", (2, B, NG, P, KT, 32), F32).ap()
    q_stack = nc.dram_tensor("q_stack", (2, B, H, ROWS, S), BF16).ap()
    x1, x2, x3 = (nc.dram_tensor(n, (NT, P, P), F32).ap() for n in ("x1", "x2", "x3"))
    with ExitStack() as ctx:
        kept = {"semaphores": ctx, "ident": ctx.enter_context(nc.sbuf_tensor("ident", [P, P], F32)),
                "gates": ctx.enter_context(nc.sbuf_tensor("gates", [P, 4], F32)),
                "late_only": ctx.enter_context(nc.sbuf_tensor("late_only", [1, 1], I32))}
        constants(nc, kept, w)
        context_phase(nc, kept, w, k_stack, v_rows)
        queries_phase(nc, kept, w, 0, w["x"], q_stack)
        attention_phase(nc, kept, w, 0, k_stack, v_rows, q_stack, w["x"], x1)
        experts_phase(nc, kept, w, 0, x1, x2)
        queries_phase(nc, kept, w, 1, x2, q_stack)
        attention_phase(nc, kept, w, 1, k_stack, v_rows, q_stack, x2, x3, first=LATE, late=1)
        attention_phase(nc, kept, w, 1, k_stack, v_rows, q_stack, x2, x3, late=0)
        experts_phase(nc, kept, w, 1, x3, out)


def kernel(**inputs):
    import concourse.bacc as bacc
    from concourse.bass_utils import run_bass_kernel_spmd

    a = {n: np.asarray(v) for n, v in inputs.items()}
    side, mask0 = a["fside_BxSxS2_0"], a["mask_BxSxS2_ik1"]
    laid = {
        "x": a["x"].reshape(NT, P, D),
        "ctx_t": a["ctx_1024"].transpose(0, 2, 1),
        "side": side, "side_t": side[:, :, 8 * P:].transpose(0, 2, 1), "mask0": mask0,
        "mask1": a["mask_1x1xSxS2_ik0"].reshape(S, S2),
        "g_xattn": a["g_xattn"], "g_ffn": a["g_ffn"],
        "wq0": a["L0_xattn_wq_k"], "wk0": a["L0_xattn_wk_k"], "wv0": a["L0_xattn_wv_k"], "wo0": a["L0_xattn_wo_k"],
        "bq0": a["L0_xattn_wq_b"][:, None], "bk0": a["L0_xattn_wk_b"][:, None], "bv0": a["L0_xattn_wv_b"], "bo0": a["L0_xattn_wo_b"],
        "wq1": a["L1_xattn_wq"].T, "wk1": a["L1_xattn_wk"].T, "wv1": a["L1_xattn_wv"].T, "wo1": a["L1_xattn_wo"].T,
        "bq1": a["L1_xattn_bq"][:, None], "bk1": a["L1_xattn_bk"][:, None], "bv1": a["L1_xattn_bv"], "bo1": a["L1_xattn_bo"],
        "w1_0": a["L0_ffn_W1"], "w2_0": a["L0_ffn_W2"], "b2_0": a["L0_ffn_b2"], "wg0": a["L0_ffn_Wg"], "bg0": a["L0_ffn_bg"],
        "b1_0": a["L0_ffn_b1"].reshape(E, FT, P).transpose(2, 0, 1), "b1_1": a["L1_ffn_b1"].reshape(E, FT, P).transpose(2, 0, 1),
        "w1_1": a["L1_ffn_w1"], "w2_1": a["L1_ffn_w2"], "b2_1": a["L1_ffn_b2"], "wg1": a["L1_ffn_wg"], "w_red": a["L1_ffn_w_red"],
    }
    nc = bacc.Bacc("TRN2", target_bir_lowering=False, num_devices=1)
    arrays, w = {}, {}
    for name, v in laid.items():
        v = np.ascontiguousarray(v)
        arrays[f"in_{name}"] = v
        w[name] = nc.dram_tensor(f"in_{name}", v.shape, mybir.dt.from_np(v.dtype), kind="ExternalInput").ap()
    out = nc.dram_tensor("out_x", (NT, P, D), F32, kind="ExternalOutput").ap()
    build(nc, w, out)
    r = run_bass_kernel_spmd(nc, [arrays], core_ids=[0])
    return r.results[0]["out_x"].reshape(B, S, D)
```

```python
from contextlib import ExitStack, nullcontext

import numpy as np

import concourse.bass as bass
from concourse import mybir

F32 = mybir.dt.float32
BF16 = mybir.dt.bfloat16
I32 = mybir.dt.int32
U32 = mybir.dt.uint32
ALU = mybir.AluOpType
ACT = mybir.ActivationFunctionType
AX = mybir.AxisListType

P = 128
B, S, D = 16, 256, 128
S2 = 1601
H, DH = 16, 8
T = B * S
NT = T // P
E, F = 8, 512
FT = F // P
KT = -(-S2 // P)
TAIL = S2 - (KT - 1) * P
HG = 4
NG = H // HG
QT = S // P
STEPS = QT * NG
UNITS = STEPS * HG
TERMS = ((0, 0), (1, 0), (2, 0), (0, 1), (1, 1), (0, 2))
NTERM = len(TERMS)
ROWS = NTERM * DH
SCALE = float(DH) ** -0.5
EPS = 1e-5
BANK = 512
KCUTS = [(n, min(n + BANK, S2)) for n in range(0, S2, BANK)]
CH = 512
NC = T // CH
TPC = CH // P
LATE = 9


def width(kt):
    return P if kt < KT - 1 else TAIL


def held(count):
    return max(count, 0) if isinstance(count, int) else count


def looped(engine, first, last, body):
    body(first, first == last - 1)
    if last - first > 2:
        with engine.Fori(first + 1, last - 1) as i:
            body(i, False)
    if last - first > 1:
        body(last - 1, True)


def on_path(engine, kept, late):
    if late is None:
        return nullcontext()
    return engine.If(engine.value_load(kept["late_only"][0:1, 0:1], min_val=0, max_val=1) == late)


class Chip:

    def __init__(self, nc, ctx, phase):
        self.nc, self.ctx, self.phase, self.semaphores = nc, ctx, phase, []
        ctx.callback(self.clear)

    def clear(self):
        with self.nc.Block() as block:
            @block.sync
            def _(sp):
                for s in self.semaphores:
                    sp.sem_clear(s)

        for s in self.semaphores:
            self.nc.release_semaphore(s)

    def sb(self, name, shape, dt=F32):
        return self.ctx.enter_context(self.nc.sbuf_tensor(f"{self.phase}_{name}", shape, dt))

    def ps(self, name, shape, dt=F32):
        return self.ctx.enter_context(self.nc.psum_tensor(f"{self.phase}_{name}", shape, dt))

    def sem(self, name):
        s = self.nc.alloc_semaphore(name=f"{self.phase}_{name}")
        self.semaphores.append(s)
        return s


def constants(nc, kept, w):
    ident, gates, late_only = kept["ident"], kept["gates"], kept["late_only"]
    with ExitStack() as ctx:
        c = Chip(nc, ctx, "const")
        loaded, cleared, made, done = c.sem("loaded"), c.sem("cleared"), c.sem("made"), c.sem("done")
        mask_in, hidden_made, none_made, path_made, summed = (
            c.sem(n) for n in ("mask_in", "hidden_made", "none_made", "path_made", "summed"))
        raw = c.sb("raw_gates", [P, 4])
        mask, hidden = c.sb("mask", [P, QT, S2], I32), c.sb("hidden", [P, QT, S2])
        none_early, none_late, fits = c.sb("none_early", [P, QT]), c.sb("none_late", [P, QT]), c.sb("fits", [P, QT])
        ones, sum_ps = c.sb("ones", [P, 1]), c.ps("sum_ps", [P, BANK])
        with nc.Block() as block:
            @block.sync
            def _(sp):
                for n, g in enumerate((w["g_xattn"], w["g_ffn"])):
                    sp.dma_start(raw[:, 2 * n:2 * n + 2], g.partition_broadcast(P)).then_inc(loaded, 16)
                sp.dma_start(mask[:], w["mask1"].rearrange("(t p) k -> p t k", p=P)).then_inc(mask_in, 16)

            @block.gpsimd
            def _(pool):
                nc.gpsimd.memset(ones[:], 1.0).then_inc(cleared, 1)
                nc.gpsimd.memset(ident[:], 0.0).then_inc(cleared, 1)
                pool.wait_ge(cleared, 2)
                nc.gpsimd.affine_select(out=ident[:], in_=ident[:], compare_op=ALU.not_equal, fill=1.0,
                                        base=0, pattern=[[-1, P]], channel_multiplier=1).then_inc(made, 1)
                pool.wait_ge(made, 1)

            @block.scalar
            def _(act):
                act.wait_ge(loaded, 32)
                nc.scalar.activation(gates[:], raw[:], ACT.Tanh).then_inc(done, 1)
                act.wait_ge(done, 1)

            @block.vector
            def _(dve):
                dve.wait_ge(mask_in, 16)
                nc.vector.tensor_scalar(hidden[:], mask[:], 0.0, 1.0, ALU.is_equal, ALU.mult).then_inc(hidden_made, 1)
                dve.wait_ge(hidden_made, 1)
                nc.vector.tensor_reduce(none_early[:], hidden[:, :, 0:LATE * P], AX.X, ALU.min)
                nc.vector.tensor_reduce(none_late[:], hidden[:, :, LATE * P:], AX.X, ALU.min).then_inc(none_made, 1)
                dve.wait_ge(none_made, 1)
                nc.vector.tensor_tensor(fits[:], none_early[:], none_late[:], ALU.subtract).then_inc(path_made, 1)
                dve.wait_ge(summed, 1)
                nc.vector.tensor_scalar(late_only[:], sum_ps[0:1, 0:1], float(S), None, ALU.is_equal).then_inc(path_made, 1)
                dve.wait_ge(path_made, 2)

            @block.tensor
            def _(pe):
                pe.wait_ge(cleared, 2)
                pe.wait_ge(path_made, 1)
                for qt in range(QT):
                    last = nc.tensor.matmul(sum_ps[0:1, 0:1], ones[:], fits[:, qt:qt + 1], start=(qt == 0), stop=(qt == QT - 1))
                last.then_inc(summed, 1)


def context_phase(nc, kept, w, k_stack, v_rows):
    with ExitStack() as ctx:
        c = Chip(nc, ctx, "context")
        wk, wv = c.sb("wk", [P, 2, P]), c.sb("wv", [P, 2 * P])
        bk, bv = c.sb("bk", [P, 2]), c.sb("bv", [P, 2 * P])
        ctx_t = c.sb("ctx_t", [P, 2, S2])
        part = [[[c.sb(f"part{s}{l}{n}", [P, S2], BF16) for n in range(3)] for l in range(2)] for s in range(2)]
        rest = [c.sb(f"rest{l}", [P, S2]) for l in range(2)]
        v_stage = c.sb("v_stage", [P, 2, 2, NG, KT, 32])
        k_ps = c.ps("k_ps", [P, 4, BANK])
        v_ps = c.ps("v_ps", [P, 2, 4, 2 * P])
        weights_in, zeroed = c.sem("weights_in"), c.sem("zeroed")
        ctx_in = [c.sem(f"ctx_in{s}") for s in range(2)]
        k_made, v_made = c.sem("k_made"), c.sem("v_made")
        high_made, rest_made, mid_made, low_made = (c.sem(n) for n in ("high_made", "rest_made", "mid_made", "low_made"))
        v_out = c.sem("v_out")
        k_stored = [c.sem(f"k_stored{s}") for s in range(2)]
        v_stored = [c.sem(f"v_stored{s}") for s in range(2)]
        VC = -(-KT // 4)
        kview = k_ps[:].rearrange("p a b -> p (a b)")[:, 0:S2]

        with nc.Block() as block:
            @block.sync
            def _(sp):
                for l in range(2):
                    sp.dma_start(wk[:, l, :], w[f"wk{l}"]).then_inc(weights_in, 16)
                    sp.dma_start(wv[:, l * P:(l + 1) * P], w[f"wv{l}"]).then_inc(weights_in, 16)
                    sp.dma_start(bk[:, l:l + 1], w[f"bk{l}"]).then_inc(weights_in, 16)
                    sp.dma_start(bv[:, l * P:(l + 1) * P], w[f"bv{l}"].partition_broadcast(P)).then_inc(weights_in, 16)
                for s in range(2):
                    sp.dma_start(ctx_t[:, s, :], w["ctx_t"][s]).then_inc(ctx_in[s], 16)

                def store_keys(b, s, l, first):
                    for t, (_, kp) in enumerate(TERMS):
                        sp.dma_start(k_stack[l, b, :, t * DH:(t + 1) * DH, first * P:],
                                     part[s][l][kp][:, first * P:]).then_inc(k_stored[s], 16)

                def store_values(b, s, l, first):
                    sp.dma_start(v_rows[l, b, :, :, first:].rearrange("g p k c -> p g k c"),
                                 v_stage[:, s, l, :, first:]).then_inc(v_stored[s], 16)

                late_only = sp.value_load(kept["late_only"][0:1, 0:1], min_val=0, max_val=1)

                def two_batches(i, _):
                    for s in range(2):
                        b = i * 2 + s
                        sp.wait_ge(low_made, b * 2 + 1)
                        store_keys(b, s, 0, 0)
                        sp.wait_ge(low_made, b * 2 + 2)
                        sp.wait_ge(v_out, b * VC + VC)
                        store_values(b, s, 0, 0)
                        with sp.If(late_only == 1):
                            store_keys(b, s, 1, LATE)
                            store_values(b, s, 1, LATE)
                        with sp.Else():
                            store_keys(b, s, 1, 0)
                            store_values(b, s, 1, 0)

                looped(sp, 0, B // 2, two_batches)
                for s in range(2):
                    sp.wait_ge(k_stored[s], B // 2 * 2 * NTERM * 16)
                    sp.wait_ge(v_stored[s], B // 2 * 2 * 16)

            @block.gpsimd
            def _(pool):
                nc.gpsimd.memset(v_stage[:], 0.0).then_inc(zeroed, 1)

                def two_batches(i, _):
                    for s in range(2):
                        b = i * 2 + s
                        for l in range(2):
                            pool.wait_ge(mid_made, b * 2 + l + 1)
                            nc.gpsimd.tensor_tensor(part[s][l][2][:], rest[l][:], part[s][l][1][:],
                                                    ALU.subtract).then_inc(low_made, 1)

                looped(pool, 0, B // 2, two_batches)

            @block.tensor
            def _(pe):
                pe.wait_ge(weights_in, 8 * 16)

                def two_batches(i, _):
                    for s in range(2):
                        b = i * 2 + s
                        pe.wait_ge(ctx_in[s], i * 16 + 16)
                        for l in range(2):
                            pe.wait_ge(rest_made, b * 2 + l)
                            for n0, n1 in KCUTS:
                                last = nc.tensor.matmul(kview[:, n0:n1], wk[:, l, :], ctx_t[:, s, n0:n1], start=True, stop=True)
                            last.then_inc(k_made, 1)
                            for v in range(2 * l, 2 * l + 2):
                                pe.wait_ge(v_out, held(b * VC + v - 1))
                                for kt in range(4 * v, min(4 * v + 4, KT)):
                                    last = nc.tensor.matmul(v_ps[0:width(kt), v % 2, kt % 4, :],
                                                            ctx_t[:, s, kt * P:kt * P + width(kt)], wv[:], start=True, stop=True)
                                last.then_inc(v_made, 1)

                looped(pe, 0, B // 2, two_batches)

            @block.scalar
            def _(act):
                act.wait_ge(weights_in, 8 * 16)

                def two_batches(i, ends):
                    for s in range(2):
                        b = i * 2 + s
                        for l in range(2):
                            act.wait_ge(k_made, b * 2 + l + 1)
                            if l == 0:
                                act.wait_ge(k_stored[s], i * (2 * NTERM * 16))
                            nc.scalar.activation(part[s][l][0][:], kview, ACT.Identity, bias=bk[:, l:l + 1]).then_inc(high_made, 1)
                            act.wait_ge(rest_made, b * 2 + l + 1)
                            nc.scalar.copy(part[s][l][1][:], rest[l][:]).then_inc(mid_made, 1)
                        if not ends:
                            act.wait_ge(v_made, b * VC + VC)
                            act.dma_start(ctx_t[:, s, :], w["ctx_t"][b + 2]).then_inc(ctx_in[s], 16)

                looped(act, 0, B // 2, two_batches)

            @block.vector
            def _(dve):
                dve.wait_ge(weights_in, 8 * 16)
                dve.wait_ge(zeroed, 1)

                def two_batches(i, _):
                    for s in range(2):
                        b = i * 2 + s
                        for l in range(2):
                            dve.wait_ge(high_made, b * 2 + l + 1)
                            dve.wait_ge(low_made, held(b * 2 + l - 1))
                            nc.vector.scalar_tensor_tensor(out=rest[l][:], in0=kview, scalar=bk[:, l:l + 1],
                                                           in1=part[s][l][0][:], op0=ALU.add, op1=ALU.subtract).then_inc(rest_made, 1)
                            for v in range(2 * l, 2 * l + 2):
                                dve.wait_ge(v_made, b * VC + v + 1)
                                if v == 0:
                                    dve.wait_ge(v_stored[s], i * 32)
                                n = min(4, KT - 4 * v)
                                m = width(4 * v)
                                for k in range(2):
                                    last = nc.vector.tensor_tensor(
                                        v_stage[0:m, s, k, :, 4 * v:4 * v + n, :].rearrange("p g k c -> p k g c"),
                                        v_ps[0:m, v % 2, 0:n, k * P:(k + 1) * P].rearrange("p k (g c) -> p k g c", g=NG),
                                        bv[0:m, None, k * P:(k + 1) * P].rearrange("p k (g c) -> p k g c", g=NG).broadcast_to([m, n, NG, 32]),
                                        ALU.add)
                                last.then_inc(v_out, 1)

                looped(dve, 0, B // 2, two_batches)


def queries_phase(nc, kept, w, layer, x_rows, q_stack):
    ident = kept["ident"]
    with ExitStack() as ctx:
        c = Chip(nc, ctx, f"queries{layer}")
        wq, bq = c.sb("wq", [P, P]), c.sb("bq", [P, 1])
        x_in = c.sb("x_in", [P, 2, TPC, P])
        stats, moments = c.sb("stats", [P, TPC, 6]), c.sb("moments", [P, TPC, 2])
        deviation, inverse = c.sb("deviation", [P, TPC]), c.sb("inverse", [P, TPC])
        normed = c.sb("normed", [P, 2, TPC, P])
        x_t = c.sb("x_t", [P, 2, CH])
        scaled, rest = c.sb("scaled", [P, CH]), c.sb("rest", [P, CH])
        part = [[c.sb(f"part{s}{n}", [P, CH], BF16) for n in range(3)] for s in range(2)]
        t_ps, q_ps = c.ps("t_ps", [P, 2, BANK]), c.ps("q_ps", [P, 2, BANK])
        weights_in = c.sem("weights_in")
        x_loaded = [c.sem(f"x_loaded{s}") for s in range(2)]
        stats_made, moments_made, var_made, root_made, inverse_made, normed_made = (
            c.sem(n) for n in ("stats_made", "moments_made", "var_made", "root_made", "inverse_made", "normed_made"))
        turned, x_t_made, q_made, scaled_made, high_made, rest_made, mid_made, low_made = (
            c.sem(n) for n in ("turned", "x_t_made", "q_made", "scaled_made", "high_made", "rest_made", "mid_made", "low_made"))
        stored = [c.sem(f"stored{s}") for s in range(2)]
        per = CH // S

        with nc.Block() as block:
            @block.sync
            def _(sp):
                sp.dma_start(wq[:], w[f"wq{layer}"]).then_inc(weights_in, 16)
                sp.dma_start(bq[:], w[f"bq{layer}"]).then_inc(weights_in, 16)
                for s in range(2):
                    sp.dma_start(x_in[:, s], x_rows[s * TPC:(s + 1) * TPC].rearrange("j p d -> p j d")).then_inc(x_loaded[s], 16)

                def two_chunks(i, ends):
                    for s in range(2):
                        n = i * 2 + s
                        if not ends:
                            sp.wait_ge(normed_made, n + 1)
                            sp.dma_start(x_in[:, s], x_rows[bass.ds((n + 2) * TPC, TPC)].rearrange("j p d -> p j d")).then_inc(x_loaded[s], 16)
                        sp.wait_ge(low_made, n + 1)
                        for t, (qp, _) in enumerate(TERMS):
                            for k in range(per):
                                sp.dma_start(q_stack[layer, n * per + k, :, t * DH:(t + 1) * DH, :],
                                             part[s][qp][:, k * S:(k + 1) * S]).then_inc(stored[s], 16)

                looped(sp, 0, NC // 2, two_chunks)
                for s in range(2):
                    sp.wait_ge(stored[s], NC // 2 * NTERM * per * 16)

            @block.vector
            def _(dve):
                dve.wait_ge(weights_in, 32)

                def two_chunks(i, _):
                    for s in range(2):
                        n = i * 2 + s
                        dve.wait_ge(x_loaded[s], i * 16 + 16)
                        for j in range(TPC):
                            last = nc.vector.bn_stats(stats[:, j], x_in[:, s, j])
                        last.then_inc(stats_made, 1)
                        dve.wait_ge(stats_made, n + 1)
                        dve.nop(nofuse=True)
                        for j in range(TPC):
                            last = nc.vector.bn_aggr(moments[:, j], stats[:, j])
                        last.then_inc(moments_made, 1)
                        dve.wait_ge(moments_made, n + 1)
                        nc.vector.tensor_scalar(deviation[:], moments[:, :, 1], EPS, None, ALU.add).then_inc(var_made, 1)
                        dve.wait_ge(root_made, n + 1)
                        nc.vector.reciprocal(inverse[:], deviation[:]).then_inc(inverse_made, 1)
                        dve.wait_ge(inverse_made, n + 1)
                        dve.wait_ge(turned, n)
                        for j in range(TPC):
                            last = nc.vector.tensor_scalar(normed[:, s, j], x_in[:, s, j], moments[:, j, 0:1], inverse[:, j:j + 1],
                                                           ALU.subtract, ALU.mult)
                        last.then_inc(normed_made, 1)
                        dve.wait_ge(q_made, n + 1)
                        nc.vector.tensor_scalar(scaled[:], q_ps[:, s], bq[:], -SCALE, ALU.add, ALU.mult).then_inc(scaled_made, 1)
                        dve.wait_ge(high_made, n + 1)
                        nc.vector.tensor_tensor(rest[:], scaled[:], part[s][0][:], ALU.subtract).then_inc(rest_made, 1)
                        dve.wait_ge(mid_made, n + 1)
                        nc.vector.tensor_tensor(part[s][2][:], rest[:], part[s][1][:], ALU.subtract).then_inc(low_made, 1)

                looped(dve, 0, NC // 2, two_chunks)

            @block.scalar
            def _(act):

                def two_chunks(i, _):
                    for s in range(2):
                        n = i * 2 + s
                        act.wait_ge(var_made, n + 1)
                        nc.scalar.activation(deviation[:], deviation[:], ACT.Sqrt).then_inc(root_made, 1)
                        act.wait_ge(turned, n + 1)
                        nc.scalar.copy(x_t[:, s], t_ps[:, s]).then_inc(x_t_made, 1)
                        act.wait_ge(scaled_made, n + 1)
                        act.wait_ge(stored[s], i * (NTERM * per * 16))
                        nc.scalar.copy(part[s][0][:], scaled[:]).then_inc(high_made, 1)
                        act.wait_ge(rest_made, n + 1)
                        nc.scalar.copy(part[s][1][:], rest[:]).then_inc(mid_made, 1)

                looped(act, 0, NC // 2, two_chunks)

            @block.tensor
            def _(pe):
                pe.wait_ge(weights_in, 32)

                def two_chunks(i, _):
                    for s in range(2):
                        n = i * 2 + s
                        pe.wait_ge(normed_made, n + 1)
                        pe.wait_ge(x_t_made, n)
                        for j in range(TPC):
                            last = nc.tensor.transpose(t_ps[:, s, j * P:(j + 1) * P], normed[:, s, j], ident[:])
                        last.then_inc(turned, 1)
                        pe.wait_ge(x_t_made, n + 1)
                        pe.wait_ge(scaled_made, n)
                        nc.tensor.matmul(q_ps[:, s], wq[:], x_t[:, s], start=True, stop=True).then_inc(q_made, 1)

                looped(pe, 0, NC // 2, two_chunks)


def attention_phase(nc, kept, w, layer, k_stack, v_rows, q_stack, x_rows, x_new_rows,
                    first=0, late=None):
    weigh = layer == 0
    KEY0, KEYS, KT = first * P, S2 - first * P, -(-S2 // P) - first
    key_cuts = [(n, min(n + BANK, KEYS)) for n in range(0, KEYS, BANK)]
    GT = 8 if weigh else 0
    by_act = {0, 2} if first else set(range(8))
    by_dve = [k for k in range(KT) if k not in by_act]
    QUARTER = [0, 1, 2, 3, 4] if first else [0, 3, 6, 9, KT]
    order = [0, 1, 2, 3] if first else [0, 1, 8, 2, 3, 9, 4, 5, 10, 6, 7, 11, 12]
    NA, NV = len(by_act), len(by_dve)
    rank = {k: sum((m in by_act) == (k in by_act) for m in order[:n]) for n, k in enumerate(order)}
    CHUNKS = STEPS * KT
    NPT = 4
    LAG = 2
    END = min(LAG + 3, KT - 1)
    NSCORE = 4 // len(key_cuts)
    AHEAD = 6
    NSLOT = 16
    ident, gates = kept["ident"], kept["gates"]

    with ExitStack() as ctx:
        c = Chip(nc, ctx, f"attention{layer}{'late' if first else ''}")
        keys, queries = c.sb("keys", [P, NG, 2, KEYS], BF16), c.sb("queries", [P, QT, NG, 2, P], BF16)
        values = c.sb("values", [P, NG, KT, 32])
        mask, away = c.sb("mask", [P, QT, KEYS], I32), c.sb("away", [P, QT, KEYS])
        if weigh:
            side = c.sb("side", [P, QT, GT * P])
            side_t = c.sb("side_t", [P, QT, KT - GT, P])
        prob = c.sb("prob", [P, NSLOT, KEYS])
        lowest, total, inverse = c.sb("lowest", [P, UNITS]), c.sb("total", [P, UNITS]), c.sb("inverse", [P, UNITS])
        turned_sb = c.sb("turned_sb", [P, NPT, BANK])
        o_sb, o_rows, o_t = c.sb("o_sb", [P, P]), c.sb("o_rows", [P, P]), c.sb("o_t", [P, P])
        wo, bo = c.sb("wo", [P, P]), c.sb("bo", [P, P])
        x_old, x_new = c.sb("x_old", [P, QT, P]), c.sb("x_new", [P, QT, P])
        s_ps, t_ps = c.ps("s_ps", [P, 4, BANK]), c.ps("t_ps", [P, 2, BANK])
        o_ps = c.ps("o_ps", [P, 2, 4, P])

        def scores(u):
            at = u % NSCORE * len(key_cuts) * BANK
            return s_ps[:].rearrange("p a b -> p (a b)")[:, at:at + KEYS]

        def key_width(kt):
            return P if kt < KT - 1 else TAIL

        weights_in, bias_made, o_cleared = c.sem("weights_in"), c.sem("bias_made"), c.sem("o_cleared")
        keys_in = [c.sem(f"keys_in{g}") for g in range(NG)]
        values_in = [c.sem(f"values_in{g}") for g in range(NG)]
        queries_in, mask_in, side_in, side_t_in, x_in, x_stored = (
            [c.sem(f"{n}{q}") for q in range(QT)] for n in ("queries_in", "mask_in", "side_in", "side_t_in", "x_in", "x_stored"))
        away_made, x_ready = c.sem("away_made"), c.sem("x_ready")
        scored, masked, exped, weighted = (c.sem(n) for n in ("scored", "masked", "exped", "weighted"))
        turned, out_by_act, out_by_dve, valued = (c.sem(n) for n in ("turned", "out_by_act", "out_by_dve", "valued"))
        o_out, o_turned, inverse_made, o_normed = (c.sem(n) for n in ("o_out", "o_turned", "inverse_made", "o_normed"))
        rows_turned, rows_out, projected, finished = (c.sem(n) for n in ("rows_turned", "rows_out", "projected", "finished"))

        def walk(b, last, unit=None, turn=None, value=None, fetch=None, step_end=None, unit_late=False):
            ahead = AHEAD - 1 if unit_late else AHEAD
            for s in range(STEPS):
                for j in range(HG):
                    if unit and not unit_late:
                        one_unit(b, last, s * HG + j + ahead, unit)
                    for pos in range(QUARTER[j], QUARTER[j + 1]):
                        if turn:
                            turn(b, s, pos)
                        at = s * KT + pos - LAG
                        if value and at >= 0:
                            value(b, at // KT, at % KT)
                        if s and pos == LAG and fetch:
                            fetch(b, s - 1)
                        if s and pos == END and step_end:
                            step_end(b, s - 1)
                    if unit and unit_late:
                        one_unit(b, last, s * HG + j + ahead, unit)
            for at in range(CHUNKS - LAG, CHUNKS):
                if value:
                    value(b, at // KT, at % KT)
            if fetch:
                fetch(b, STEPS - 1)
            if step_end:
                step_end(b, STEPS - 1)

        def one_unit(b, last, u, unit):
            if u < UNITS:
                unit(b, u // HG, u % HG)
            elif not last:
                unit(b + 1, (u - UNITS) // HG, u % HG)

        with nc.Block() as block:
            @block.sync
            def _(sp):
                with on_path(sp, kept, late):
                    sp.dma_start(wo[:], w[f"wo{layer}"]).then_inc(weights_in, 16)
                    sp.dma_start(bo[:], w[f"bo{layer}"].partition_broadcast(P)).then_inc(weights_in, 16)

                    def load_queries(b, qt):
                        for par in range(2):
                            for k in range(2):
                                sp.dma_start(queries[par * 64:par * 64 + ROWS, qt, :, k, :],
                                             q_stack[layer, b, 2 * par + k:H:HG, :, qt * P:(qt + 1) * P].rearrange("g r q -> r g q")
                                             ).then_inc(queries_in[qt], 16)

                    def load_rows(b, qt):
                        rows = slice(qt * P, (qt + 1) * P)
                        if weigh:
                            sp.dma_start(mask[:, qt], w["mask0"][b, rows, KEY0:]).then_inc(mask_in[qt], 16)
                            sp.dma_start(side[:, qt], w["side"][b, rows, 0:GT * P]).then_inc(side_in[qt], 16)
                            sp.dma_start(side_t[:, qt, 0:KT - GT - 1],
                                         w["side_t"][b, 0:(KT - GT - 1) * P, rows].rearrange("(k p) q -> p k q", p=P)).then_inc(side_t_in[qt], 16)
                            sp.dma_start(side_t[0:TAIL, qt, KT - GT - 1],
                                         w["side_t"][b, (KT - GT - 1) * P:, rows]).then_inc(side_t_in[qt], 16)
                        sp.dma_start(x_old[:, qt], x_rows[b * QT + qt]).then_inc(x_in[qt], 16)

                    def load_keys(b, g):
                        for par in range(2):
                            h = g * HG + 2 * par
                            sp.dma_start(keys[par * 64:par * 64 + ROWS, g], k_stack[layer, b, h:h + 2, :, KEY0:].rearrange("h r s -> r h s")
                                         ).then_inc(keys_in[g], 16)

                    def load_values(b, g):
                        sp.dma_start(values[:, g], v_rows[layer, b, g, :, first:]).then_inc(values_in[g], 16)

                    def store(b, qt):
                        sp.wait_ge(finished, b * QT + qt + 1)
                        sp.dma_start(x_new_rows[b * QT + qt], x_new[:, qt]).then_inc(x_stored[qt], 16)

                    load_queries(0, 0)
                    load_keys(0, 0)
                    if not weigh:
                        for qt in range(QT):
                            sp.dma_start(mask[:, qt], w["mask1"][qt * P:(qt + 1) * P, KEY0:]).then_inc(mask_in[qt], 16)
                    load_rows(0, 0)
                    load_values(0, 0)
                    for g in range(1, NG):
                        load_keys(0, g)
                        load_values(0, g)
                    load_queries(0, 1)
                    load_rows(0, 1)

                    def free_rows(b, qt):
                        sp.wait_ge(masked, b * UNITS + (qt + 1) * NG * HG)
                        if weigh:
                            sp.wait_ge(weighted, b * UNITS + (qt + 1) * NG * HG)
                            sp.wait_ge(out_by_dve, (b * STEPS + (qt + 1) * NG) * NV)

                    def fetch_next(b, ends):
                        if ends:
                            store(b, 0)
                            store(b, 1)
                            return
                        sp.wait_ge(scored, b * UNITS + NG * HG)
                        load_queries(b + 1, 0)
                        for g in range(NG):
                            sp.wait_ge(scored, b * UNITS + (NG + g + 1) * HG)
                            load_keys(b + 1, g)
                            if g:
                                sp.wait_ge(valued, (b * STEPS + NG + g) * KT)
                                load_values(b + 1, g - 1)
                            if g == 1:
                                store(b, 0)
                                free_rows(b, 0)
                                load_rows(b + 1, 0)
                        load_queries(b + 1, 1)
                        sp.wait_ge(valued, (b + 1) * CHUNKS)
                        load_values(b + 1, NG - 1)
                        store(b, 1)
                        free_rows(b, 1)
                        load_rows(b + 1, 1)

                    looped(sp, 0, B, fetch_next)
                    for qt in range(QT):
                        sp.wait_ge(x_stored[qt], B * 16)

            @block.gpsimd
            def _(pool):
                with on_path(pool, kept, late):
                    def unit(b, s, j):
                        qt, g = s // NG, s % NG
                        if g == 0 and j == 0:
                            pool.wait_ge(bias_made, 1)
                            pool.wait_ge(x_in[qt], b * 16 + 16)
                            nc.gpsimd.tensor_tensor(x_old[:, qt], x_old[:, qt], bo[:], ALU.add).then_inc(x_ready, 1)
                            if weigh:
                                pool.wait_ge(side_in[qt], b * 16 + 16)
                        if weigh:
                            slot = (s * HG + j) % NSLOT
                            pool.wait_ge(exped, (b * STEPS + s) * HG + j + 1)
                            nc.gpsimd.tensor_tensor(prob[:, slot, 0:GT * P], prob[:, slot, 0:GT * P], side[:, qt], ALU.mult).then_inc(weighted, 1)

                    for u in range(AHEAD):
                        unit(0, u // HG, u % HG)
                    looped(pool, 0, B, lambda b, last: walk(b, last, unit))

            @block.tensor
            def _(pe):
                with on_path(pe, kept, late):
                    pe.wait_ge(weights_in, 32)
                    pe.wait_ge(o_cleared, 1)

                    def unit(b, s, j):
                        qt, g, par, k = s // NG, s % NG, j // 2, j % 2
                        if j == 0 and g == 0:
                            pe.wait_ge(queries_in[qt], b * 64 + 64)
                        if j == 0 and qt == 0:
                            pe.wait_ge(keys_in[g], b * 32 + 32)
                        pe.wait_ge(masked, held((b * STEPS + s) * HG + j + 1 - NSCORE))
                        rows = slice(par * 64, par * 64 + ROWS)
                        for n0, n1 in key_cuts:
                            last = nc.tensor.matmul(scores(s * HG + j)[:, n0:n1], queries[rows, qt, g, k, :], keys[rows, g, k, n0:n1], start=True, stop=True)
                        last.then_inc(scored, 1)

                    def turn(b, s, pos):
                        kt, n = order[pos], b * CHUNKS + s * KT + pos
                        if pos == 0:
                            pe.wait_ge(exped, (b * STEPS + s + 1) * HG)
                        if weigh and kt in by_act and rank[kt] == 0:
                            pe.wait_ge(weighted, (b * STEPS + s + 1) * HG)
                        was = order[(pos - 2) % KT]
                        back = s if pos >= 2 else s - 1
                        if was in by_act:
                            pe.wait_ge(out_by_act, held((b * STEPS + back) * NA + rank[was] + 1))
                        else:
                            pe.wait_ge(out_by_dve, held((b * STEPS + back) * NV + rank[was] + 1))
                        m = key_width(kt)
                        for j in range(HG):
                            last = nc.tensor.transpose(t_ps[0:m, (s * KT + pos) % 2, j * P:(j + 1) * P],
                                                       prob[:, (s * HG + j) % NSLOT, kt * P:kt * P + m], ident[:])
                        last.then_inc(turned, 1)

                    def value(b, s, pos):
                        kt, g, m = order[pos], s % NG, key_width(order[pos])
                        if pos == 0:
                            pe.wait_ge(o_normed, held(b * STEPS + s - 1))
                            if (s - 2) % NG == NG - 1:
                                pe.wait_ge(finished, held(b * QT + (s - 2) // NG + 1))
                            if s < NG:
                                pe.wait_ge(values_in[g], b * 16 + 16)
                        if kt in by_act:
                            pe.wait_ge(out_by_act, (b * STEPS + s) * NA + rank[kt] + 1)
                        else:
                            pe.wait_ge(out_by_dve, (b * STEPS + s) * NV + rank[kt] + 1)
                        for j in range(HG):
                            last = nc.tensor.matmul(o_ps[32 * j:32 * j + DH, s % 2, 0], values[0:m, g, kt, j * DH:(j + 1) * DH],
                                                    turned_sb[0:m, (s * KT + pos) % NPT, j * P:(j + 1) * P],
                                                    start=(pos == 0), stop=(pos == KT - 1))
                        last.then_inc(valued, 1)

                    def step_end(b, s):
                        qt, g = s // NG, s % NG
                        pe.wait_ge(o_out, b * STEPS + s + 1)
                        nc.tensor.transpose(o_ps[:, s % 2, 1], o_sb[:], ident[:]).then_inc(o_turned, 1)
                        if g == NG - 1:
                            pe.wait_ge(o_normed, b * STEPS + s + 1)
                            nc.tensor.transpose(o_ps[:, s % 2, 2], o_rows[:], ident[:]).then_inc(rows_turned, 1)
                            pe.wait_ge(rows_out, b * QT + qt + 1)
                            nc.tensor.matmul(o_ps[:, s % 2, 3], o_t[:], wo[:], start=True, stop=True).then_inc(projected, 1)

                    for u in range(AHEAD):
                        unit(0, u // HG, u % HG)
                    looped(pe, 0, B, lambda b, last: walk(b, last, unit, turn, value, None, step_end))

            @block.scalar
            def _(act):
                with on_path(act, kept, late):
                    def unit(b, s, j):
                        u = s * HG + j
                        slot = (s * HG + j) % NSLOT
                        act.wait_ge(masked, b * UNITS + u + 1)
                        nc.scalar.activation(prob[:, slot], prob[:, slot], ACT.Exp, bias=lowest[:, u:u + 1], scale=-1.0,
                                             accum_out=total[:, u:u + 1]).then_inc(exped, 1)

                    def turn(b, s, pos):
                        kt, n = order[pos], b * CHUNKS + s * KT + pos
                        if kt not in by_act:
                            return
                        act.wait_ge(turned, n + 1)
                        act.wait_ge(valued, held(n - NPT + 1))
                        m = key_width(kt)
                        nc.scalar.copy(turned_sb[0:m, (s * KT + pos) % NPT], t_ps[0:m, (s * KT + pos) % 2]).then_inc(out_by_act, 1)

                    def fetch(b, s):
                        act.wait_ge(valued, (b * STEPS + s + 1) * KT)
                        act.wait_ge(o_turned, b * STEPS + s)
                        nc.scalar.copy(o_sb[:], o_ps[:, s % 2, 0]).then_inc(o_out, 1)

                    def step_end(b, s):
                        qt, g = s // NG, s % NG
                        if g == NG - 1:
                            act.wait_ge(rows_turned, b * QT + qt + 1)
                            act.wait_ge(projected, b * QT + qt)
                            nc.scalar.copy(o_t[:], o_ps[:, s % 2, 2]).then_inc(rows_out, 1)

                    for u in range(AHEAD - 1):
                        unit(0, u // HG, u % HG)
                    looped(act, 0, B, lambda b, last: walk(b, last, unit, turn, None, fetch, step_end, unit_late=True))

            @block.vector
            def _(dve):
                with on_path(dve, kept, late):
                    nc.vector.memset(o_ps[:], 0.0).then_inc(o_cleared, 1)
                    dve.wait_ge(weights_in, 32)
                    nc.vector.tensor_scalar(bo[:], bo[:], gates[:, layer:layer + 1], None, ALU.mult).then_inc(bias_made, 1)

                    def push_away(b, qt):
                        if weigh:
                            dve.wait_ge(mask_in[qt], b * 16 + 16)
                            nc.vector.tensor_scalar(away[:, qt], mask[:, qt], -1e9, 1e9, ALU.mult, ALU.add).then_inc(away_made, 1)
                            dve.wait_ge(away_made, b * QT + qt + 1)
                        else:
                            dve.wait_ge(mask_in[qt], 16)
                            nc.vector.tensor_scalar(away[:, qt], mask[:, qt], 0.0, 1e30, ALU.is_equal, ALU.mult).then_inc(away_made, 1)
                            dve.wait_ge(away_made, qt + 1)

                    if not weigh:
                        for qt in range(QT):
                            push_away(0, qt)

                    def unit(b, s, j):
                        qt, g, u = s // NG, s % NG, s * HG + j
                        if weigh and g == 0 and j == 0:
                            push_away(b, qt)
                        dve.wait_ge(turned, held((b * STEPS + s + 1 - NSLOT // HG) * KT))
                        dve.wait_ge(scored, b * UNITS + u + 1)
                        dve.nop(nofuse=True)
                        nc.vector.tensor_tensor_reduce(prob[:, (s * HG + j) % NSLOT], scores(u), away[:, qt], 1.0, 3e38,
                                                       ALU.add, ALU.min, lowest[:, u:u + 1]).then_inc(masked, 1)

                    def turn(b, s, pos):
                        kt, n, qt = order[pos], b * CHUNKS + s * KT + pos, s // NG
                        if kt in by_act:
                            return
                        if weigh and s % NG == 0 and rank[kt] == 0:
                            dve.wait_ge(side_t_in[qt], b * 32 + 32)
                        dve.wait_ge(turned, n + 1)
                        dve.wait_ge(valued, held(n - NPT + 1))
                        m = key_width(kt)
                        out, bank = turned_sb[0:m, (s * KT + pos) % NPT], t_ps[0:m, (s * KT + pos) % 2]
                        if weigh:
                            last = nc.vector.tensor_tensor(out.rearrange("p (j q) -> p j q", j=HG), bank.rearrange("p (j q) -> p j q", j=HG),
                                                           side_t[0:m, qt, None, kt - GT, :].broadcast_to([m, HG, P]), ALU.mult)
                        else:
                            last = nc.vector.tensor_copy(out, bank)
                        last.then_inc(out_by_dve, 1)

                    def step_end(b, s):
                        qt, g, u = s // NG, s % NG, s * HG
                        dve.wait_ge(exped, (b * STEPS + s + 1) * HG)
                        nc.vector.reciprocal(inverse[:, u:u + HG], total[:, u:u + HG]).then_inc(inverse_made, 1)
                        dve.wait_ge(inverse_made, b * STEPS + s + 1)
                        if g == 0:
                            dve.wait_ge(rows_turned, b * QT + qt)
                        dve.wait_ge(o_turned, b * STEPS + s + 1)
                        nc.vector.tensor_tensor(o_rows[:, g * 32:(g + 1) * 32].rearrange("p (j d) -> p j d", d=DH),
                                                o_ps[:, s % 2, 1].rearrange("p (j x) -> p j x", j=HG)[:, :, 0:DH],
                                                inverse[:, u:u + HG, None].broadcast_to([P, HG, DH]), ALU.mult).then_inc(o_normed, 1)
                        if g == NG - 1:
                            dve.wait_ge(projected, b * QT + qt + 1)
                            dve.wait_ge(x_ready, b * QT + qt + 1)
                            dve.wait_ge(x_stored[qt], b * 16)
                            nc.vector.scalar_tensor_tensor(out=x_new[:, qt], in0=o_ps[:, s % 2, 3], scalar=gates[:, layer:layer + 1],
                                                           in1=x_old[:, qt], op0=ALU.mult, op1=ALU.add).then_inc(finished, 1)

                    for u in range(AHEAD):
                        unit(0, u // HG, u % HG)
                    looped(dve, 0, B, lambda b, last: walk(b, last, unit, turn, None, None, step_end))


def slots_of(layer):
    need = (2 if layer == 0 else 1) * T // P + E - 1
    return -(-need // 8) * 8


def one(at):
    return slice(at, at + 1) if isinstance(at, int) else bass.ds(at, 1)


def experts_phase(nc, kept, w, layer, x_rows, x_new_rows, sorted_rows, expert_rows):
    CHOICES = 2 if layer == 0 else 1
    SLOTS = slots_of(layer)
    GS = 4
    GROUPS = SLOTS // GS
    RING = 4
    experts = [e for e in range(E) if e % 2 == 0] + [e for e in range(E) if e % 2] if layer == 0 else list(range(E))
    ident, gates = kept["ident"], kept["gates"]
    RED = 16
    SMALL = 2 + 2 * E
    NX = 4
    TPX = NT // NX

    with ExitStack() as ctx:
        c = Chip(nc, ctx, f"experts{layer}")
        w1, w2 = c.sb("w1", [P, E, F]), c.sb("w2", [P, E, FT, P])
        b1, b2 = c.sb("b1", [P, E, F]), c.sb("b2", [P, E, P])
        x_in, normed = c.sb("x_in", [P, NT, P]), c.sb("normed", [P, NT, P])
        stats, moments = c.sb("stats", [P, NT, 6]), c.sb("moments", [P, NT, 2])
        deviation, inverse = c.sb("deviation", [P, NT]), c.sb("inverse", [P, NT])
        x_t = c.sb("x_t", [P, 2, CH])
        logits, top, index = c.sb("logits", [P, NT, E]), c.sb("top", [P, NT, E]), c.sb("index", [P, NT, E], U32)
        chosen, below, grown = c.sb("chosen", [P, NT, 2]), c.sb("below", [P, NT, E]), c.sb("grown", [P, NT, E])
        bottom, share = c.sb("bottom", [P, NT]), c.sb("share", [P, CHOICES, NT])
        picked = c.sb("picked", [P, CHOICES, NT, E])
        member = c.sb("member", [P, NT, E])
        totals = c.sb("totals", [P, NT, E])
        sums = c.sb("sums", [P, 2, NT, E])
        reaches, slots_used = c.sb("reaches", [P, E, NT]), c.sb("slots_used", [P, E])
        before, first_slot = c.sb("before", [P, E, E]), c.sb("first_slot", [P, E])
        first_row = c.sb("first_row", [P, E])
        place, placed = c.sb("place", [P, NT, E]), c.sb("placed", [P, CHOICES, NT, E])
        place_of, place_index = c.sb("place_of", [P, CHOICES, NT]), c.sb("place_index", [P, CHOICES * NT], U32)
        started, slot_expert, slot_index = c.sb("started", [1, SLOTS, E]), c.sb("slot_expert", [1, SLOTS]), c.sb("slot_index", [1, SLOTS], I32)
        even_slots = c.sb("even_slots", [1, 1], I32)
        count, number, full, earlier = c.sb("count", [P, SLOTS]), c.sb("number", [P, E]), c.sb("full", [P, NT]), c.sb("earlier", [P, P])
        ones, zeros = c.sb("ones", [P, P]), c.sb("zeros", [P, GS * P])
        rows_in, rows_t = c.sb("rows_in", [P, 2, GS, P]), c.sb("rows_t", [P, 2, GS * P])
        acts, acts_t, y_out = c.sb("acts", [P, RING, F]), c.sb("acts_t", [P, RING, F]), c.sb("y_out", [P, 2, GS, P])
        fetched = c.sb("fetched", [P, CHOICES, NT, P])
        x_new = normed
        if layer == 0:
            wg, bg = c.sb("wg", [P, E]), c.sb("bg", [P, E])
        else:
            w_red, wg, wg_t = c.sb("w_red", [P, RED]), c.sb("wg", [E, RED]), c.sb("wg_t", [RED, E])
            squares, norm = c.sb("squares", [E, RED]), c.sb("norm", [E, 4])
            reduced = c.sb("reduced", [RED, CH])
        t_ps, h_ps, y_ps = c.ps("t_ps", [P, 2, BANK]), c.ps("h_ps", [P, 2, BANK]), c.ps("y_ps", [P, 2, BANK])
        acts_ps = c.ps("acts_ps", [P, 2, BANK])
        gate_ps = acts_ps[:, 0, 0:NT * E].rearrange("p (j e) -> p j e", e=E)
        rank_ps = acts_ps[:, 1].rearrange("p (a j e) -> p a j e", a=2, e=E)

        small_in, weights_in, setup, wg_rooted, wg_turned = (c.sem(n) for n in ("small_in", "weights_in", "setup", "wg_rooted", "wg_turned"))
        made_by_pool, ones_made, zeroed, cleared = (c.sem(n) for n in ("made_by_pool", "ones_made", "zeroed", "cleared"))
        x_loaded = [c.sem(f"x_loaded{n}") for n in range(NX)]
        stats_made, moments_made, var_made, root_made, inverse_made, normed_made = (
            c.sem(n) for n in ("stats_made", "moments_made", "var_made", "root_made", "inverse_made", "normed_made"))
        turned, x_t_made, reduced_made, reduced_out, gated, below_made, grown_made = (
            c.sem(n) for n in ("turned", "x_t_made", "reduced_made", "reduced_out", "gated", "below_made", "grown_made"))
        step_made, member_made, ranked, routed = (c.sem(n) for n in ("step_made", "member_made", "ranked", "routed"))
        
        scattered, fetched_in = kept["scattered"], kept["fetched_in"]
        BEFORE = 2 if layer else 0
        rows_turned, rows_t_made, upped, acted, downed, y_made = (
            c.sem(n) for n in ("rows_turned", "rows_t_made", "upped", "acted", "downed", "y_made"))
        biased, acts_turned, acts_t_made = (c.sem(n) for n in ("biased", "acts_turned", "acts_t_made"))
        rows_loaded = [c.sem(f"rows_loaded{s}") for s in range(2)]
        y_stored = [c.sem(f"y_stored{s}") for s in range(2)]
        summed, stored = c.sem("summed"), c.sem("stored")
        half_summed = c.sem("half_summed")

        def all_slots(i):
            return slice(i * GS * P, (i + 1) * GS * P) if isinstance(i, int) else bass.ds(i * (GS * P), GS * P)

        with nc.Block() as block:
            @block.sync
            def _(sp):
                for n in range(NX):
                    sp.dma_start(x_in[:, n * TPX:(n + 1) * TPX], x_rows[n * TPX:(n + 1) * TPX].rearrange("j p d -> p j d")).then_inc(x_loaded[n], 16)
                if layer == 0:
                    sp.wait_ge(zeroed, 1)
                    for i in range(GROUPS):
                        sp.dma_start(sorted_rows[all_slots(i)].rearrange("(k p) d -> p k d", p=P),
                                     zeros[:].rearrange("p (k d) -> p k d", d=P)).then_inc(cleared, 16)
                for k, e in enumerate(experts):
                    sp.dma_start(w1[:, k], w[f"w1_{layer}"][e]).then_inc(weights_in, 16)
                    sp.dma_start(w2[:, k], w[f"w2_{layer}"][e].rearrange("(f p) d -> p f d", p=P)).then_inc(weights_in, 16)

                sp.wait_ge(scattered, (BEFORE + CHOICES) * NT * 16)

                def load(i, s):
                    sp.dma_start(rows_in[:, s], sorted_rows[all_slots(i)].rearrange("(k p) d -> p k d", p=P)).then_inc(rows_loaded[s], 16)

                def two_groups(i, ends):
                    for s in range(2):
                        g = i * 2 + s
                        sp.wait_ge(y_made, (g + 1) * GS)
                        sp.dma_start(expert_rows[all_slots(g)].rearrange("(k p) d -> p k d", p=P), y_out[:, s]).then_inc(y_stored[s], 16)
                        if not ends or isinstance(g, int) and g + 2 < GROUPS:
                            sp.wait_ge(rows_turned, g + 1)
                            load(g + 2, s)

                for s in range(2):
                    load(s, s)
                looped(sp, 0, GROUPS // 2, two_groups)
                for n in range(NC):
                    sp.wait_ge(summed, (n + 1) * TPC)
                    sp.dma_start(x_new_rows[n * TPC:(n + 1) * TPC].rearrange("j p d -> p j d"), x_new[:, n * TPC:(n + 1) * TPC]).then_inc(stored, 16)
                sp.wait_ge(stored, NC * 16)

            @block.gpsimd
            def _(pool):
                if layer == 0:
                    nc.gpsimd.memset(zeros[:], 0.0).then_inc(zeroed, 1)
                nc.gpsimd.memset(ones[:], 1.0).then_inc(ones_made, 1)
                pool.wait_ge(ones_made, 1)
                nc.gpsimd.affine_select(out=earlier[:], in_=ones[:], compare_op=ALU.is_ge, fill=0.0,
                                        base=-1, pattern=[[1, P]], channel_multiplier=-1).then_inc(made_by_pool, 1)
                nc.gpsimd.iota(count[:], pattern=[[1, SLOTS]], base=0, channel_multiplier=0, allow_small_or_imprecise_dtypes=True).then_inc(made_by_pool, 1)
                nc.gpsimd.iota(full[:], pattern=[[P, NT]], base=0, channel_multiplier=0, allow_small_or_imprecise_dtypes=True).then_inc(made_by_pool, 1)
                pool.wait_ge(routed, 1)
                if layer == 0:
                    pool.wait_ge(cleared, GROUPS * 16)
                for j in range(NT):
                    for k in range(CHOICES):
                        at = k * NT + j
                        nc.gpsimd.indirect_dma_start(sorted_rows, bass.IndirectOffsetOnAxis(place_index[:, at:at + 1], 0),
                                                     normed[:, j], None).then_inc(scattered, 16)
                for s in range(2):
                    pool.wait_ge(y_stored[s], GROUPS // 2 * 16)
                for j in range(NT):
                    for k in range(CHOICES):
                        at = k * NT + j
                        nc.gpsimd.indirect_dma_start(fetched[:, k, j], None, expert_rows,
                                                     bass.IndirectOffsetOnAxis(place_index[:, at:at + 1], 0)).then_inc(fetched_in[j // TPC], 16)

            @block.tensor
            def _(pe):
                pe.wait_ge(small_in, SMALL * 16)
                if layer == 1:
                    pe.wait_ge(setup, 5)
                    nc.tensor.transpose(gate_ps[0:RED, 0, 0:E], wg[:], ident[0:E, 0:E]).then_inc(wg_turned, 1)
                    pe.wait_ge(setup, 6)
                for n in range(NC):
                    pe.wait_ge(normed_made, n + 1)
                    for j in range(TPC):
                        last = nc.tensor.transpose(t_ps[:, n % 2, j * P:(j + 1) * P], normed[:, n * TPC + j], ident[:])
                    last.then_inc(turned, 1)
                    pe.wait_ge(x_t_made, n + 1)
                    if layer == 0:
                        for j in range(TPC):
                            last = nc.tensor.matmul(gate_ps[:, n * TPC + j], x_t[:, n % 2, j * P:(j + 1) * P], wg[:], start=True, stop=True)
                    else:
                        nc.tensor.matmul(h_ps[0:RED, 0], w_red[:], x_t[:, n % 2], start=True, stop=True).then_inc(reduced_made, 1)
                        pe.wait_ge(reduced_out, n + 1)
                        for j in range(TPC):
                            last = nc.tensor.matmul(gate_ps[:, n * TPC + j], reduced[:, j * P:(j + 1) * P], wg_t[:], start=True, stop=True)
                    last.then_inc(gated, 1)
                pe.wait_ge(made_by_pool, 1)
                pe.wait_ge(member_made, 1)
                nc.tensor.matmul(rank_ps[:, 0], earlier[:], member[:], start=True, stop=True)
                nc.tensor.matmul(rank_ps[:, 1], ones[:], member[:], start=True, stop=True).then_inc(ranked, 1)

                pe.wait_ge(weights_in, 2 * E * 16)

                def turn(g, s):
                    pe.wait_ge(rows_loaded[s], (g // 2 + 1) * 16 if isinstance(g, int) else g * 8 + (16 if s == 0 else 8))
                    for k in range(GS):
                        last = nc.tensor.transpose(t_ps[:, s, k * P:(k + 1) * P], rows_in[:, s, k], ident[:])
                    last.then_inc(rows_turned, 1)

                def expert_of(n):
                    return bass.ds(pe.value_load(slot_index[0:1, one(n)], min_val=0, max_val=E - 1), 1)

                def up(n, g, s, k):
                    e = expert_of(n)
                    if k == 0:
                        pe.wait_ge(rows_t_made, g + 1)
                    pe.wait_ge(biased, held(n - 1))
                    nc.tensor.matmul(h_ps[:, k % 2], rows_t[:, s, k * P:(k + 1) * P], w1[:, e].rearrange("p a b -> p (a b)"),
                                     start=True, stop=True).then_inc(upped, 1)

                def turn_acts(n, k):
                    pe.wait_ge(acted, n + 1)
                    pe.wait_ge(acts_t_made, held(n - 1))
                    for f in range(FT):
                        last = nc.tensor.transpose(acts_ps[:, k % 2, f * P:(f + 1) * P], acts[:, k % RING, f * P:(f + 1) * P], ident[:])
                    last.then_inc(acts_turned, 1)

                def down(n, g, s, k):
                    e = expert_of(n)
                    pe.wait_ge(y_made, held(n - 1))
                    pe.wait_ge(acts_t_made, n + 1)
                    for f in range(FT):
                        last = nc.tensor.matmul(y_ps[:, k % 2, 0:P], acts_t[:, k % RING, f * P:(f + 1) * P],
                                                w2[:, e, f].rearrange("p a b -> p (a b)"), start=(f == 0), stop=(f == FT - 1))
                    last.then_inc(downed, 1)

                def two_groups(i, ends):
                    for s in range(2):
                        g = i * 2 + s
                        final = ends and isinstance(g, int) and g + 1 == GROUPS
                        for k in range(GS):
                            n = g * GS + k
                            first = isinstance(n, int) and n < 2
                            up(n, g, s, k)
                            if k == 2 and not final:
                                turn(g + 1, 1 - s)
                            if not first or n == 1:
                                turn_acts(n - 1, (k - 1) % GS)
                            if not first:
                                down(n - 2, g if k >= 2 else g - 1, s if k >= 2 else 1 - s, (k - 2) % GS)
                        if final:
                            down(n - 1, g, s, GS - 2)
                            turn_acts(n, GS - 1)
                            down(n, g, s, GS - 1)

                pe.wait_ge(routed, 1)
                turn(0, 0)
                looped(pe, 0, GROUPS // 2, two_groups)

            @block.scalar
            def _(act):
                if layer == 0:
                    act.dma_start(wg[:], w["wg0"]).then_inc(small_in, 16)
                    act.dma_start(bg[:], w["bg0"].partition_broadcast(P)).then_inc(small_in, 16)
                else:
                    act.dma_start(wg[:], w["wg1"]).then_inc(small_in, 16)
                    act.dma_start(w_red[:], w["w_red"]).then_inc(small_in, 16)
                for k, e in enumerate(experts):
                    act.dma_start(b1[:, k], w[f"b1_{layer}"][e].partition_broadcast(P)).then_inc(small_in, 16)
                    act.dma_start(b2[:, k], w[f"b2_{layer}"][e].partition_broadcast(P)).then_inc(small_in, 16)
                act.wait_ge(small_in, SMALL * 16)
                if layer == 1:
                    act.wait_ge(setup, 2)
                    nc.scalar.activation(norm[:, 1:2], norm[:, 0:1], ACT.Sqrt).then_inc(wg_rooted, 1)
                act.wait_ge(var_made, 1)
                nc.scalar.activation(deviation[:], deviation[:], ACT.Sqrt).then_inc(root_made, 1)
                for n in range(NC):
                    act.wait_ge(turned, n + 1)
                    if n >= 2:
                        act.wait_ge(gated, n - 1)
                    nc.scalar.copy(x_t[:, n % 2], t_ps[:, n % 2]).then_inc(x_t_made, 1)
                    if layer == 1:
                        act.wait_ge(reduced_made, n + 1)
                        nc.scalar.copy(reduced[:], h_ps[0:RED, 0]).then_inc(reduced_out, 1)
                act.wait_ge(below_made, 1)
                nc.scalar.activation(grown[:], below[:], ACT.Exp).then_inc(grown_made, 1)
                act.wait_ge(routed, 1)
                even = act.value_load(even_slots[0:1, 0:1], min_val=0, max_val=SLOTS) if layer == 0 else None

                def activate(n, k, func):
                    act.wait_ge(biased, n + 1)
                    nc.scalar.activation(acts[:, k % RING], acts[:, k % RING], func).then_inc(acted, 1)

                def activate_by_kind(n, k):
                    if layer == 1:
                        activate(n, k, ACT.Gelu)
                        return
                    with act.If(even > n):
                        activate(n, k, ACT.Gelu)
                    with act.Else():
                        activate(n, k, ACT.Silu)

                def copy_acts(n, k):
                    act.wait_ge(acts_turned, n + 1)
                    act.wait_ge(downed, held(n + 1 - RING))
                    nc.scalar.copy(acts_t[:, k % RING], acts_ps[:, k % 2]).then_inc(acts_t_made, 1)

                def two_groups(i, ends):
                    for s in range(2):
                        for k in range(GS):
                            n = (i * 2 + s) * GS + k
                            activate_by_kind(n, k)
                            if not isinstance(n, int) or n > 0:
                                copy_acts(n - 1, (k - 1) % GS)
                    if ends and isinstance(n, int) and n == SLOTS - 1:
                        copy_acts(n, GS - 1)

                looped(act, 0, GROUPS // 2, two_groups)

            @block.vector
            def _(dve):
                dve.wait_ge(small_in, SMALL * 16)
                if layer == 1:
                    nc.vector.memset(norm[:], 0.0).then_inc(setup, 1)
                    dve.wait_ge(setup, 1)
                    nc.vector.tensor_tensor_reduce(squares[:], wg[:], wg[:], 1.0, 0.0, ALU.mult, ALU.add, norm[:, 0:1]).then_inc(setup, 1)
                    dve.wait_ge(wg_rooted, 1)
                    nc.vector.tensor_scalar(norm[:, 2:3], norm[:, 1:2], 1e-4, None, ALU.max).then_inc(setup, 1)
                    dve.wait_ge(setup, 3)
                    nc.vector.reciprocal(norm[:, 3:4], norm[:, 2:3]).then_inc(setup, 1)
                    dve.wait_ge(setup, 4)
                    nc.vector.tensor_scalar(wg[:], wg[:], norm[:, 3:4], None, ALU.mult).then_inc(setup, 1)
                    dve.wait_ge(wg_turned, 1)
                    nc.vector.tensor_copy(wg_t[:], gate_ps[0:RED, 0, 0:E]).then_inc(setup, 1)
                for n in range(NX):
                    dve.wait_ge(x_loaded[n], 16)
                    for j in range(n * TPX, (n + 1) * TPX):
                        last = nc.vector.bn_stats(stats[:, j], x_in[:, j])
                last.then_inc(stats_made, 1)
                dve.wait_ge(stats_made, 1)
                for j in range(NT):
                    last = nc.vector.bn_aggr(moments[:, j], stats[:, j])
                last.then_inc(moments_made, 1)
                dve.wait_ge(moments_made, 1)
                nc.vector.tensor_scalar(deviation[:], moments[:, :, 1], EPS, None, ALU.add).then_inc(var_made, 1)
                dve.wait_ge(root_made, 1)
                nc.vector.reciprocal(inverse[:], deviation[:]).then_inc(inverse_made, 1)
                dve.wait_ge(inverse_made, 1)
                for n in range(NC):
                    for j in range(n * TPC, (n + 1) * TPC):
                        last = nc.vector.tensor_scalar(normed[:, j], x_in[:, j], moments[:, j, 0:1], inverse[:, j:j + 1], ALU.subtract, ALU.mult)
                    last.then_inc(normed_made, 1)

                made = 0

                def step(ins):
                    nonlocal made
                    made += 1
                    ins.then_inc(step_made, 1)
                    dve.wait_ge(step_made, made)

                dve.wait_ge(made_by_pool, 3)
                if layer == 0:
                    nc.vector.tensor_scalar(number[:, 0:E // 2], count[:, 0:E // 2], 2.0, None, ALU.mult)
                    nc.vector.tensor_scalar(number[:, E // 2:], count[:, 0:E // 2], 2.0, 1.0, ALU.mult, ALU.add)
                else:
                    nc.vector.tensor_copy(number[:], count[:, 0:E])
                step(nc.vector.tensor_tensor(before[:], count[:, 0:E, None].broadcast_to([P, E, E]),
                                             count[:, None, 0:E].broadcast_to([P, E, E]), ALU.is_gt))

                dve.wait_ge(gated, NC)
                if layer == 0:
                    step(nc.vector.tensor_tensor(logits[:], gate_ps, bg[:, None, :].broadcast_to([P, NT, E]), ALU.add))
                else:
                    step(nc.vector.tensor_copy(logits[:], gate_ps))
                for j in range(NT):
                    last = nc.vector.max(top[:, j], logits[:, j])
                step(last)
                nc.vector.tensor_tensor(below[:], logits[:] if layer else top[:], top[:, :, 0:1].broadcast_to([P, NT, E]),
                                        ALU.subtract).then_inc(below_made, 1)
                for j in range(NT):
                    last = nc.vector.max_index(index[:, j], top[:, j], logits[:, j])
                step(last)
                step(nc.vector.tensor_copy(chosen[:], index[:, :, 0:2]))
                for k in range(CHOICES):
                    last = nc.vector.tensor_tensor(picked[:, k], number[:, None, :].broadcast_to([P, NT, E]),
                                                   chosen[:, :, k:k + 1].broadcast_to([P, NT, E]), ALU.is_equal)
                step(last)
                if layer == 0:
                    nc.vector.tensor_tensor(member[:], picked[:, 0], picked[:, 1], ALU.add).then_inc(member_made, 1)
                else:
                    nc.vector.tensor_copy(member[:], picked[:, 0]).then_inc(member_made, 1)

                dve.wait_ge(grown_made, 1)
                if layer == 0:
                    step(nc.vector.tensor_scalar(bottom[:], grown[:, :, 1], 1.0, None, ALU.add))
                else:
                    step(nc.vector.tensor_reduce(bottom[:], grown[:], AX.X, ALU.add))
                step(nc.vector.reciprocal(bottom[:], bottom[:]))
                step(nc.vector.tensor_scalar(share[:, 0], bottom[:], gates[:, 2 + layer:3 + layer], None, ALU.mult))
                if layer == 0:
                    step(nc.vector.tensor_tensor(share[:, 1], grown[:, :, 1], share[:, 0], ALU.mult))

                dve.wait_ge(ranked, 1)
                nc.vector.tensor_copy(totals[:], rank_ps[:, 1])
                step(nc.vector.tensor_copy(sums[:, 0], rank_ps[:, 1]))
                at, shift = 0, 1
                while shift < NT:
                    nc.vector.tensor_copy(sums[:, 1 - at, 0:shift], sums[:, at, 0:shift])
                    step(nc.vector.tensor_tensor(sums[:, 1 - at, shift:], sums[:, at, shift:], sums[:, at, 0:NT - shift], ALU.add))
                    at, shift = 1 - at, shift * 2
                step(nc.vector.tensor_tensor(reaches[:], sums[:, at, NT - 1, :, None].broadcast_to([P, E, NT]),
                                             full[:, None, :].broadcast_to([P, E, NT]), ALU.is_gt))
                step(nc.vector.tensor_reduce(slots_used[:], reaches[:], AX.X, ALU.add))
                step(nc.vector.tensor_tensor(before[:], before[:], slots_used[:, None, :].broadcast_to([P, E, E]), ALU.mult))
                step(nc.vector.tensor_reduce(first_slot[:], before[:], AX.X, ALU.add))
                step(nc.vector.tensor_tensor(started[:], count[0:1, :, None].broadcast_to([1, SLOTS, E]),
                                             first_slot[0:1, None, :].broadcast_to([1, SLOTS, E]), ALU.is_ge))
                step(nc.vector.tensor_reduce(slot_expert[:], started[:], AX.X, ALU.add))
                nc.vector.tensor_scalar(slot_index[:], slot_expert[:], -1.0, None, ALU.add)
                nc.vector.tensor_copy(even_slots[:], first_slot[0:1, E // 2:E // 2 + 1])
                step(nc.vector.tensor_scalar(first_row[:], first_slot[:], float(P), None, ALU.mult))
                nc.vector.tensor_tensor(place[:], rank_ps[:, 0], first_row[:, None, :].broadcast_to([P, NT, E]), ALU.add)
                step(nc.vector.tensor_tensor(totals[:], sums[:, at], totals[:], ALU.subtract))
                step(nc.vector.tensor_tensor(place[:], place[:], totals[:], ALU.add))
                for k in range(CHOICES):
                    last = nc.vector.tensor_tensor(placed[:, k], picked[:, k], place[:], ALU.mult)
                step(last)
                for k in range(CHOICES):
                    last = nc.vector.tensor_reduce(place_of[:, k], placed[:, k], AX.X, ALU.add)
                step(last)
                nc.vector.tensor_copy(place_index[:], place_of[:].rearrange("p k j -> p (k j)")).then_inc(routed, 1)

                def expert_of(n):
                    return bass.ds(dve.value_load(slot_index[0:1, one(n)], min_val=0, max_val=E - 1), 1)

                def bias_up(n, k):
                    e = expert_of(n)
                    dve.wait_ge(acts_turned, held(n + 1 - RING))
                    dve.wait_ge(upped, n + 1)
                    nc.vector.tensor_tensor(acts[:, k % RING], h_ps[:, k % 2], b1[:, e].rearrange("p a b -> p (a b)"), ALU.add).then_inc(biased, 1)

                def bias_down(n, g, s, k):
                    e = expert_of(n)
                    if k == 0:
                        dve.wait_ge(y_stored[s], g // 2 * 16 if isinstance(g, int) else g * 8 - 8 * s)
                    dve.wait_ge(downed, n + 1)
                    nc.vector.tensor_tensor(y_out[:, s, k], y_ps[:, k % 2, 0:P],
                                            b2[:, e].rearrange("p a b -> p (a b)"), ALU.add).then_inc(y_made, 1)

                def copy_rows(g, s):
                    dve.wait_ge(rows_turned, g + 1)
                    dve.wait_ge(upped, held((g - 1) * GS))
                    nc.vector.tensor_copy(rows_t[:, s], t_ps[:, s]).then_inc(rows_t_made, 1)

                def two_groups(i, ends):
                    for s in range(2):
                        g = i * 2 + s
                        final = ends and isinstance(g, int) and g + 1 == GROUPS
                        for k in range(GS):
                            n = g * GS + k
                            bias_up(n, k)
                            if k == 2 and not final:
                                copy_rows(g + 1, 1 - s)
                            if not isinstance(n, int) or n >= 2:
                                bias_down(n - 2, g if k >= 2 else g - 1, s if k >= 2 else 1 - s, (k - 2) % GS)
                        if final:
                            bias_down(n - 1, g, s, GS - 2)
                            bias_down(n, g, s, GS - 1)

                dve.wait_ge(routed, 1)
                copy_rows(0, 0)
                looped(dve, 0, GROUPS // 2, two_groups)
                for n in range(NC):
                    dve.wait_ge(fetched_in[n], (BEFORE + CHOICES) * TPC * 16)
                    for j in range(n * TPC, (n + 1) * TPC):
                        last = nc.vector.scalar_tensor_tensor(out=x_new[:, j], in0=fetched[:, 0, j], scalar=share[:, 0, j:j + 1],
                                                              in1=x_in[:, j], op0=ALU.mult, op1=ALU.add)
                        if CHOICES == 1:
                            last.then_inc(summed, 1)
                    if CHOICES == 2:
                        last.then_inc(half_summed, 1)
                        dve.wait_ge(half_summed, n + 1)
                        for j in range(n * TPC, (n + 1) * TPC):
                            nc.vector.scalar_tensor_tensor(out=x_new[:, j], in0=fetched[:, 1, j], scalar=share[:, 1, j:j + 1],
                                                           in1=x_new[:, j], op0=ALU.mult, op1=ALU.add).then_inc(summed, 1)


def build(nc, w, out):
    k_stack = nc.dram_tensor("k_stack", (2, B, H, ROWS, S2), BF16).ap()
    v_rows = nc.dram_tensor("v_rows", (2, B, NG, P, KT, 32), F32).ap()
    q_stack = nc.dram_tensor("q_stack", (2, B, H, ROWS, S), BF16).ap()
    x1, x2, x3 = (nc.dram_tensor(n, (NT, P, P), F32).ap() for n in ("x1", "x2", "x3"))
    sorted_rows = nc.dram_tensor("sorted_rows", (slots_of(0) * P, P), F32).ap()
    expert_rows = nc.dram_tensor("expert_rows", (slots_of(0) * P, P), F32).ap()
    with ExitStack() as ctx:
        lasting = {"scattered": nc.alloc_semaphore(name="scattered"), "fetched_in": [nc.alloc_semaphore(name=f"fetched_in{n}") for n in range(NC)]}
        kept = {**lasting, "ident": ctx.enter_context(nc.sbuf_tensor("ident", [P, P], F32)),
                "gates": ctx.enter_context(nc.sbuf_tensor("gates", [P, 4], F32)),
                "late_only": ctx.enter_context(nc.sbuf_tensor("late_only", [1, 1], I32))}
        constants(nc, kept, w)
        context_phase(nc, kept, w, k_stack, v_rows)
        queries_phase(nc, kept, w, 0, w["x"], q_stack)
        attention_phase(nc, kept, w, 0, k_stack, v_rows, q_stack, w["x"], x1)
        experts_phase(nc, kept, w, 0, x1, x2, sorted_rows, expert_rows)
        queries_phase(nc, kept, w, 1, x2, q_stack)
        attention_phase(nc, kept, w, 1, k_stack, v_rows, q_stack, x2, x3, first=LATE, late=1)
        attention_phase(nc, kept, w, 1, k_stack, v_rows, q_stack, x2, x3, late=0)
        experts_phase(nc, kept, w, 1, x3, out, sorted_rows, expert_rows)


def kernel(**inputs):
    import concourse.bacc as bacc
    from concourse.bass_utils import run_bass_kernel_spmd

    a = {n: np.asarray(v) for n, v in inputs.items()}
    side, mask0 = a["fside_BxSxS2_0"], a["mask_BxSxS2_ik1"]
    laid = {
        "x": a["x"].reshape(NT, P, D),
        "ctx_t": a["ctx_1024"].transpose(0, 2, 1),
        "side": side, "side_t": side[:, :, 8 * P:].transpose(0, 2, 1), "mask0": mask0,
        "mask1": a["mask_1x1xSxS2_ik0"].reshape(S, S2),
        "g_xattn": a["g_xattn"], "g_ffn": a["g_ffn"],
        "wq0": a["L0_xattn_wq_k"], "wk0": a["L0_xattn_wk_k"], "wv0": a["L0_xattn_wv_k"], "wo0": a["L0_xattn_wo_k"],
        "bq0": a["L0_xattn_wq_b"][:, None], "bk0": a["L0_xattn_wk_b"][:, None], "bv0": a["L0_xattn_wv_b"], "bo0": a["L0_xattn_wo_b"],
        "wq1": a["L1_xattn_wq"].T, "wk1": a["L1_xattn_wk"].T, "wv1": a["L1_xattn_wv"].T, "wo1": a["L1_xattn_wo"].T,
        "bq1": a["L1_xattn_bq"][:, None], "bk1": a["L1_xattn_bk"][:, None], "bv1": a["L1_xattn_bv"], "bo1": a["L1_xattn_bo"],
        "w1_0": a["L0_ffn_W1"], "w2_0": a["L0_ffn_W2"], "b2_0": a["L0_ffn_b2"], "wg0": a["L0_ffn_Wg"], "bg0": a["L0_ffn_bg"],
        "b1_0": a["L0_ffn_b1"], "b1_1": a["L1_ffn_b1"],
        "w1_1": a["L1_ffn_w1"], "w2_1": a["L1_ffn_w2"], "b2_1": a["L1_ffn_b2"], "wg1": a["L1_ffn_wg"], "w_red": a["L1_ffn_w_red"],
    }
    nc = bacc.Bacc("TRN2", target_bir_lowering=False, num_devices=1)
    arrays, w = {}, {}
    for name, v in laid.items():
        v = np.ascontiguousarray(v)
        arrays[f"in_{name}"] = v
        w[name] = nc.dram_tensor(f"in_{name}", v.shape, mybir.dt.from_np(v.dtype), kind="ExternalInput").ap()
    out = nc.dram_tensor("out_x", (NT, P, D), F32, kind="ExternalOutput").ap()
    build(nc, w, out)
    r = run_bass_kernel_spmd(nc, [arrays], core_ids=[0])
    return r.results[0]["out_x"].reshape(B, S, D)
```

```python
from contextlib import ExitStack, nullcontext

import numpy as np

import concourse.bass as bass
from concourse import mybir

F32 = mybir.dt.float32
BF16 = mybir.dt.bfloat16
I32 = mybir.dt.int32
U32 = mybir.dt.uint32
ALU = mybir.AluOpType
ACT = mybir.ActivationFunctionType
AX = mybir.AxisListType

P = 128
B, S, D = 16, 256, 128
S2 = 1601
H, DH = 16, 8
T = B * S
NT = T // P
E, F = 8, 512
FT = F // P
KT = -(-S2 // P)
TAIL = S2 - (KT - 1) * P
HG = 4
NG = H // HG
QT = S // P
STEPS = QT * NG
UNITS = STEPS * HG
TERMS = ((0, 0), (0, 1), (0, 2), (1, 0), (1, 1), (2, 0))
KRUNS = ((0, 3), (3, 2), (5, 1))
NTERM = len(TERMS)
ROWS = NTERM * DH
SCALE = float(DH) ** -0.5
EPS = 1e-5
BANK = 512
KCUTS = [(n, min(n + BANK, S2)) for n in range(0, S2, BANK)]
CH = 512
NC = T // CH
TPC = CH // P
LATE = 9


def width(kt):
    return P if kt < KT - 1 else TAIL


def held(count):
    return max(count, 0) if isinstance(count, int) else count


def looped(engine, first, last, body):
    body(first, first == last - 1)
    if last - first > 2:
        with engine.Fori(first + 1, last - 1) as i:
            body(i, False)
    if last - first > 1:
        body(last - 1, True)


def on_path(engine, kept, late):
    if late is None:
        return nullcontext()
    return engine.If(engine.value_load(kept["late_only"][0:1, 0:1], min_val=0, max_val=1) == late)


class Chip:

    def __init__(self, nc, ctx, phase):
        self.nc, self.ctx, self.phase, self.semaphores = nc, ctx, phase, []
        ctx.callback(self.clear)

    def clear(self):
        with self.nc.Block() as block:
            @block.sync
            def _(sp):
                for s in self.semaphores:
                    sp.sem_clear(s)

        for s in self.semaphores:
            self.nc.release_semaphore(s)

    def sb(self, name, shape, dt=F32):
        return self.ctx.enter_context(self.nc.sbuf_tensor(f"{self.phase}_{name}", shape, dt))

    def ps(self, name, shape, dt=F32):
        return self.ctx.enter_context(self.nc.psum_tensor(f"{self.phase}_{name}", shape, dt))

    def sem(self, name):
        s = self.nc.alloc_semaphore(name=f"{self.phase}_{name}")
        self.semaphores.append(s)
        return s


def constants(nc, kept, w):
    ident, gates, late_only = kept["ident"], kept["gates"], kept["late_only"]
    with ExitStack() as ctx:
        c = Chip(nc, ctx, "const")
        loaded, cleared, made, done = c.sem("loaded"), c.sem("cleared"), c.sem("made"), c.sem("done")
        mask_in, hidden_made, none_made, path_made, summed = (
            c.sem(n) for n in ("mask_in", "hidden_made", "none_made", "path_made", "summed"))
        raw = c.sb("raw_gates", [P, 4])
        mask, hidden = c.sb("mask", [P, QT, S2], I32), c.sb("hidden", [P, QT, S2])
        none_early, none_late, fits = c.sb("none_early", [P, QT]), c.sb("none_late", [P, QT]), c.sb("fits", [P, QT])
        ones, sum_ps = c.sb("ones", [P, 1]), c.ps("sum_ps", [P, BANK])
        with nc.Block() as block:
            @block.sync
            def _(sp):
                for n, g in enumerate((w["g_xattn"], w["g_ffn"])):
                    sp.dma_start(raw[:, 2 * n:2 * n + 2], g.partition_broadcast(P)).then_inc(loaded, 16)
                sp.dma_start(mask[:], w["mask1"].rearrange("(t p) k -> p t k", p=P)).then_inc(mask_in, 16)

            @block.gpsimd
            def _(pool):
                nc.gpsimd.memset(ones[:], 1.0).then_inc(cleared, 1)
                nc.gpsimd.memset(ident[:], 0.0).then_inc(cleared, 1)
                pool.wait_ge(cleared, 2)
                nc.gpsimd.affine_select(out=ident[:], in_=ident[:], compare_op=ALU.not_equal, fill=1.0,
                                        base=0, pattern=[[-1, P]], channel_multiplier=1).then_inc(made, 1)
                pool.wait_ge(made, 1)

            @block.scalar
            def _(act):
                act.wait_ge(loaded, 32)
                nc.scalar.activation(gates[:], raw[:], ACT.Tanh).then_inc(done, 1)
                act.wait_ge(done, 1)

            @block.vector
            def _(dve):
                dve.wait_ge(mask_in, 16)
                nc.vector.tensor_scalar(hidden[:], mask[:], 0.0, 1.0, ALU.is_equal, ALU.mult).then_inc(hidden_made, 1)
                dve.wait_ge(hidden_made, 1)
                nc.vector.tensor_reduce(none_early[:], hidden[:, :, 0:LATE * P], AX.X, ALU.min)
                nc.vector.tensor_reduce(none_late[:], hidden[:, :, LATE * P:], AX.X, ALU.min).then_inc(none_made, 1)
                dve.wait_ge(none_made, 1)
                nc.vector.tensor_tensor(fits[:], none_early[:], none_late[:], ALU.subtract).then_inc(path_made, 1)
                dve.wait_ge(summed, 1)
                nc.vector.tensor_scalar(late_only[:], sum_ps[0:1, 0:1], float(S), None, ALU.is_equal).then_inc(path_made, 1)
                dve.wait_ge(path_made, 2)

            @block.tensor
            def _(pe):
                pe.wait_ge(cleared, 2)
                pe.wait_ge(path_made, 1)
                for qt in range(QT):
                    last = nc.tensor.matmul(sum_ps[0:1, 0:1], ones[:], fits[:, qt:qt + 1], start=(qt == 0), stop=(qt == QT - 1))
                last.then_inc(summed, 1)


def context_phase(nc, kept, w, k_stack, v_rows):
    with ExitStack() as ctx:
        c = Chip(nc, ctx, "context")
        wk, wv = c.sb("wk", [P, 2, P]), c.sb("wv", [P, 2 * P])
        bk, bv = c.sb("bk", [P, 2]), c.sb("bv", [P, 2 * P])
        ctx_t = c.sb("ctx_t", [P, 2, S2])
        part = [[[c.sb(f"part{s}{l}{n}", [P, S2], BF16) for n in range(3)] for l in range(2)] for s in range(2)]
        rest = [c.sb(f"rest{l}", [P, S2]) for l in range(2)]
        v_stage = c.sb("v_stage", [P, 2, 2, NG, KT, 32])
        k_ps = c.ps("k_ps", [P, 4, BANK])
        v_ps = c.ps("v_ps", [P, 2, 4, 2 * P])
        weights_in, zeroed = c.sem("weights_in"), c.sem("zeroed")
        ctx_in = [c.sem(f"ctx_in{s}") for s in range(2)]
        k_made, v_made = c.sem("k_made"), c.sem("v_made")
        high_made, rest_made, mid_made, low_made = (c.sem(n) for n in ("high_made", "rest_made", "mid_made", "low_made"))
        v_out = c.sem("v_out")
        k_stored = [c.sem(f"k_stored{s}") for s in range(2)]
        v_stored = [c.sem(f"v_stored{s}") for s in range(2)]
        VC = -(-KT // 4)
        kview = k_ps[:].rearrange("p a b -> p (a b)")[:, 0:S2]
        HALVES = ((0, 2 * BANK), (2 * BANK, S2))

        with nc.Block() as block:
            @block.sync
            def _(sp):
                for l in range(2):
                    sp.dma_start(wk[:, l, :], w[f"wk{l}"]).then_inc(weights_in, 16)
                    sp.dma_start(wv[:, l * P:(l + 1) * P], w[f"wv{l}"]).then_inc(weights_in, 16)
                    sp.dma_start(bk[:, l:l + 1], w[f"bk{l}"]).then_inc(weights_in, 16)
                    sp.dma_start(bv[:, l * P:(l + 1) * P], w[f"bv{l}"].partition_broadcast(P)).then_inc(weights_in, 16)
                for s in range(2):
                    sp.dma_start(ctx_t[:, s, :], w["ctx_t"][s]).then_inc(ctx_in[s], 16)

                def store_keys(b, s, l, first):
                    for n in range(3):
                        sp.dma_start(k_stack[l, b, :, n * DH:(n + 1) * DH, first * P:],
                                     part[s][l][n][:, first * P:]).then_inc(k_stored[s], 16)

                def store_values(b, s, l, first):
                    sp.dma_start(v_rows[l, b, :, :, first:].rearrange("g p k c -> p g k c"),
                                 v_stage[:, s, l, :, first:]).then_inc(v_stored[s], 16)

                late_only = sp.value_load(kept["late_only"][0:1, 0:1], min_val=0, max_val=1)

                def two_batches(i, _):
                    for s in range(2):
                        b = i * 2 + s
                        sp.wait_ge(low_made, b * 2 + 1)
                        store_keys(b, s, 0, 0)
                        sp.wait_ge(low_made, b * 2 + 2)
                        sp.wait_ge(v_out, b * VC + VC)
                        store_values(b, s, 0, 0)
                        with sp.If(late_only == 1):
                            store_keys(b, s, 1, LATE)
                            store_values(b, s, 1, LATE)
                        with sp.Else():
                            store_keys(b, s, 1, 0)
                            store_values(b, s, 1, 0)

                looped(sp, 0, B // 2, two_batches)
                for s in range(2):
                    sp.wait_ge(k_stored[s], B // 2 * 2 * 3 * 16)
                    sp.wait_ge(v_stored[s], B // 2 * 2 * 16)

            @block.gpsimd
            def _(pool):
                nc.gpsimd.memset(v_stage[:], 0.0).then_inc(zeroed, 1)

                def two_batches(i, _):
                    for s in range(2):
                        b = i * 2 + s
                        for l in range(2):
                            pool.wait_ge(mid_made, b * 2 + l + 1)
                            nc.gpsimd.tensor_tensor(part[s][l][2][:], rest[l][:], part[s][l][1][:],
                                                    ALU.subtract).then_inc(low_made, 1)

                looped(pool, 0, B // 2, two_batches)

            @block.tensor
            def _(pe):
                pe.wait_ge(weights_in, 8 * 16)

                def two_batches(i, _):
                    for s in range(2):
                        b = i * 2 + s
                        pe.wait_ge(ctx_in[s], i * 16 + 16)
                        for l in range(2):
                            for h in range(2):
                                pe.wait_ge(rest_made, held((b * 2 + l) * 2 - 1 + h))
                                for n0, n1 in KCUTS[2 * h:2 * h + 2]:
                                    last = nc.tensor.matmul(kview[:, n0:n1], wk[:, l, :], ctx_t[:, s, n0:n1], start=True, stop=True)
                                last.then_inc(k_made, 1)
                            for v in range(2 * l, 2 * l + 2):
                                pe.wait_ge(v_out, held(b * VC + v - 1))
                                for kt in range(4 * v, min(4 * v + 4, KT)):
                                    last = nc.tensor.matmul(v_ps[0:width(kt), v % 2, kt % 4, :],
                                                            ctx_t[:, s, kt * P:kt * P + width(kt)], wv[:], start=True, stop=True)
                                last.then_inc(v_made, 1)

                looped(pe, 0, B // 2, two_batches)

            @block.scalar
            def _(act):
                act.wait_ge(weights_in, 8 * 16)

                def two_batches(i, ends):
                    for s in range(2):
                        b = i * 2 + s
                        for l in range(2):
                            if l == 0:
                                act.wait_ge(k_stored[s], i * (2 * 3 * 16))
                            for h, (n0, n1) in enumerate(HALVES):
                                act.wait_ge(k_made, (b * 2 + l) * 2 + h + 1)
                                nc.scalar.activation(part[s][l][0][:, n0:n1], kview[:, n0:n1], ACT.Identity, bias=bk[:, l:l + 1]).then_inc(high_made, 1)
                            act.wait_ge(rest_made, (b * 2 + l) * 2 + 2)
                            nc.scalar.copy(part[s][l][1][:], rest[l][:]).then_inc(mid_made, 1)
                        if not ends:
                            act.wait_ge(v_made, b * VC + VC)
                            act.dma_start(ctx_t[:, s, :], w["ctx_t"][b + 2]).then_inc(ctx_in[s], 16)

                looped(act, 0, B // 2, two_batches)

            @block.vector
            def _(dve):
                dve.wait_ge(weights_in, 8 * 16)
                dve.wait_ge(zeroed, 1)

                def two_batches(i, _):
                    for s in range(2):
                        b = i * 2 + s
                        for l in range(2):
                            dve.wait_ge(low_made, held(b * 2 + l - 1))
                            for h, (n0, n1) in enumerate(HALVES):
                                dve.wait_ge(high_made, (b * 2 + l) * 2 + h + 1)
                                nc.vector.scalar_tensor_tensor(out=rest[l][:, n0:n1], in0=kview[:, n0:n1], scalar=bk[:, l:l + 1],
                                                               in1=part[s][l][0][:, n0:n1], op0=ALU.add, op1=ALU.subtract).then_inc(rest_made, 1)
                            for v in range(2 * l, 2 * l + 2):
                                dve.wait_ge(v_made, b * VC + v + 1)
                                if v == 0:
                                    dve.wait_ge(v_stored[s], i * 32)
                                n = min(4, KT - 4 * v)
                                m = width(4 * v)
                                for k in range(2):
                                    last = nc.vector.tensor_tensor(
                                        v_stage[0:m, s, k, :, 4 * v:4 * v + n, :].rearrange("p g k c -> p k g c"),
                                        v_ps[0:m, v % 2, 0:n, k * P:(k + 1) * P].rearrange("p k (g c) -> p k g c", g=NG),
                                        bv[0:m, None, k * P:(k + 1) * P].rearrange("p k (g c) -> p k g c", g=NG).broadcast_to([m, n, NG, 32]),
                                        ALU.add)
                                last.then_inc(v_out, 1)

                looped(dve, 0, B // 2, two_batches)


def queries_phase(nc, kept, w, layer, x_rows, q_stack):
    ident = kept["ident"]
    NX = 4
    TPX = NT // NX
    with ExitStack() as ctx:
        c = Chip(nc, ctx, f"queries{layer}")
        wq, bq = c.sb("wq", [P, P]), c.sb("bq", [P, 1])
        x_in, normed = c.sb("x_in", [P, NT, P]), c.sb("normed", [P, NT, P])
        stats, moments = c.sb("stats", [P, NT, 6]), c.sb("moments", [P, NT, 2])
        deviation, inverse = c.sb("deviation", [P, NT]), c.sb("inverse", [P, NT])
        x_t = c.sb("x_t", [P, 2, CH])
        scaled, rest = c.sb("scaled", [P, 2, CH]), c.sb("rest", [P, 2, CH])
        part = c.sb("part", [P, 2, 3, CH], BF16)
        t_ps, q_ps = c.ps("t_ps", [P, 2, BANK]), c.ps("q_ps", [P, 2, BANK])
        weights_in = c.sem("weights_in")
        x_loaded = [c.sem(f"x_loaded{n}") for n in range(NX)]
        stats_made, moments_made, var_made, root_made, inverse_made, normed_made = (
            c.sem(n) for n in ("stats_made", "moments_made", "var_made", "root_made", "inverse_made", "normed_made"))
        turned, x_t_made, q_made, scaled_made, high_made, rest_made, mid_made, low_made = (
            c.sem(n) for n in ("turned", "x_t_made", "q_made", "scaled_made", "high_made", "rest_made", "mid_made", "low_made"))
        stored = [c.sem(f"stored{s}") for s in range(2)]

        with nc.Block() as block:
            @block.sync
            def _(sp):
                for n in range(NX):
                    sp.dma_start(x_in[:, n * TPX:(n + 1) * TPX], x_rows[n * TPX:(n + 1) * TPX].rearrange("j p d -> p j d")).then_inc(x_loaded[n], 16)
                sp.dma_start(wq[:], w[f"wq{layer}"]).then_inc(weights_in, 16)
                sp.dma_start(bq[:], w[f"bq{layer}"]).then_inc(weights_in, 16)
                for n in range(NC):
                    sp.wait_ge(low_made, n + 1)
                    for t, (qp, _) in enumerate(TERMS):
                        sp.dma_start(q_stack[layer, :, t * DH:(t + 1) * DH, n * CH:(n + 1) * CH],
                                     part[:, n % 2, qp]).then_inc(stored[n % 2], 16)
                for s in range(2):
                    sp.wait_ge(stored[s], NC // 2 * NTERM * 16)

            @block.vector
            def _(dve):
                dve.wait_ge(weights_in, 32)
                for n in range(NX):
                    dve.wait_ge(x_loaded[n], 16)
                    for j in range(n * TPX, (n + 1) * TPX):
                        last = nc.vector.bn_stats(stats[:, j], x_in[:, j])
                last.then_inc(stats_made, 1)
                dve.wait_ge(stats_made, 1)
                for j in range(NT):
                    last = nc.vector.bn_aggr(moments[:, j], stats[:, j])
                last.then_inc(moments_made, 1)
                dve.wait_ge(moments_made, 1)
                nc.vector.tensor_scalar(deviation[:], moments[:, :, 1], EPS, None, ALU.add).then_inc(var_made, 1)
                dve.wait_ge(root_made, 1)
                nc.vector.reciprocal(inverse[:], deviation[:]).then_inc(inverse_made, 1)
                dve.wait_ge(inverse_made, 1)

                def normalise(n):
                    for j in range(n * TPC, (n + 1) * TPC):
                        last = nc.vector.tensor_scalar(normed[:, j], x_in[:, j], moments[:, j, 0:1], inverse[:, j:j + 1],
                                                       ALU.subtract, ALU.mult)
                    last.then_inc(normed_made, 1)

                def lowest(n):
                    dve.wait_ge(mid_made, n + 1)
                    nc.vector.tensor_tensor(part[:, n % 2, 2], rest[:, n % 2], part[:, n % 2, 1], ALU.subtract).then_inc(low_made, 1)

                normalise(0)
                normalise(1)
                for n in range(NC):
                    dve.wait_ge(q_made, n + 1)
                    nc.vector.tensor_scalar(scaled[:, n % 2], q_ps[:, n % 2], bq[:], -SCALE, ALU.add, ALU.mult).then_inc(scaled_made, 1)
                    if n:
                        lowest(n - 1)
                    if n + 2 < NC:
                        normalise(n + 2)
                    dve.wait_ge(high_made, n + 1)
                    nc.vector.tensor_tensor(rest[:, n % 2], scaled[:, n % 2], part[:, n % 2, 0], ALU.subtract).then_inc(rest_made, 1)
                lowest(NC - 1)

            @block.scalar
            def _(act):
                def copy_x(n):
                    act.wait_ge(turned, n + 1)
                    if n >= 2:
                        act.wait_ge(q_made, n - 1)
                    nc.scalar.copy(x_t[:, n % 2], t_ps[:, n % 2]).then_inc(x_t_made, 1)

                act.wait_ge(var_made, 1)
                nc.scalar.activation(deviation[:], deviation[:], ACT.Sqrt).then_inc(root_made, 1)
                copy_x(0)
                for n in range(NC):
                    if n + 1 < NC:
                        copy_x(n + 1)
                    act.wait_ge(scaled_made, n + 1)
                    if n >= 2:
                        act.wait_ge(stored[n % 2], n // 2 * NTERM * 16)
                    nc.scalar.copy(part[:, n % 2, 0], scaled[:, n % 2]).then_inc(high_made, 1)
                    act.wait_ge(rest_made, n + 1)
                    nc.scalar.copy(part[:, n % 2, 1], rest[:, n % 2]).then_inc(mid_made, 1)

            @block.tensor
            def _(pe):
                def turn(n):
                    pe.wait_ge(normed_made, n + 1)
                    if n >= 2:
                        pe.wait_ge(x_t_made, n - 1)
                    for j in range(TPC):
                        last = nc.tensor.transpose(t_ps[:, n % 2, j * P:(j + 1) * P], normed[:, n * TPC + j], ident[:])
                    last.then_inc(turned, 1)

                pe.wait_ge(weights_in, 32)
                turn(0)
                for n in range(NC):
                    if n + 1 < NC:
                        turn(n + 1)
                    pe.wait_ge(x_t_made, n + 1)
                    if n >= 2:
                        pe.wait_ge(scaled_made, n - 1)
                    nc.tensor.matmul(q_ps[:, n % 2], wq[:], x_t[:, n % 2], start=True, stop=True).then_inc(q_made, 1)


def attention_phase(nc, kept, w, layer, k_stack, v_rows, q_stack, x_rows, x_new_rows,
                    first=0, late=None):
    weigh = layer == 0
    KEY0, KEYS, KT = first * P, S2 - first * P, -(-S2 // P) - first
    key_cuts = [(n, min(n + BANK, KEYS)) for n in range(0, KEYS, BANK)]
    GT = 8 if weigh else 0
    by_act = {0, 2} if first else set(range(8))
    by_dve = [k for k in range(KT) if k not in by_act]
    QUARTER = [0, 1, 2, 3, 4] if first else [0, 3, 6, 9, KT]
    order = [0, 1, 2, 3] if first else [0, 1, 8, 2, 3, 9, 4, 5, 10, 6, 7, 11, 12]
    NA, NV = len(by_act), len(by_dve)
    rank = {k: sum((m in by_act) == (k in by_act) for m in order[:n]) for n, k in enumerate(order)}
    CHUNKS = STEPS * KT
    NPT = 8 if first else 4
    NBANK = 4 if first else 2
    LAG = 3 if first else 2
    END_STEPS, END = (2, 0) if first else (1, LAG + 5)
    NSCORE = 2 if first else 1
    AHEAD = 8
    NSLOT = 16
    ident, gates = kept["ident"], kept["gates"]

    with ExitStack() as ctx:
        c = Chip(nc, ctx, f"attention{layer}{'late' if first else ''}")
        keys, queries = c.sb("keys", [P, NG, 2, KEYS], BF16), c.sb("queries", [P, QT, NG, 2, P], BF16)
        values = c.sb("values", [P, NG, KT, 32])
        mask, away = c.sb("mask", [P, QT, KEYS], I32), c.sb("away", [P, QT, KEYS])
        if weigh:
            side = c.sb("side", [P, QT, GT * P])
            side_t = c.sb("side_t", [P, QT, KT - GT, P])
        prob = c.sb("prob", [P, NSLOT, KEYS])
        lowest, total, inverse = c.sb("lowest", [P, UNITS]), c.sb("total", [P, UNITS]), c.sb("inverse", [P, UNITS])
        turned_sb = c.sb("turned_sb", [P, NPT, BANK])
        o_sb, o_rows, o_t = c.sb("o_sb", [P, P]), c.sb("o_rows", [P, P]), c.sb("o_t", [P, P])
        wo, bo = c.sb("wo", [P, P]), c.sb("bo", [P, P])
        x_old, x_new = c.sb("x_old", [P, QT, P]), c.sb("x_new", [P, QT, P])
        s_ps, t_ps = c.ps("s_ps", [P, NSCORE * len(key_cuts), BANK]), c.ps("t_ps", [P, NBANK, BANK])
        o_ps = c.ps("o_ps", [P, 2, 4, P])

        def scores(u):
            at = u % NSCORE * len(key_cuts) * BANK
            return s_ps[:].rearrange("p a b -> p (a b)")[:, at:at + KEYS]

        def key_width(kt):
            return P if kt < KT - 1 else TAIL

        weights_in, bias_made, o_cleared = c.sem("weights_in"), c.sem("bias_made"), c.sem("o_cleared")
        keys_in = [c.sem(f"keys_in{g}") for g in range(NG)]
        values_in = [c.sem(f"values_in{g}") for g in range(NG)]
        queries_in, mask_in, side_in, side_t_in, x_in, x_stored = (
            [c.sem(f"{n}{q}") for q in range(QT)] for n in ("queries_in", "mask_in", "side_in", "side_t_in", "x_in", "x_stored"))
        away_made, x_ready = c.sem("away_made"), c.sem("x_ready")
        scored, masked, exped, weighted = (c.sem(n) for n in ("scored", "masked", "exped", "weighted"))
        turned, out_by_act, out_by_dve, valued = (c.sem(n) for n in ("turned", "out_by_act", "out_by_dve", "valued"))
        o_out, o_turned, inverse_made, o_normed = (c.sem(n) for n in ("o_out", "o_turned", "inverse_made", "o_normed"))
        rows_turned, rows_out, projected, finished = (c.sem(n) for n in ("rows_turned", "rows_out", "projected", "finished"))

        def walk(b, last, unit=None, turn=None, value=None, fetch=None, step_end=None, unit_late=False):
            ahead = AHEAD - 1 if unit_late else AHEAD
            for s in range(STEPS):
                for j in range(HG):
                    if unit and not unit_late:
                        one_unit(b, last, s * HG + j + ahead, unit)
                    for pos in range(QUARTER[j], QUARTER[j + 1]):
                        if turn:
                            turn(b, s, pos)
                        at = s * KT + pos - LAG
                        if value and at >= 0:
                            value(b, at // KT, at % KT)
                        if s and pos == LAG and fetch:
                            fetch(b, s - 1)
                        if s >= END_STEPS and pos == END and step_end:
                            step_end(b, s - END_STEPS)
                    if unit and unit_late:
                        one_unit(b, last, s * HG + j + ahead, unit)
            if step_end and END_STEPS == 2:
                step_end(b, STEPS - 2)
            for at in range(CHUNKS - LAG, CHUNKS):
                if value:
                    value(b, at // KT, at % KT)
            if fetch:
                fetch(b, STEPS - 1)
            if step_end:
                step_end(b, STEPS - 1)

        def one_unit(b, last, u, unit):
            if u < UNITS:
                unit(b, u // HG, u % HG)
            elif not last:
                unit(b + 1, (u - UNITS) // HG, u % HG)

        with nc.Block() as block:
            @block.sync
            def _(sp):
                with on_path(sp, kept, late):
                    sp.dma_start(wo[:], w[f"wo{layer}"]).then_inc(weights_in, 16)
                    sp.dma_start(bo[:], w[f"bo{layer}"].partition_broadcast(P)).then_inc(weights_in, 16)

                    def queries_at(b, qt):
                        at = b * S + qt * P
                        return slice(at, at + P) if isinstance(at, int) else bass.ds(at, P)

                    def load_queries(b, qt):
                        for par in range(2):
                            for k in range(2):
                                sp.dma_start(queries[par * 64:par * 64 + ROWS, qt, :, k, :],
                                             q_stack[layer, 2 * par + k:H:HG, :, queries_at(b, qt)].rearrange("g r q -> r g q")
                                             ).then_inc(queries_in[qt], 16)

                    def load_rows(b, qt):
                        rows = slice(qt * P, (qt + 1) * P)
                        if weigh:
                            sp.dma_start(mask[:, qt], w["mask0"][b, rows, KEY0:]).then_inc(mask_in[qt], 16)
                            sp.dma_start(side[:, qt], w["side"][b, rows, 0:GT * P]).then_inc(side_in[qt], 16)
                            sp.dma_start(side_t[:, qt, 0:KT - GT - 1],
                                         w["side_t"][b, 0:(KT - GT - 1) * P, rows].rearrange("(k p) q -> p k q", p=P)).then_inc(side_t_in[qt], 16)
                            sp.dma_start(side_t[0:TAIL, qt, KT - GT - 1],
                                         w["side_t"][b, (KT - GT - 1) * P:, rows]).then_inc(side_t_in[qt], 16)
                        sp.dma_start(x_old[:, qt], x_rows[b * QT + qt]).then_inc(x_in[qt], 16)

                    def load_keys(b, g):
                        for par in range(2):
                            h = g * HG + 2 * par
                            for term, parts in KRUNS:
                                at = par * 64 + term * DH
                                sp.dma_start(keys[at:at + parts * DH, g], k_stack[layer, b, h:h + 2, 0:parts * DH, KEY0:].rearrange("h r s -> r h s")
                                             ).then_inc(keys_in[g], 16)

                    def load_values(b, g):
                        sp.dma_start(values[:, g], v_rows[layer, b, g, :, first:]).then_inc(values_in[g], 16)

                    def store(b, qt):
                        sp.wait_ge(finished, b * QT + qt + 1)
                        sp.dma_start(x_new_rows[b * QT + qt], x_new[:, qt]).then_inc(x_stored[qt], 16)

                    load_queries(0, 0)
                    load_keys(0, 0)
                    if not weigh:
                        for qt in range(QT):
                            sp.dma_start(mask[:, qt], w["mask1"][qt * P:(qt + 1) * P, KEY0:]).then_inc(mask_in[qt], 16)
                    load_rows(0, 0)
                    load_values(0, 0)
                    for g in range(1, NG):
                        load_keys(0, g)
                        load_values(0, g)
                    load_queries(0, 1)
                    load_rows(0, 1)

                    def free_rows(b, qt):
                        sp.wait_ge(masked, b * UNITS + (qt + 1) * NG * HG)
                        if weigh:
                            sp.wait_ge(weighted, b * UNITS + (qt + 1) * NG * HG)
                            sp.wait_ge(out_by_dve, (b * STEPS + (qt + 1) * NG) * NV)

                    def fetch_next(b, ends):
                        if ends:
                            store(b, 0)
                            store(b, 1)
                            return
                        sp.wait_ge(scored, b * UNITS + NG * HG)
                        load_queries(b + 1, 0)
                        for g in range(NG):
                            sp.wait_ge(scored, b * UNITS + (NG + g + 1) * HG)
                            load_keys(b + 1, g)
                            if g:
                                sp.wait_ge(valued, (b * STEPS + NG + g) * KT)
                                load_values(b + 1, g - 1)
                            if g == 1:
                                store(b, 0)
                                free_rows(b, 0)
                                load_rows(b + 1, 0)
                        load_queries(b + 1, 1)
                        sp.wait_ge(valued, (b + 1) * CHUNKS)
                        load_values(b + 1, NG - 1)
                        store(b, 1)
                        free_rows(b, 1)
                        load_rows(b + 1, 1)

                    looped(sp, 0, B, fetch_next)
                    for qt in range(QT):
                        sp.wait_ge(x_stored[qt], B * 16)

            @block.gpsimd
            def _(pool):
                with on_path(pool, kept, late):
                    def unit(b, s, j):
                        qt, g = s // NG, s % NG
                        if g == 0 and j == 0:
                            pool.wait_ge(bias_made, 1)
                            pool.wait_ge(x_in[qt], b * 16 + 16)
                            nc.gpsimd.tensor_tensor(x_old[:, qt], x_old[:, qt], bo[:], ALU.add).then_inc(x_ready, 1)
                            if weigh:
                                pool.wait_ge(side_in[qt], b * 16 + 16)
                        if weigh:
                            slot = (s * HG + j) % NSLOT
                            pool.wait_ge(exped, (b * STEPS + s) * HG + j + 1)
                            nc.gpsimd.tensor_tensor(prob[:, slot, 0:GT * P], prob[:, slot, 0:GT * P], side[:, qt], ALU.mult).then_inc(weighted, 1)

                    for u in range(AHEAD):
                        unit(0, u // HG, u % HG)
                    looped(pool, 0, B, lambda b, last: walk(b, last, unit))

            @block.tensor
            def _(pe):
                with on_path(pe, kept, late):
                    pe.wait_ge(weights_in, 32)
                    pe.wait_ge(o_cleared, 1)

                    def unit(b, s, j):
                        qt, g, par, k = s // NG, s % NG, j // 2, j % 2
                        if j == 0 and g == 0:
                            pe.wait_ge(queries_in[qt], b * 64 + 64)
                        if j == 0 and qt == 0:
                            pe.wait_ge(keys_in[g], b * 96 + 96)
                        pe.wait_ge(masked, held((b * STEPS + s) * HG + j + 1 - NSCORE))
                        rows = slice(par * 64, par * 64 + ROWS)
                        for n0, n1 in key_cuts:
                            last = nc.tensor.matmul(scores(s * HG + j)[:, n0:n1], queries[rows, qt, g, k, :], keys[rows, g, k, n0:n1], start=True, stop=True)
                        last.then_inc(scored, 1)

                    def turn(b, s, pos):
                        kt, n = order[pos], b * CHUNKS + s * KT + pos
                        if pos == 0:
                            pe.wait_ge(exped, (b * STEPS + s + 1) * HG)
                        if weigh and kt in by_act and rank[kt] == 0:
                            pe.wait_ge(weighted, (b * STEPS + s + 1) * HG)
                        was = order[(pos - NBANK) % KT]
                        back = s + (pos - NBANK) // KT
                        if was in by_act:
                            pe.wait_ge(out_by_act, held((b * STEPS + back) * NA + rank[was] + 1))
                        else:
                            pe.wait_ge(out_by_dve, held((b * STEPS + back) * NV + rank[was] + 1))
                        m = key_width(kt)
                        for j in range(HG):
                            last = nc.tensor.transpose(t_ps[0:m, (s * KT + pos) % NBANK, j * P:(j + 1) * P],
                                                       prob[:, (s * HG + j) % NSLOT, kt * P:kt * P + m], ident[:])
                        last.then_inc(turned, 1)

                    def value(b, s, pos):
                        kt, g, m = order[pos], s % NG, key_width(order[pos])
                        if pos == 0:
                            pe.wait_ge(o_normed, held(b * STEPS + s - 1))
                            if (s - 2) % NG == NG - 1:
                                pe.wait_ge(finished, held(b * QT + (s - 2) // NG + 1))
                            if s < NG:
                                pe.wait_ge(values_in[g], b * 16 + 16)
                        if kt in by_act:
                            pe.wait_ge(out_by_act, (b * STEPS + s) * NA + rank[kt] + 1)
                        else:
                            pe.wait_ge(out_by_dve, (b * STEPS + s) * NV + rank[kt] + 1)
                        for j in range(HG):
                            last = nc.tensor.matmul(o_ps[32 * j:32 * j + DH, s % 2, 0], values[0:m, g, kt, j * DH:(j + 1) * DH],
                                                    turned_sb[0:m, (s * KT + pos) % NPT, j * P:(j + 1) * P],
                                                    start=(pos == 0), stop=(pos == KT - 1))
                        last.then_inc(valued, 1)

                    def step_end(b, s):
                        qt, g = s // NG, s % NG
                        pe.wait_ge(o_out, b * STEPS + s + 1)
                        nc.tensor.transpose(o_ps[:, s % 2, 1], o_sb[:], ident[:]).then_inc(o_turned, 1)
                        if g == NG - 1:
                            pe.wait_ge(o_normed, b * STEPS + s + 1)
                            nc.tensor.transpose(o_ps[:, s % 2, 2], o_rows[:], ident[:]).then_inc(rows_turned, 1)
                            pe.wait_ge(rows_out, b * QT + qt + 1)
                            nc.tensor.matmul(o_ps[:, s % 2, 3], o_t[:], wo[:], start=True, stop=True).then_inc(projected, 1)

                    for u in range(AHEAD):
                        unit(0, u // HG, u % HG)
                    looped(pe, 0, B, lambda b, last: walk(b, last, unit, turn, value, None, step_end))

            @block.scalar
            def _(act):
                with on_path(act, kept, late):
                    def unit(b, s, j):
                        u = s * HG + j
                        slot = (s * HG + j) % NSLOT
                        act.wait_ge(masked, b * UNITS + u + 1)
                        nc.scalar.activation(prob[:, slot], prob[:, slot], ACT.Exp, bias=lowest[:, u:u + 1], scale=-1.0,
                                             accum_out=total[:, u:u + 1]).then_inc(exped, 1)

                    def turn(b, s, pos):
                        kt, n = order[pos], b * CHUNKS + s * KT + pos
                        if kt not in by_act:
                            return
                        act.wait_ge(turned, n + 1)
                        act.wait_ge(valued, held(n - NPT + 1))
                        m = key_width(kt)
                        nc.scalar.copy(turned_sb[0:m, (s * KT + pos) % NPT], t_ps[0:m, (s * KT + pos) % NBANK]).then_inc(out_by_act, 1)

                    def fetch(b, s):
                        act.wait_ge(valued, (b * STEPS + s + 1) * KT)
                        act.wait_ge(o_turned, b * STEPS + s)
                        nc.scalar.copy(o_sb[:], o_ps[:, s % 2, 0]).then_inc(o_out, 1)

                    def step_end(b, s):
                        qt, g = s // NG, s % NG
                        if g == NG - 1:
                            act.wait_ge(rows_turned, b * QT + qt + 1)
                            act.wait_ge(projected, b * QT + qt)
                            nc.scalar.copy(o_t[:], o_ps[:, s % 2, 2]).then_inc(rows_out, 1)

                    for u in range(AHEAD - 1):
                        unit(0, u // HG, u % HG)
                    looped(act, 0, B, lambda b, last: walk(b, last, unit, turn, None, fetch, step_end, unit_late=True))

            @block.vector
            def _(dve):
                with on_path(dve, kept, late):
                    nc.vector.memset(o_ps[:], 0.0).then_inc(o_cleared, 1)
                    dve.wait_ge(weights_in, 32)
                    nc.vector.tensor_scalar(bo[:], bo[:], gates[:, layer:layer + 1], None, ALU.mult).then_inc(bias_made, 1)

                    def push_away(b, qt):
                        if weigh:
                            dve.wait_ge(mask_in[qt], b * 16 + 16)
                            nc.vector.tensor_scalar(away[:, qt], mask[:, qt], -1e9, 1e9, ALU.mult, ALU.add).then_inc(away_made, 1)
                            dve.wait_ge(away_made, b * QT + qt + 1)
                        else:
                            dve.wait_ge(mask_in[qt], 16)
                            nc.vector.tensor_scalar(away[:, qt], mask[:, qt], 0.0, 1e30, ALU.is_equal, ALU.mult).then_inc(away_made, 1)
                            dve.wait_ge(away_made, qt + 1)

                    if not weigh:
                        for qt in range(QT):
                            push_away(0, qt)

                    def unit(b, s, j):
                        qt, g, u = s // NG, s % NG, s * HG + j
                        if weigh and g == 0 and j == 0:
                            push_away(b, qt)
                        dve.wait_ge(turned, held((b * STEPS + s + 1 - NSLOT // HG) * KT))
                        dve.wait_ge(scored, b * UNITS + u + 1)
                        dve.nop(nofuse=True)
                        nc.vector.tensor_tensor_reduce(prob[:, (s * HG + j) % NSLOT], scores(u), away[:, qt], 1.0, 3e38,
                                                       ALU.add, ALU.min, lowest[:, u:u + 1]).then_inc(masked, 1)

                    def turn(b, s, pos):
                        kt, n, qt = order[pos], b * CHUNKS + s * KT + pos, s // NG
                        if kt in by_act:
                            return
                        if weigh and s % NG == 0 and rank[kt] == 0:
                            dve.wait_ge(side_t_in[qt], b * 32 + 32)
                        dve.wait_ge(turned, n + 1)
                        dve.wait_ge(valued, held(n - NPT + 1))
                        m = key_width(kt)
                        out, bank = turned_sb[0:m, (s * KT + pos) % NPT], t_ps[0:m, (s * KT + pos) % NBANK]
                        if weigh:
                            last = nc.vector.tensor_tensor(out.rearrange("p (j q) -> p j q", j=HG), bank.rearrange("p (j q) -> p j q", j=HG),
                                                           side_t[0:m, qt, None, kt - GT, :].broadcast_to([m, HG, P]), ALU.mult)
                        else:
                            last = nc.vector.tensor_copy(out, bank)
                        last.then_inc(out_by_dve, 1)

                    def step_end(b, s):
                        qt, g, u = s // NG, s % NG, s * HG
                        dve.wait_ge(exped, (b * STEPS + s + 1) * HG)
                        nc.vector.reciprocal(inverse[:, u:u + HG], total[:, u:u + HG]).then_inc(inverse_made, 1)
                        dve.wait_ge(inverse_made, b * STEPS + s + 1)
                        if g == 0:
                            dve.wait_ge(rows_turned, b * QT + qt)
                        dve.wait_ge(o_turned, b * STEPS + s + 1)
                        nc.vector.tensor_tensor(o_rows[:, g * 32:(g + 1) * 32].rearrange("p (j d) -> p j d", d=DH),
                                                o_ps[:, s % 2, 1].rearrange("p (j x) -> p j x", j=HG)[:, :, 0:DH],
                                                inverse[:, u:u + HG, None].broadcast_to([P, HG, DH]), ALU.mult).then_inc(o_normed, 1)
                        if g == NG - 1:
                            dve.wait_ge(projected, b * QT + qt + 1)
                            dve.wait_ge(x_ready, b * QT + qt + 1)
                            dve.wait_ge(x_stored[qt], b * 16)
                            nc.vector.scalar_tensor_tensor(out=x_new[:, qt], in0=o_ps[:, s % 2, 3], scalar=gates[:, layer:layer + 1],
                                                           in1=x_old[:, qt], op0=ALU.mult, op1=ALU.add).then_inc(finished, 1)

                    for u in range(AHEAD):
                        unit(0, u // HG, u % HG)
                    looped(dve, 0, B, lambda b, last: walk(b, last, unit, turn, None, None, step_end))


def slots_of(layer):
    need = (2 if layer == 0 else 1) * T // P + E - 1
    return -(-need // 8) * 8


def one(at):
    return slice(at, at + 1) if isinstance(at, int) else bass.ds(at, 1)


def experts_phase(nc, kept, w, layer, x_rows, x_new_rows, sorted_rows, expert_rows, q_stack):
    CHOICES = 2 if layer == 0 else 1
    SLOTS = slots_of(layer)
    GS = 4
    GROUPS = SLOTS // GS
    RING = 4
    experts = [e for e in range(E) if e % 2 == 0] + [e for e in range(E) if e % 2] if layer == 0 else list(range(E))
    ident, gates = kept["ident"], kept["gates"]
    RED = 16
    NX = 4
    TPX = NT // NX

    with ExitStack() as ctx:
        c = Chip(nc, ctx, f"experts{layer}")
        w1, w2 = c.sb("w1", [P, E, F]), c.sb("w2", [P, E, FT, P])
        b1, b2 = c.sb("b1", [P, E, F]), c.sb("b2", [P, E, P])
        x_in, normed = c.sb("x_in", [P, NT, P]), c.sb("normed", [P, NT, P])
        stats, moments = c.sb("stats", [P, NT, 6]), c.sb("moments", [P, NT, 2])
        deviation, inverse = c.sb("deviation", [P, NT]), c.sb("inverse", [P, NT])
        x_t = c.sb("x_t", [P, 2, CH])
        logits, top, index = c.sb("logits", [P, NT, E]), c.sb("top", [P, NT, E]), c.sb("index", [P, NT, E], U32)
        chosen, below, grown = c.sb("chosen", [P, NT, 2]), c.sb("below", [P, NT, E]), c.sb("grown", [P, NT, E])
        bottom, share = c.sb("bottom", [P, NT]), c.sb("share", [P, CHOICES, NT])
        picked = c.sb("picked", [P, CHOICES, NT, E])
        member = c.sb("member", [P, NT, E])
        totals = c.sb("totals", [P, NT, E])
        sums = c.sb("sums", [P, 2, NT, E])
        reaches, slots_used = c.sb("reaches", [P, E, NT]), c.sb("slots_used", [P, E])
        before, first_slot = c.sb("before", [P, E, E]), c.sb("first_slot", [P, E])
        first_row = c.sb("first_row", [P, E])
        place, placed = c.sb("place", [P, NT, E]), c.sb("placed", [P, CHOICES, NT, E])
        place_of, place_index = c.sb("place_of", [P, CHOICES, NT]), c.sb("place_index", [P, CHOICES * NT], U32)
        started, slot_expert, slot_index = c.sb("started", [1, SLOTS, E]), c.sb("slot_expert", [1, SLOTS]), c.sb("slot_index", [1, SLOTS], I32)
        even_slots = c.sb("even_slots", [1, 1], I32)
        count, number, full, earlier = c.sb("count", [P, SLOTS]), c.sb("number", [P, E]), c.sb("full", [P, NT]), c.sb("earlier", [P, P])
        ones, zeros = c.sb("ones", [P, P]), c.sb("zeros", [P, GS * P])
        rows_in, rows_t = c.sb("rows_in", [P, 2, GS, P]), c.sb("rows_t", [P, 2, GS * P])
        acts, acts_t, y_out = c.sb("acts", [P, RING, F]), c.sb("acts_t", [P, RING, F]), c.sb("y_out", [P, 2, GS, P])
        fetched = c.sb("fetched", [P, CHOICES, NT, P])
        x_new = normed
        if layer == 0:
            wg, bg = c.sb("wg", [P, E]), c.sb("bg", [P, E])
        else:
            w_red, wg, wg_t = c.sb("w_red", [P, RED]), c.sb("wg", [E, RED]), c.sb("wg_t", [RED, E])
            squares, norm = c.sb("squares", [E, RED]), c.sb("norm", [E, 4])
            reduced = c.sb("reduced", [RED, CH])
        if q_stack is not None:
            wq, bq = c.sb("wq", [P, P]), c.sb("bq", [P, 1])
            part = c.sb("part", [P, 2, 3, CH], BF16)
            scaled, rest = acts, acts_t
            next_in, sqrt_ready, root_again, stats_again, moments_again, inverse_again = (
                c.sem(n) for n in ("next_in", "sqrt_ready", "root_again", "stats_again", "moments_again", "inverse_again"))
            normed_again, turned_again, x_t_again, q_made, scaled_made, high_made, rest_made, mid_made, low_made = (
                c.sem(n) for n in ("normed_again", "turned_again", "x_t_again", "q_made", "scaled_made", "high_made", "rest_made",
                                   "mid_made", "low_made"))
            part_stored = [c.sem(f"part_stored{s}") for s in range(2)]
        t_ps, h_ps, y_ps = c.ps("t_ps", [P, 2, BANK]), c.ps("h_ps", [P, 2, BANK]), c.ps("y_ps", [P, 2, BANK])
        acts_ps = c.ps("acts_ps", [P, 2, BANK])
        gate_ps = acts_ps[:, 0, 0:NT * E].rearrange("p (j e) -> p j e", e=E)
        rank_ps = acts_ps[:, 1].rearrange("p (a j e) -> p a j e", a=2, e=E)

        small_in, weights_in, setup, wg_rooted, wg_turned = (c.sem(n) for n in ("small_in", "weights_in", "setup", "wg_rooted", "wg_turned"))
        biases_in = c.sem("biases_in")
        made_by_pool, ones_made, zeroed, cleared = (c.sem(n) for n in ("made_by_pool", "ones_made", "zeroed", "cleared"))
        x_loaded = [c.sem(f"x_loaded{n}") for n in range(NX)]
        stats_made, moments_made, var_made, root_made, inverse_made, normed_made = (
            c.sem(n) for n in ("stats_made", "moments_made", "var_made", "root_made", "inverse_made", "normed_made"))
        turned, x_t_made, reduced_made, reduced_out, gated, below_made, grown_made = (
            c.sem(n) for n in ("turned", "x_t_made", "reduced_made", "reduced_out", "gated", "below_made", "grown_made"))
        step_made, member_made, ranked, routed = (c.sem(n) for n in ("step_made", "member_made", "ranked", "routed"))
        
        scattered, fetched_in = kept["scattered"], kept["fetched_in"]
        BEFORE = 2 if layer else 0
        rows_turned, rows_t_made, upped, acted, downed, y_made = (
            c.sem(n) for n in ("rows_turned", "rows_t_made", "upped", "acted", "downed", "y_made"))
        biased, acts_turned, acts_t_made = (c.sem(n) for n in ("biased", "acts_turned", "acts_t_made"))
        rows_loaded = [c.sem(f"rows_loaded{s}") for s in range(2)]
        y_stored = [c.sem(f"y_stored{s}") for s in range(2)]
        summed, stored = c.sem("summed"), c.sem("stored")
        half_summed = c.sem("half_summed")

        def all_slots(i):
            return slice(i * GS * P, (i + 1) * GS * P) if isinstance(i, int) else bass.ds(i * (GS * P), GS * P)

        with nc.Block() as block:
            @block.sync
            def _(sp):
                for n in range(NX):
                    sp.dma_start(x_in[:, n * TPX:(n + 1) * TPX], x_rows[n * TPX:(n + 1) * TPX].rearrange("j p d -> p j d")).then_inc(x_loaded[n], 16)
                if layer == 0:
                    sp.wait_ge(zeroed, 1)
                    for i in range(GROUPS):
                        sp.dma_start(sorted_rows[all_slots(i)].rearrange("(k p) d -> p k d", p=P),
                                     zeros[:].rearrange("p (k d) -> p k d", d=P)).then_inc(cleared, 16)
                for k, e in enumerate(experts):
                    sp.dma_start(w1[:, k], w[f"w1_{layer}"][e]).then_inc(weights_in, 16)
                    sp.dma_start(w2[:, k], w[f"w2_{layer}"][e].rearrange("(f p) d -> p f d", p=P)).then_inc(weights_in, 16)

                sp.wait_ge(scattered, (BEFORE + CHOICES) * NT * 16)

                def load(i, s):
                    sp.dma_start(rows_in[:, s], sorted_rows[all_slots(i)].rearrange("(k p) d -> p k d", p=P)).then_inc(rows_loaded[s], 16)

                def two_groups(i, ends):
                    for s in range(2):
                        g = i * 2 + s
                        if not ends or isinstance(g, int) and g + 2 < GROUPS:
                            sp.wait_ge(rows_turned, g + 1)
                            load(g + 2, s)
                        sp.wait_ge(y_made, (g + 1) * GS)
                        sp.dma_start(expert_rows[all_slots(g)].rearrange("(k p) d -> p k d", p=P), y_out[:, s]).then_inc(y_stored[s], 16)

                for s in range(2):
                    load(s, s)
                looped(sp, 0, GROUPS // 2, two_groups)

                def store_parts(n):
                    sp.wait_ge(low_made, n + 1)
                    for t, (qp, _) in enumerate(TERMS):
                        sp.dma_start(q_stack[layer + 1, :, t * DH:(t + 1) * DH, n * CH:(n + 1) * CH], part[:, n % 2, qp]
                                     ).then_inc(part_stored[n % 2], 16)

                for n in range(NC):
                    sp.wait_ge(summed, (n + 1) * TPC)
                    sp.dma_start(x_new_rows[n * TPC:(n + 1) * TPC].rearrange("j p d -> p j d"), x_new[:, n * TPC:(n + 1) * TPC]).then_inc(stored, 16)
                    if q_stack is not None and n:
                        store_parts(n - 1)
                if q_stack is not None:
                    store_parts(NC - 1)
                    for s in range(2):
                        sp.wait_ge(part_stored[s], NC // 2 * NTERM * 16)
                sp.wait_ge(stored, NC * 16)

            @block.gpsimd
            def _(pool):
                if layer == 0:
                    nc.gpsimd.memset(zeros[:], 0.0).then_inc(zeroed, 1)
                nc.gpsimd.memset(ones[:], 1.0).then_inc(ones_made, 1)
                pool.wait_ge(ones_made, 1)
                nc.gpsimd.affine_select(out=earlier[:], in_=ones[:], compare_op=ALU.is_ge, fill=0.0,
                                        base=-1, pattern=[[1, P]], channel_multiplier=-1).then_inc(made_by_pool, 1)
                nc.gpsimd.iota(count[:], pattern=[[1, SLOTS]], base=0, channel_multiplier=0, allow_small_or_imprecise_dtypes=True).then_inc(made_by_pool, 1)
                nc.gpsimd.iota(full[:], pattern=[[P, NT]], base=0, channel_multiplier=0, allow_small_or_imprecise_dtypes=True).then_inc(made_by_pool, 1)
                pool.wait_ge(routed, 1)
                if layer == 0:
                    pool.wait_ge(cleared, GROUPS * 16)
                for j in range(NT):
                    for k in range(CHOICES):
                        at = k * NT + j
                        nc.gpsimd.indirect_dma_start(sorted_rows, bass.IndirectOffsetOnAxis(place_index[:, at:at + 1], 0),
                                                     normed[:, j], None).then_inc(scattered, 16)
                for s in range(2):
                    pool.wait_ge(y_stored[s], GROUPS // 2 * 16)
                for j in range(NT):
                    for k in range(CHOICES):
                        at = k * NT + j
                        nc.gpsimd.indirect_dma_start(fetched[:, k, j], None, expert_rows,
                                                     bass.IndirectOffsetOnAxis(place_index[:, at:at + 1], 0)).then_inc(fetched_in[j // TPC], 16)

            @block.tensor
            def _(pe):
                pe.wait_ge(small_in, 2 * 16)
                if layer == 1:
                    pe.wait_ge(setup, 5)
                    nc.tensor.transpose(gate_ps[0:RED, 0, 0:E], wg[:], ident[0:E, 0:E]).then_inc(wg_turned, 1)
                    pe.wait_ge(setup, 6)

                def turn_x(n):
                    pe.wait_ge(normed_made, n + 1)
                    if n >= 2:
                        pe.wait_ge(x_t_made, n - 1)
                    for j in range(TPC):
                        last = nc.tensor.transpose(t_ps[:, n % 2, j * P:(j + 1) * P], normed[:, n * TPC + j], ident[:])
                    last.then_inc(turned, 1)

                turn_x(0)
                for n in range(NC):
                    if n + 1 < NC:
                        turn_x(n + 1)
                    pe.wait_ge(x_t_made, n + 1)
                    if layer == 0:
                        for j in range(TPC):
                            last = nc.tensor.matmul(gate_ps[:, n * TPC + j], x_t[:, n % 2, j * P:(j + 1) * P], wg[:], start=True, stop=True)
                    else:
                        nc.tensor.matmul(h_ps[0:RED, 0], w_red[:], x_t[:, n % 2], start=True, stop=True).then_inc(reduced_made, 1)
                        pe.wait_ge(reduced_out, n + 1)
                        for j in range(TPC):
                            last = nc.tensor.matmul(gate_ps[:, n * TPC + j], reduced[:, j * P:(j + 1) * P], wg_t[:], start=True, stop=True)
                    last.then_inc(gated, 1)
                pe.wait_ge(made_by_pool, 1)
                pe.wait_ge(member_made, 1)
                nc.tensor.matmul(rank_ps[:, 0], earlier[:], member[:], start=True, stop=True)
                nc.tensor.matmul(rank_ps[:, 1], ones[:], member[:], start=True, stop=True).then_inc(ranked, 1)

                pe.wait_ge(weights_in, 2 * E * 16)

                def turn(g, s):
                    pe.wait_ge(rows_loaded[s], (g // 2 + 1) * 16 if isinstance(g, int) else g * 8 + (16 if s == 0 else 8))
                    for k in range(GS):
                        last = nc.tensor.transpose(t_ps[:, s, k * P:(k + 1) * P], rows_in[:, s, k], ident[:])
                    last.then_inc(rows_turned, 1)

                def expert_of(n):
                    return bass.ds(pe.value_load(slot_index[0:1, one(n)], min_val=0, max_val=E - 1), 1)

                def up(n, g, s, k):
                    e = expert_of(n)
                    if k == 0:
                        pe.wait_ge(rows_t_made, g + 1)
                    pe.wait_ge(biased, held(n - 1))
                    nc.tensor.matmul(h_ps[:, k % 2], rows_t[:, s, k * P:(k + 1) * P], w1[:, e].rearrange("p a b -> p (a b)"),
                                     start=True, stop=True).then_inc(upped, 1)

                def turn_acts(n, k):
                    pe.wait_ge(acted, n + 1)
                    pe.wait_ge(acts_t_made, held(n - 1))
                    for f in range(FT):
                        last = nc.tensor.transpose(acts_ps[:, k % 2, f * P:(f + 1) * P], acts[:, k % RING, f * P:(f + 1) * P], ident[:])
                    last.then_inc(acts_turned, 1)

                def down(n, g, s, k):
                    e = expert_of(n)
                    pe.wait_ge(y_made, held(n - 1))
                    pe.wait_ge(acts_t_made, n + 1)
                    for f in range(FT):
                        last = nc.tensor.matmul(y_ps[:, k % 2, 0:P], acts_t[:, k % RING, f * P:(f + 1) * P],
                                                w2[:, e, f].rearrange("p a b -> p (a b)"), start=(f == 0), stop=(f == FT - 1))
                    last.then_inc(downed, 1)

                def two_groups(i, ends):
                    for s in range(2):
                        g = i * 2 + s
                        final = ends and isinstance(g, int) and g + 1 == GROUPS
                        for k in range(GS):
                            n = g * GS + k
                            first = isinstance(n, int) and n < 2
                            up(n, g, s, k)
                            if k == 2 and not final:
                                turn(g + 1, 1 - s)
                            if not first or n == 1:
                                turn_acts(n - 1, (k - 1) % GS)
                            if not first:
                                down(n - 2, g if k >= 2 else g - 1, s if k >= 2 else 1 - s, (k - 2) % GS)
                        if final:
                            down(n - 1, g, s, GS - 2)
                            turn_acts(n, GS - 1)
                            down(n, g, s, GS - 1)

                pe.wait_ge(routed, 1)
                turn(0, 0)
                looped(pe, 0, GROUPS // 2, two_groups)
                if q_stack is not None:
                    pe.wait_ge(next_in, 32)
                    for n in range(NC):
                        pe.wait_ge(normed_again, n + 1)
                        for j in range(TPC):
                            last = nc.tensor.transpose(t_ps[:, n % 2, j * P:(j + 1) * P], x_in[:, n * TPC + j], ident[:])
                        last.then_inc(turned_again, 1)
                        pe.wait_ge(x_t_again, n + 1)
                        nc.tensor.matmul(h_ps[:, n % 2], wq[:], x_t[:, n % 2], start=True, stop=True).then_inc(q_made, 1)

            @block.scalar
            def _(act):
                if layer == 0:
                    act.dma_start(wg[:], w["wg0"]).then_inc(small_in, 16)
                    act.dma_start(bg[:], w["bg0"].partition_broadcast(P)).then_inc(small_in, 16)
                else:
                    act.dma_start(wg[:], w["wg1"]).then_inc(small_in, 16)
                    act.dma_start(w_red[:], w["w_red"]).then_inc(small_in, 16)
                if q_stack is not None:
                    act.dma_start(wq[:], w[f"wq{layer + 1}"]).then_inc(next_in, 16)
                    act.dma_start(bq[:], w[f"bq{layer + 1}"]).then_inc(next_in, 16)
                act.wait_ge(small_in, 2 * 16)
                if layer == 1:
                    act.wait_ge(setup, 2)
                    nc.scalar.activation(norm[:, 1:2], norm[:, 0:1], ACT.Sqrt).then_inc(wg_rooted, 1)
                act.wait_ge(var_made, 1)
                nc.scalar.activation(deviation[:], deviation[:], ACT.Sqrt).then_inc(root_made, 1)

                def copy_x(n):
                    act.wait_ge(turned, n + 1)
                    if n >= 2:
                        act.wait_ge(gated, n - 1)
                    nc.scalar.copy(x_t[:, n % 2], t_ps[:, n % 2]).then_inc(x_t_made, 1)

                copy_x(0)
                for n in range(NC):
                    if n + 1 < NC:
                        copy_x(n + 1)
                    if layer == 1:
                        act.wait_ge(reduced_made, n + 1)
                        nc.scalar.copy(reduced[:], h_ps[0:RED, 0]).then_inc(reduced_out, 1)
                for k, e in enumerate(experts):
                    act.dma_start(b1[:, k], w[f"b1_{layer}"][e].partition_broadcast(P)).then_inc(biases_in, 16)
                    act.dma_start(b2[:, k], w[f"b2_{layer}"][e].partition_broadcast(P)).then_inc(biases_in, 16)
                act.wait_ge(below_made, 1)
                nc.scalar.activation(grown[:], below[:], ACT.Exp).then_inc(grown_made, 1)
                act.wait_ge(routed, 1)
                even = act.value_load(even_slots[0:1, 0:1], min_val=0, max_val=SLOTS) if layer == 0 else None

                def activate(n, k, func):
                    act.wait_ge(biased, n + 1)
                    nc.scalar.activation(acts[:, k % RING], acts[:, k % RING], func).then_inc(acted, 1)

                def activate_by_kind(n, k):
                    if layer == 1:
                        activate(n, k, ACT.Gelu)
                        return
                    with act.If(even > n):
                        activate(n, k, ACT.Gelu)
                    with act.Else():
                        activate(n, k, ACT.Silu)

                def two_groups(i, ends):
                    for s in range(2):
                        for k in range(GS):
                            n = (i * 2 + s) * GS + k
                            activate_by_kind(n, k)

                looped(act, 0, GROUPS // 2, two_groups)
                if q_stack is not None:
                    for n in range(NC + 1):
                        if n < NC:
                            rows = slice(n * TPC, (n + 1) * TPC)
                            act.wait_ge(sqrt_ready, n + 1)
                            nc.scalar.activation(deviation[:, rows], deviation[:, rows], ACT.Sqrt).then_inc(root_again, 1)
                        if n:
                            m = n - 1
                            act.wait_ge(scaled_made, m + 1)
                            if m >= 2:
                                act.wait_ge(part_stored[m % 2], m // 2 * NTERM * 16)
                            nc.scalar.copy(part[:, m % 2, 0], scaled[:, m % 2]).then_inc(high_made, 1)
                        if n < NC:
                            act.wait_ge(turned_again, n + 1)
                            nc.scalar.copy(x_t[:, n % 2], t_ps[:, n % 2]).then_inc(x_t_again, 1)
                        if n:
                            act.wait_ge(rest_made, m + 1)
                            nc.scalar.copy(part[:, m % 2, 1], rest[:, m % 2]).then_inc(mid_made, 1)

            @block.vector
            def _(dve):
                dve.wait_ge(small_in, 2 * 16)
                if layer == 1:
                    nc.vector.memset(norm[:], 0.0).then_inc(setup, 1)
                    dve.wait_ge(setup, 1)
                    nc.vector.tensor_tensor_reduce(squares[:], wg[:], wg[:], 1.0, 0.0, ALU.mult, ALU.add, norm[:, 0:1]).then_inc(setup, 1)
                    dve.wait_ge(wg_rooted, 1)
                    nc.vector.tensor_scalar(norm[:, 2:3], norm[:, 1:2], 1e-4, None, ALU.max).then_inc(setup, 1)
                    dve.wait_ge(setup, 3)
                    nc.vector.reciprocal(norm[:, 3:4], norm[:, 2:3]).then_inc(setup, 1)
                    dve.wait_ge(setup, 4)
                    nc.vector.tensor_scalar(wg[:], wg[:], norm[:, 3:4], None, ALU.mult).then_inc(setup, 1)
                    dve.wait_ge(wg_turned, 1)
                    nc.vector.tensor_copy(wg_t[:], gate_ps[0:RED, 0, 0:E]).then_inc(setup, 1)
                for n in range(NX):
                    dve.wait_ge(x_loaded[n], 16)
                    for j in range(n * TPX, (n + 1) * TPX):
                        last = nc.vector.bn_stats(stats[:, j], x_in[:, j])
                last.then_inc(stats_made, 1)
                dve.wait_ge(stats_made, 1)
                for j in range(NT):
                    last = nc.vector.bn_aggr(moments[:, j], stats[:, j])
                last.then_inc(moments_made, 1)
                dve.wait_ge(moments_made, 1)
                nc.vector.tensor_scalar(deviation[:], moments[:, :, 1], EPS, None, ALU.add).then_inc(var_made, 1)
                dve.wait_ge(root_made, 1)
                nc.vector.reciprocal(inverse[:], deviation[:]).then_inc(inverse_made, 1)
                dve.wait_ge(inverse_made, 1)
                for n in range(NC):
                    for j in range(n * TPC, (n + 1) * TPC):
                        last = nc.vector.tensor_scalar(normed[:, j], x_in[:, j], moments[:, j, 0:1], inverse[:, j:j + 1], ALU.subtract, ALU.mult)
                    last.then_inc(normed_made, 1)

                made = 0

                def step(ins):
                    nonlocal made
                    made += 1
                    ins.then_inc(step_made, 1)
                    dve.wait_ge(step_made, made)

                dve.wait_ge(made_by_pool, 3)
                if layer == 0:
                    nc.vector.tensor_scalar(number[:, 0:E // 2], count[:, 0:E // 2], 2.0, None, ALU.mult)
                    nc.vector.tensor_scalar(number[:, E // 2:], count[:, 0:E // 2], 2.0, 1.0, ALU.mult, ALU.add)
                else:
                    nc.vector.tensor_copy(number[:], count[:, 0:E])
                step(nc.vector.tensor_tensor(before[:], count[:, 0:E, None].broadcast_to([P, E, E]),
                                             count[:, None, 0:E].broadcast_to([P, E, E]), ALU.is_gt))

                dve.wait_ge(gated, NC)
                if layer == 0:
                    step(nc.vector.tensor_tensor(logits[:], gate_ps, bg[:, None, :].broadcast_to([P, NT, E]), ALU.add))
                else:
                    step(nc.vector.tensor_copy(logits[:], gate_ps))
                for j in range(NT):
                    last = nc.vector.max(top[:, j], logits[:, j])
                step(last)
                nc.vector.tensor_tensor(below[:], logits[:] if layer else top[:], top[:, :, 0:1].broadcast_to([P, NT, E]),
                                        ALU.subtract).then_inc(below_made, 1)
                for j in range(NT):
                    last = nc.vector.max_index(index[:, j], top[:, j], logits[:, j])
                step(last)
                step(nc.vector.tensor_copy(chosen[:], index[:, :, 0:2]))
                for k in range(CHOICES):
                    last = nc.vector.tensor_tensor(picked[:, k], number[:, None, :].broadcast_to([P, NT, E]),
                                                   chosen[:, :, k:k + 1].broadcast_to([P, NT, E]), ALU.is_equal)
                step(last)
                if layer == 0:
                    nc.vector.tensor_tensor(member[:], picked[:, 0], picked[:, 1], ALU.add).then_inc(member_made, 1)
                else:
                    nc.vector.tensor_copy(member[:], picked[:, 0]).then_inc(member_made, 1)

                dve.wait_ge(grown_made, 1)
                if layer == 0:
                    step(nc.vector.tensor_scalar(bottom[:], grown[:, :, 1], 1.0, None, ALU.add))
                else:
                    step(nc.vector.tensor_reduce(bottom[:], grown[:], AX.X, ALU.add))
                step(nc.vector.reciprocal(bottom[:], bottom[:]))
                step(nc.vector.tensor_scalar(share[:, 0], bottom[:], gates[:, 2 + layer:3 + layer], None, ALU.mult))
                if layer == 0:
                    step(nc.vector.tensor_tensor(share[:, 1], grown[:, :, 1], share[:, 0], ALU.mult))

                dve.wait_ge(ranked, 1)
                nc.vector.tensor_copy(totals[:], rank_ps[:, 1])
                step(nc.vector.tensor_copy(sums[:, 0], rank_ps[:, 1]))
                at, shift = 0, 1
                while shift < NT:
                    nc.vector.tensor_copy(sums[:, 1 - at, 0:shift], sums[:, at, 0:shift])
                    step(nc.vector.tensor_tensor(sums[:, 1 - at, shift:], sums[:, at, shift:], sums[:, at, 0:NT - shift], ALU.add))
                    at, shift = 1 - at, shift * 2
                step(nc.vector.tensor_tensor(reaches[:], sums[:, at, NT - 1, :, None].broadcast_to([P, E, NT]),
                                             full[:, None, :].broadcast_to([P, E, NT]), ALU.is_gt))
                step(nc.vector.tensor_reduce(slots_used[:], reaches[:], AX.X, ALU.add))
                step(nc.vector.tensor_tensor(before[:], before[:], slots_used[:, None, :].broadcast_to([P, E, E]), ALU.mult))
                step(nc.vector.tensor_reduce(first_slot[:], before[:], AX.X, ALU.add))
                step(nc.vector.tensor_tensor(started[:], count[0:1, :, None].broadcast_to([1, SLOTS, E]),
                                             first_slot[0:1, None, :].broadcast_to([1, SLOTS, E]), ALU.is_ge))
                step(nc.vector.tensor_reduce(slot_expert[:], started[:], AX.X, ALU.add))
                nc.vector.tensor_scalar(slot_index[:], slot_expert[:], -1.0, None, ALU.add)
                nc.vector.tensor_copy(even_slots[:], first_slot[0:1, E // 2:E // 2 + 1])
                step(nc.vector.tensor_scalar(first_row[:], first_slot[:], float(P), None, ALU.mult))
                nc.vector.tensor_tensor(place[:], rank_ps[:, 0], first_row[:, None, :].broadcast_to([P, NT, E]), ALU.add)
                step(nc.vector.tensor_tensor(totals[:], sums[:, at], totals[:], ALU.subtract))
                step(nc.vector.tensor_tensor(place[:], place[:], totals[:], ALU.add))
                for k in range(CHOICES):
                    last = nc.vector.tensor_tensor(placed[:, k], picked[:, k], place[:], ALU.mult)
                step(last)
                for k in range(CHOICES):
                    last = nc.vector.tensor_reduce(place_of[:, k], placed[:, k], AX.X, ALU.add)
                step(last)
                nc.vector.tensor_copy(place_index[:], place_of[:].rearrange("p k j -> p (k j)")).then_inc(routed, 1)

                def expert_of(n):
                    return bass.ds(dve.value_load(slot_index[0:1, one(n)], min_val=0, max_val=E - 1), 1)

                def bias_up(n, k):
                    e = expert_of(n)
                    dve.wait_ge(acts_turned, held(n + 1 - RING))
                    dve.wait_ge(upped, n + 1)
                    nc.vector.tensor_tensor(acts[:, k % RING], h_ps[:, k % 2], b1[:, e].rearrange("p a b -> p (a b)"), ALU.add).then_inc(biased, 1)

                def copy_acts(n, k):
                    dve.wait_ge(acts_turned, n + 1)
                    dve.wait_ge(downed, held(n + 1 - RING))
                    nc.vector.tensor_copy(acts_t[:, k % RING], acts_ps[:, k % 2]).then_inc(acts_t_made, 1)

                def bias_down(n, g, s, k):
                    e = expert_of(n)
                    if k == 0:
                        dve.wait_ge(y_stored[s], g // 2 * 16 if isinstance(g, int) else g * 8 - 8 * s)
                    dve.wait_ge(downed, n + 1)
                    nc.vector.tensor_tensor(y_out[:, s, k], y_ps[:, k % 2, 0:P],
                                            b2[:, e].rearrange("p a b -> p (a b)"), ALU.add).then_inc(y_made, 1)

                def copy_rows(g, s):
                    dve.wait_ge(rows_turned, g + 1)
                    dve.wait_ge(upped, held((g - 1) * GS))
                    nc.vector.tensor_copy(rows_t[:, s], t_ps[:, s]).then_inc(rows_t_made, 1)

                def two_groups(i, ends):
                    for s in range(2):
                        g = i * 2 + s
                        final = ends and isinstance(g, int) and g + 1 == GROUPS
                        for k in range(GS):
                            n = g * GS + k
                            bias_up(n, k)
                            if k == 2 and not final:
                                copy_rows(g + 1, 1 - s)
                            if not isinstance(n, int) or n >= 1:
                                copy_acts(n - 1, (k - 1) % GS)
                            if not isinstance(n, int) or n >= 2:
                                bias_down(n - 2, g if k >= 2 else g - 1, s if k >= 2 else 1 - s, (k - 2) % GS)
                        if final:
                            bias_down(n - 1, g, s, GS - 2)
                            copy_acts(n, GS - 1)
                            bias_down(n, g, s, GS - 1)

                dve.wait_ge(routed, 1)
                dve.wait_ge(biases_in, 2 * E * 16)
                copy_rows(0, 0)
                looped(dve, 0, GROUPS // 2, two_groups)
                def sum_up(n):
                    dve.wait_ge(fetched_in[n], (BEFORE + CHOICES) * TPC * 16)
                    for j in range(n * TPC, (n + 1) * TPC):
                        last = nc.vector.scalar_tensor_tensor(out=x_new[:, j], in0=fetched[:, 0, j], scalar=share[:, 0, j:j + 1],
                                                              in1=x_in[:, j], op0=ALU.mult, op1=ALU.add)
                        if CHOICES == 1:
                            last.then_inc(summed, 1)
                    if CHOICES == 2:
                        last.then_inc(half_summed, 1)
                        dve.wait_ge(half_summed, n + 1)
                        for j in range(n * TPC, (n + 1) * TPC):
                            nc.vector.scalar_tensor_tensor(out=x_new[:, j], in0=fetched[:, 1, j], scalar=share[:, 1, j:j + 1],
                                                           in1=x_new[:, j], op0=ALU.mult, op1=ALU.add).then_inc(summed, 1)

                def next_stats(n):
                    rows = range(n * TPC, (n + 1) * TPC)
                    dve.wait_ge(summed, (n + 1) * TPC)
                    for j in rows:
                        last = nc.vector.bn_stats(stats[:, j], x_new[:, j])
                    last.then_inc(stats_again, 1)
                    dve.wait_ge(stats_again, n + 1)
                    for j in rows:
                        last = nc.vector.bn_aggr(moments[:, j], stats[:, j])
                    last.then_inc(moments_again, 1)
                    dve.wait_ge(moments_again, n + 1)
                    nc.vector.tensor_scalar(deviation[:, rows.start:rows.stop], moments[:, rows.start:rows.stop, 1], EPS, None,
                                            ALU.add).then_inc(sqrt_ready, 1)

                def next_norm(n):
                    rows = range(n * TPC, (n + 1) * TPC)
                    dve.wait_ge(root_again, n + 1)
                    nc.vector.reciprocal(inverse[:, rows.start:rows.stop], deviation[:, rows.start:rows.stop]).then_inc(inverse_again, 1)
                    dve.wait_ge(inverse_again, n + 1)
                    for j in rows:
                        last = nc.vector.tensor_scalar(x_in[:, j], x_new[:, j], moments[:, j, 0:1], inverse[:, j:j + 1], ALU.subtract, ALU.mult)
                    last.then_inc(normed_again, 1)

                if q_stack is None:
                    for n in range(NC):
                        sum_up(n)
                else:
                    dve.wait_ge(next_in, 32)
                    for n in range(NC + 1):
                        m = n - 1
                        if n < NC:
                            sum_up(n)
                            next_stats(n)
                        if n:
                            dve.wait_ge(q_made, m + 1)
                            nc.vector.tensor_scalar(scaled[:, m % 2], h_ps[:, m % 2], bq[:], -SCALE, ALU.add, ALU.mult).then_inc(scaled_made, 1)
                        if n < NC:
                            next_norm(n)
                        if n:
                            dve.wait_ge(high_made, m + 1)
                            nc.vector.tensor_tensor(rest[:, m % 2], scaled[:, m % 2], part[:, m % 2, 0], ALU.subtract).then_inc(rest_made, 1)
                            dve.wait_ge(mid_made, m + 1)
                            nc.vector.tensor_tensor(part[:, m % 2, 2], rest[:, m % 2], part[:, m % 2, 1], ALU.subtract).then_inc(low_made, 1)


def build(nc, w, out):
    k_stack = nc.dram_tensor("k_stack", (2, B, H, 3 * DH, S2), BF16).ap()
    v_rows = nc.dram_tensor("v_rows", (2, B, NG, P, KT, 32), F32).ap()
    q_stack = nc.dram_tensor("q_stack", (2, H, ROWS, T), BF16).ap()
    x1, x2, x3 = (nc.dram_tensor(n, (NT, P, P), F32).ap() for n in ("x1", "x2", "x3"))
    sorted_rows = nc.dram_tensor("sorted_rows", (slots_of(0) * P, P), F32).ap()
    expert_rows = nc.dram_tensor("expert_rows", (slots_of(0) * P, P), F32).ap()
    with ExitStack() as ctx:
        lasting = {"scattered": nc.alloc_semaphore(name="scattered"), "fetched_in": [nc.alloc_semaphore(name=f"fetched_in{n}") for n in range(NC)]}
        kept = {**lasting, "ident": ctx.enter_context(nc.sbuf_tensor("ident", [P, P], F32)),
                "gates": ctx.enter_context(nc.sbuf_tensor("gates", [P, 4], F32)),
                "late_only": ctx.enter_context(nc.sbuf_tensor("late_only", [1, 1], I32))}
        constants(nc, kept, w)
        context_phase(nc, kept, w, k_stack, v_rows)
        queries_phase(nc, kept, w, 0, w["x"], q_stack)
        attention_phase(nc, kept, w, 0, k_stack, v_rows, q_stack, w["x"], x1)
        experts_phase(nc, kept, w, 0, x1, x2, sorted_rows, expert_rows, q_stack)
        attention_phase(nc, kept, w, 1, k_stack, v_rows, q_stack, x2, x3, first=LATE, late=1)
        attention_phase(nc, kept, w, 1, k_stack, v_rows, q_stack, x2, x3, late=0)
        experts_phase(nc, kept, w, 1, x3, out, sorted_rows, expert_rows, None)


def kernel(**inputs):
    import concourse.bacc as bacc
    from concourse.bass_utils import run_bass_kernel_spmd

    a = {n: np.asarray(v) for n, v in inputs.items()}
    side, mask0 = a["fside_BxSxS2_0"], a["mask_BxSxS2_ik1"]
    laid = {
        "x": a["x"].reshape(NT, P, D),
        "ctx_t": a["ctx_1024"].transpose(0, 2, 1),
        "side": side, "side_t": side[:, :, 8 * P:].transpose(0, 2, 1), "mask0": mask0,
        "mask1": a["mask_1x1xSxS2_ik0"].reshape(S, S2),
        "g_xattn": a["g_xattn"], "g_ffn": a["g_ffn"],
        "wq0": a["L0_xattn_wq_k"], "wk0": a["L0_xattn_wk_k"], "wv0": a["L0_xattn_wv_k"], "wo0": a["L0_xattn_wo_k"],
        "bq0": a["L0_xattn_wq_b"][:, None], "bk0": a["L0_xattn_wk_b"][:, None], "bv0": a["L0_xattn_wv_b"], "bo0": a["L0_xattn_wo_b"],
        "wq1": a["L1_xattn_wq"].T, "wk1": a["L1_xattn_wk"].T, "wv1": a["L1_xattn_wv"].T, "wo1": a["L1_xattn_wo"].T,
        "bq1": a["L1_xattn_bq"][:, None], "bk1": a["L1_xattn_bk"][:, None], "bv1": a["L1_xattn_bv"], "bo1": a["L1_xattn_bo"],
        "w1_0": a["L0_ffn_W1"], "w2_0": a["L0_ffn_W2"], "b2_0": a["L0_ffn_b2"], "wg0": a["L0_ffn_Wg"], "bg0": a["L0_ffn_bg"],
        "b1_0": a["L0_ffn_b1"], "b1_1": a["L1_ffn_b1"],
        "w1_1": a["L1_ffn_w1"], "w2_1": a["L1_ffn_w2"], "b2_1": a["L1_ffn_b2"], "wg1": a["L1_ffn_wg"], "w_red": a["L1_ffn_w_red"],
    }
    nc = bacc.Bacc("TRN2", target_bir_lowering=False, num_devices=1)
    arrays, w = {}, {}
    for name, v in laid.items():
        v = np.ascontiguousarray(v)
        arrays[f"in_{name}"] = v
        w[name] = nc.dram_tensor(f"in_{name}", v.shape, mybir.dt.from_np(v.dtype), kind="ExternalInput").ap()
    out = nc.dram_tensor("out_x", (NT, P, D), F32, kind="ExternalOutput").ap()
    build(nc, w, out)
    r = run_bass_kernel_spmd(nc, [arrays], core_ids=[0])
    return r.results[0]["out_x"].reshape(B, S, D)
```
